# Optimizing a Trainium2 kernel written in Bass

```python
import numpy as np
import jax
import jax.numpy as jnp

def _softmax(x, axis=-1):
    return jax.nn.softmax(x, axis=axis)

def _gelu(x):
    return jax.nn.gelu(x, approximate=True)

def _silu(x):
    return jax.nn.silu(x)

def _sigmoid(x):
    return jax.nn.sigmoid(x)

def _layernorm(x, axis=-1, eps=1e-05):
    m = jnp.mean(x, axis=axis, keepdims=True)
    v = jnp.var(x, axis=axis, keepdims=True)
    return (x - m) / jnp.sqrt(v + eps)

def _scatter_add(tgt, idx, src, axis=0):
    return tgt.at[idx].add(src)

def _segment_sum(src, seg, n):
    return jax.ops.segment_sum(src, seg, n)
kernel_name = 'mk_lm_tower_d2_tok_ids256_r4_8cbc64'

def setup_inputs(seed: int=0):
    np.random.seed(seed)
    _w = jnp.asarray

    def _rec_inputs():
        import jax
        import jax.numpy as jnp
        _rk = jax.random.key(seed)
        x = jax.random.randint(jax.random.fold_in(_rk, 1), (1, 2048), 0, 2048, jnp.int32)
        return x
    x = _rec_inputs()

    def _L0_tok_setup():
        import jax, jax.numpy as jnp
        import numpy as np
        D = 64
        NLEAF = 8
        N_INTERNAL = 7
        N_STRUCT = 2048
        COMP_V = 256
        OP_V = 64
        EPS = 1e-05

        def _layer_norm(x, gamma, beta):
            mu = jnp.mean(x, axis=-1, keepdims=True)
            var = jnp.mean(jnp.square(x - mu), axis=-1, keepdims=True)
            return (x - mu) * jax.lax.rsqrt(var + EPS) * gamma + beta
        key = jax.random.key(seed)
        ks = jax.random.split(key, 8)
        struct_indices = jax.random.randint(ks[0], (32, 512), 0, N_STRUCT)
        leaf_ids = jax.random.randint(ks[1], (N_STRUCT, NLEAF), 0, COMP_V).astype(jnp.int32)
        op_ids = jax.random.randint(ks[2], (N_STRUCT, N_INTERNAL), 0, OP_V).astype(jnp.int32)
        comp_emb = jax.random.normal(ks[3], (COMP_V, D), dtype=jnp.float32)
        op_emb = jax.random.normal(ks[4], (OP_V, D), dtype=jnp.float32)
        W_bin = jax.random.normal(ks[5], (3 * D, D), dtype=jnp.float32) / np.sqrt(3 * D)
        b_bin = jnp.zeros((D,), dtype=jnp.float32)
        gamma = jnp.ones((D,), dtype=jnp.float32)
        beta = jnp.zeros((D,), dtype=jnp.float32)
        return {'struct_indices': struct_indices, 'leaf_ids': leaf_ids, 'op_ids': op_ids, 'comp_emb': comp_emb, 'op_emb': op_emb, 'W_bin': W_bin, 'b_bin': b_bin, 'gamma': gamma, 'beta': beta}
    _L0_tok_all = _L0_tok_setup()
    _L0_tok_in = {k: v for k, v in _L0_tok_all.items() if k in ('leaf_ids', 'op_ids', 'comp_emb', 'op_emb', 'W_bin', 'b_bin', 'gamma', 'beta')}
    del _L0_tok_all

    def _L0_attn_setup():
        import jax, jax.numpy as jnp
        import numpy as np
        D, H, L, S_MAX = (64, 8, 4, 1024)
        DH = D // H
        FF = 4 * D
        B, S = (16, 1024)

        def _pe(seq_len, d):
            pos = jnp.arange(seq_len, dtype=jnp.float32)[:, None]
            div = jnp.exp(jnp.arange(0, d, 2, dtype=jnp.float32) * (-jnp.log(10000.0) / d))
            pe = jnp.zeros((seq_len, d), dtype=jnp.float32)
            pe = pe.at[:, 0::2].set(jnp.sin(pos * div))
            pe = pe.at[:, 1::2].set(jnp.cos(pos * div))
            return pe

        def _ln(x, g, b, eps=1e-05):
            mu = jnp.mean(x, axis=-1, keepdims=True)
            var = jnp.var(x, axis=-1, keepdims=True)
            return (x - mu) * jax.lax.rsqrt(var + eps) * g + b
        key = jax.random.key(seed)
        ks = jax.random.split(key, 12)
        s = 0.02
        return {'x': jax.random.normal(ks[0], (B, S, D), dtype=jnp.float32), 'Wq': jax.random.normal(ks[1], (L, D, D), dtype=jnp.float32) * s, 'Wk': jax.random.normal(ks[2], (L, D, D), dtype=jnp.float32) * s, 'Wv': jax.random.normal(ks[3], (L, D, D), dtype=jnp.float32) * s, 'Wo': jax.random.normal(ks[4], (L, D, D), dtype=jnp.float32) * s, 'bo': jnp.zeros((L, D), dtype=jnp.float32), 'g1': jnp.ones((L, D), dtype=jnp.float32), 'b1': jnp.zeros((L, D), dtype=jnp.float32), 'W1': jax.random.normal(ks[5], (L, D, FF), dtype=jnp.float32) * s, 'bf1': jnp.zeros((L, FF), dtype=jnp.float32), 'W2': jax.random.normal(ks[6], (L, FF, D), dtype=jnp.float32) * s, 'bf2': jnp.zeros((L, D), dtype=jnp.float32), 'g2': jnp.ones((L, D), dtype=jnp.float32), 'b2': jnp.zeros((L, D), dtype=jnp.float32)}
    _L0_attn_all = _L0_attn_setup()
    _L0_attn_in = {k: v for k, v in _L0_attn_all.items() if k in ('Wq', 'Wk', 'Wv', 'Wo', 'bo', 'g1', 'b1', 'W1', 'bf1', 'W2', 'bf2', 'g2', 'b2')}
    del _L0_attn_all

    def _L0_ffn_setup():
        import jax, jax.numpy as jnp
        import numpy as np
        C = 64
        EPS = 1e-05
        N_ITERS = 30

        def _layernorm(x, w, bias):
            mu = jnp.mean(x, axis=-1, keepdims=True)
            var = jnp.mean(jnp.square(x - mu), axis=-1, keepdims=True)
            return (x - mu) * jax.lax.rsqrt(var + EPS) * w + bias
        key = jax.random.key(seed)
        kx, kw, kb, klw, klb = jax.random.split(key, 5)
        x = jax.random.normal(kx, (8, 512, C), dtype=jnp.float32)
        bound = 1.0 / np.sqrt(C)
        W = jax.random.uniform(kw, (C, C), minval=-bound, maxval=bound, dtype=jnp.float32)
        b = jax.random.uniform(kb, (C,), minval=-bound, maxval=bound, dtype=jnp.float32)
        ln_w = jnp.ones((C,), dtype=jnp.float32)
        ln_b = jnp.zeros((C,), dtype=jnp.float32)
        return {'x': x, 'ln_w': ln_w, 'ln_b': ln_b, 'W': W, 'b': b}
    _L0_ffn_all = _L0_ffn_setup()
    _L0_ffn_in = {k: v for k, v in _L0_ffn_all.items() if k in ('ln_w', 'ln_b', 'W', 'b')}
    del _L0_ffn_all

    def _L1_attn_setup():
        import jax, jax.numpy as jnp
        import numpy as np
        import math
        CHUNK = 128

        def _build_slopes(n):

            def p2(n):
                start = 2.0 ** (-2.0 ** (-(math.log2(n) - 3)))
                return [start ** (i + 1) for i in range(n)]
            if math.log2(n).is_integer():
                s = p2(n)
            else:
                c = 2 ** math.floor(math.log2(n))
                s = p2(c) + p2(2 * c)[0::2][:n - c]
            return np.asarray(s, dtype=np.float32)

        def _lightning_attn(q, k, v, slopes):
            b, h, l, d = q.shape
            n = l // CHUNK
            s = slopes.reshape(h, 1, 1)
            pos = jnp.arange(CHUNK, dtype=q.dtype)
            diff = pos[:, None] - pos[None, :]
            mask = jnp.where(diff >= 0, jnp.exp(-s * diff), 0.0)[None]
            q_dec = jnp.exp(-slopes[:, None] * pos)[None, :, :, None]
            k_dec = jnp.exp(-slopes[:, None] * (CHUNK - pos))[None, :, :, None]
            blk = jnp.exp(-slopes * CHUNK).reshape(1, h, 1, 1)
            qc = q.reshape(b, h, n, CHUNK, d).transpose(2, 0, 1, 3, 4)
            kc = k.reshape(b, h, n, CHUNK, d).transpose(2, 0, 1, 3, 4)
            vc = v.reshape(b, h, n, CHUNK, d).transpose(2, 0, 1, 3, 4)

            def step(S, xs):
                qi, ki, vi = xs
                scores = jnp.einsum('bhcd,bhed->bhce', qi, ki) * mask
                intra = jnp.einsum('bhce,bhed->bhcd', scores, vi)
                inter = jnp.einsum('bhcd,bhde->bhce', qi * q_dec, S)
                S_new = blk * S + jnp.einsum('bhcd,bhce->bhde', ki * k_dec, vi)
                return (S_new, intra + inter)
            S0 = jnp.zeros((b, h, d, d), q.dtype)
            _, o = jax.lax.scan(step, S0, (qc, kc, vc))
            return o.transpose(1, 2, 0, 3, 4).reshape(b, h, l, d)
        key = jax.random.key(seed)
        k1, k2, k3 = jax.random.split(key, 3)
        b, l, c, h = (8, 4096, 64, 8)
        x = jax.random.normal(k1, (b, l, c), dtype=jnp.float32)
        w_qkv = jax.random.normal(k2, (c, 3 * c), dtype=jnp.float32) * 0.02
        w_proj = jax.random.normal(k3, (c, c), dtype=jnp.float32) * 0.02
        b_proj = jnp.zeros((c,), dtype=jnp.float32)
        slopes = jnp.asarray(_build_slopes(h))
        return {'x': x, 'w_qkv': w_qkv, 'w_proj': w_proj, 'b_proj': b_proj, 'slopes': slopes}
    _L1_attn_all = _L1_attn_setup()
    _L1_attn_in = {k: v for k, v in _L1_attn_all.items() if k in ('w_qkv', 'w_proj', 'b_proj', 'slopes')}
    del _L1_attn_all

    def _L1_ffn_setup():
        import jax, jax.numpy as jnp
        import numpy as np
        E = 8
        K = 2
        D = 64
        H = 128
        DOUT = 64
        EPS = 1e-05
        key = jax.random.key(seed)
        ks = jax.random.split(key, 9)
        s = 0.02
        return {'x': jax.random.normal(ks[0], (4, 2048, D), jnp.float32), 'gamma': 1.0 + 0.05 * jax.random.normal(ks[1], (D,), jnp.float32), 'beta': 0.05 * jax.random.normal(ks[2], (D,), jnp.float32), 'Wr': 0.01 * jax.random.normal(ks[3], (D, E), jnp.float32), 'br': jnp.zeros((E,), jnp.float32), 'W1': s * jax.random.normal(ks[4], (E, D, H), jnp.float32), 'b1': s * jax.random.normal(ks[5], (E, H), jnp.float32), 'W2': s * jax.random.normal(ks[6], (E, H, DOUT), jnp.float32), 'b2': s * jax.random.normal(ks[7], (E, DOUT), jnp.float32)}
    _L1_ffn_all = _L1_ffn_setup()
    _L1_ffn_in = {k: v for k, v in _L1_ffn_all.items() if k in ('gamma', 'beta', 'Wr', 'br', 'W1', 'b1', 'W2', 'b2')}
    del _L1_ffn_all
    return {'x': x, 'L0_tok_leaf_ids': _L0_tok_in['leaf_ids'], 'L0_tok_op_ids': _L0_tok_in['op_ids'], 'L0_tok_comp_emb': _L0_tok_in['comp_emb'], 'L0_tok_op_emb': _L0_tok_in['op_emb'], 'L0_tok_W_bin': _L0_tok_in['W_bin'], 'L0_tok_b_bin': _L0_tok_in['b_bin'], 'L0_tok_gamma': _L0_tok_in['gamma'], 'L0_tok_beta': _L0_tok_in['beta'], 'L0_attn_Wq': _L0_attn_in['Wq'], 'L0_attn_Wk': _L0_attn_in['Wk'], 'L0_attn_Wv': _L0_attn_in['Wv'], 'L0_attn_Wo': _L0_attn_in['Wo'], 'L0_attn_bo': _L0_attn_in['bo'], 'L0_attn_g1': _L0_attn_in['g1'], 'L0_attn_b1': _L0_attn_in['b1'], 'L0_attn_W1': _L0_attn_in['W1'], 'L0_attn_bf1': _L0_attn_in['bf1'], 'L0_attn_W2': _L0_attn_in['W2'], 'L0_attn_bf2': _L0_attn_in['bf2'], 'L0_attn_g2': _L0_attn_in['g2'], 'L0_attn_b2': _L0_attn_in['b2'], 'L0_ffn_ln_w': _L0_ffn_in['ln_w'], 'L0_ffn_ln_b': _L0_ffn_in['ln_b'], 'L0_ffn_W': _L0_ffn_in['W'], 'L0_ffn_b': _L0_ffn_in['b'], 'L1_attn_w_qkv': _L1_attn_in['w_qkv'], 'L1_attn_w_proj': _L1_attn_in['w_proj'], 'L1_attn_b_proj': _L1_attn_in['b_proj'], 'L1_attn_slopes': _L1_attn_in['slopes'], 'L1_ffn_gamma': _L1_ffn_in['gamma'], 'L1_ffn_beta': _L1_ffn_in['beta'], 'L1_ffn_Wr': _L1_ffn_in['Wr'], 'L1_ffn_br': _L1_ffn_in['br'], 'L1_ffn_W1': _L1_ffn_in['W1'], 'L1_ffn_b1': _L1_ffn_in['b1'], 'L1_ffn_W2': _L1_ffn_in['W2'], 'L1_ffn_b2': _L1_ffn_in['b2']}

def reference(x, L0_tok_leaf_ids, L0_tok_op_ids, L0_tok_comp_emb, L0_tok_op_emb, L0_tok_W_bin, L0_tok_b_bin, L0_tok_gamma, L0_tok_beta, L0_attn_Wq, L0_attn_Wk, L0_attn_Wv, L0_attn_Wo, L0_attn_bo, L0_attn_g1, L0_attn_b1, L0_attn_W1, L0_attn_bf1, L0_attn_W2, L0_attn_bf2, L0_attn_g2, L0_attn_b2, L0_ffn_ln_w, L0_ffn_ln_b, L0_ffn_W, L0_ffn_b, L1_attn_w_qkv, L1_attn_w_proj, L1_attn_b_proj, L1_attn_slopes, L1_ffn_gamma, L1_ffn_beta, L1_ffn_Wr, L1_ffn_br, L1_ffn_W1, L1_ffn_b1, L1_ffn_W2, L1_ffn_b2):
    import jax
    import jax.numpy as jnp

    def _L0_tok_ref(struct_indices, leaf_ids, op_ids, comp_emb, op_emb, W_bin, b_bin, gamma, beta):
        import jax, jax.numpy as jnp
        import numpy as np
        D = 64
        NLEAF = 8
        N_INTERNAL = 7
        N_STRUCT = 2048
        COMP_V = 256
        OP_V = 64
        EPS = 1e-05

        def _layer_norm(x, gamma, beta):
            mu = jnp.mean(x, axis=-1, keepdims=True)
            var = jnp.mean(jnp.square(x - mu), axis=-1, keepdims=True)
            return (x - mu) * jax.lax.rsqrt(var + EPS) * gamma + beta
        h = _layer_norm(comp_emb[leaf_ids], gamma, beta)
        off = 0
        while h.shape[1] > 1:
            n = h.shape[1] // 2
            ops = op_emb[op_ids[:, off:off + n]]
            cat = jnp.concatenate([ops, h[:, 0::2], h[:, 1::2]], axis=-1)
            h = _layer_norm(jnp.einsum('nkc,cd->nkd', cat, W_bin) + b_bin, gamma, beta)
            off += n
        root = h[:, 0]
        out = root[struct_indices]
        mask = (struct_indices > 1)[..., None]
        return jnp.where(mask, out, jnp.zeros((), dtype=out.dtype))

    def _L0_attn_ref(x, Wq, Wk, Wv, Wo, bo, g1, b1, W1, bf1, W2, bf2, g2, b2):
        import jax, jax.numpy as jnp
        import numpy as np
        D, H, L, S_MAX = (64, 8, 4, 1024)
        DH = D // H
        FF = 4 * D
        B, S = (16, 1024)

        def _pe(seq_len, d):
            pos = jnp.arange(seq_len, dtype=jnp.float32)[:, None]
            div = jnp.exp(jnp.arange(0, d, 2, dtype=jnp.float32) * (-jnp.log(10000.0) / d))
            pe = jnp.zeros((seq_len, d), dtype=jnp.float32)
            pe = pe.at[:, 0::2].set(jnp.sin(pos * div))
            pe = pe.at[:, 1::2].set(jnp.cos(pos * div))
            return pe

        def _ln(x, g, b, eps=1e-05):
            mu = jnp.mean(x, axis=-1, keepdims=True)
            var = jnp.var(x, axis=-1, keepdims=True)
            return (x - mu) * jax.lax.rsqrt(var + eps) * g + b
        b, s, d = x.shape
        x = x + _pe(s, d)[None, :, :]
        scale = DH ** (-0.5)
        for l in range(L):
            h = _ln(x, g1[l], b1[l])
            q = (h @ Wq[l]).reshape(b, s, H, DH).transpose(0, 2, 1, 3)
            k = (h @ Wk[l]).reshape(b, s, H, DH).transpose(0, 2, 1, 3)
            v = (h @ Wv[l]).reshape(b, s, H, DH).transpose(0, 2, 1, 3)
            q = jax.nn.softmax(q, axis=-1) * scale
            k = jax.nn.softmax(k, axis=-2)
            ctx = jnp.einsum('bhnd,bhne->bhde', k, v)
            attn = jnp.einsum('bhnd,bhde->bhne', q, ctx)
            attn = attn.transpose(0, 2, 1, 3).reshape(b, s, d)
            x = x + attn @ Wo[l] + bo[l]
            h = _ln(x, g2[l], b2[l])
            x = x + jax.nn.gelu(h @ W1[l] + bf1[l], approximate=False) @ W2[l] + bf2[l]
        return x

    def _L0_ffn_ref(x, ln_w, ln_b, W, b):
        import jax, jax.numpy as jnp
        import numpy as np
        C = 64
        EPS = 1e-05
        N_ITERS = 30

        def _layernorm(x, w, bias):
            mu = jnp.mean(x, axis=-1, keepdims=True)
            var = jnp.mean(jnp.square(x - mu), axis=-1, keepdims=True)
            return (x - mu) * jax.lax.rsqrt(var + EPS) * w + bias

        def step(h, _):
            h = h + 0.01 * jnp.tanh(h)
            h = h * jax.nn.sigmoid(h)
            h = _layernorm(h, ln_w, ln_b)
            h = jnp.einsum('bsc,dc->bsd', h, W) + b
            return (h, None)
        x, _ = jax.lax.scan(step, x, None, length=N_ITERS)
        return x

    def _L1_attn_ref(x, w_qkv, w_proj, b_proj, slopes):
        import jax, jax.numpy as jnp
        import numpy as np
        import math
        CHUNK = 128

        def _build_slopes(n):

            def p2(n):
                start = 2.0 ** (-2.0 ** (-(math.log2(n) - 3)))
                return [start ** (i + 1) for i in range(n)]
            if math.log2(n).is_integer():
                s = p2(n)
            else:
                c = 2 ** math.floor(math.log2(n))
                s = p2(c) + p2(2 * c)[0::2][:n - c]
            return np.asarray(s, dtype=np.float32)

        def _lightning_attn(q, k, v, slopes):
            b, h, l, d = q.shape
            n = l // CHUNK
            s = slopes.reshape(h, 1, 1)
            pos = jnp.arange(CHUNK, dtype=q.dtype)
            diff = pos[:, None] - pos[None, :]
            mask = jnp.where(diff >= 0, jnp.exp(-s * diff), 0.0)[None]
            q_dec = jnp.exp(-slopes[:, None] * pos)[None, :, :, None]
            k_dec = jnp.exp(-slopes[:, None] * (CHUNK - pos))[None, :, :, None]
            blk = jnp.exp(-slopes * CHUNK).reshape(1, h, 1, 1)
            qc = q.reshape(b, h, n, CHUNK, d).transpose(2, 0, 1, 3, 4)
            kc = k.reshape(b, h, n, CHUNK, d).transpose(2, 0, 1, 3, 4)
            vc = v.reshape(b, h, n, CHUNK, d).transpose(2, 0, 1, 3, 4)

            def step(S, xs):
                qi, ki, vi = xs
                scores = jnp.einsum('bhcd,bhed->bhce', qi, ki) * mask
                intra = jnp.einsum('bhce,bhed->bhcd', scores, vi)
                inter = jnp.einsum('bhcd,bhde->bhce', qi * q_dec, S)
                S_new = blk * S + jnp.einsum('bhcd,bhce->bhde', ki * k_dec, vi)
                return (S_new, intra + inter)
            S0 = jnp.zeros((b, h, d, d), q.dtype)
            _, o = jax.lax.scan(step, S0, (qc, kc, vc))
            return o.transpose(1, 2, 0, 3, 4).reshape(b, h, l, d)
        b, l, c = x.shape
        h = slopes.shape[0]
        d = c // h
        scale = d ** (-0.5)
        qkv = (x @ w_qkv).reshape(b, l, 3, h, d)
        q = qkv[:, :, 0].transpose(0, 2, 1, 3) * scale
        k = qkv[:, :, 1].transpose(0, 2, 1, 3)
        v = qkv[:, :, 2].transpose(0, 2, 1, 3)
        o = _lightning_attn(q, k, v, slopes)
        out = o.transpose(0, 2, 1, 3).reshape(b, l, c) @ w_proj + b_proj
        return out

    def _L1_ffn_ref(x, gamma, beta, Wr, br, W1, b1, W2, b2):
        import jax, jax.numpy as jnp
        import numpy as np
        E = 8
        K = 2
        D = 64
        H = 128
        DOUT = 64
        EPS = 1e-05
        mu = jnp.mean(x, axis=-1, keepdims=True)
        var = jnp.mean(jnp.square(x - mu), axis=-1, keepdims=True)
        xn = (x - mu) * jax.lax.rsqrt(var + EPS) * gamma + beta
        logits = jnp.einsum('bsd,de->bse', xn, Wr) + br
        top_vals, top_idx = jax.lax.top_k(logits, K)
        w = jax.nn.softmax(top_vals, axis=-1)
        w_full = jnp.einsum('bsk,bske->bse', w, jax.nn.one_hot(top_idx, E, dtype=w.dtype))
        y = jnp.zeros(x.shape[:-1] + (DOUT,), x.dtype)
        for e in range(E):
            h = jax.nn.gelu(jnp.einsum('bsd,dh->bsh', xn, W1[e]) + b1[e], approximate=False)
            y_e = jnp.einsum('bsh,hd->bsd', h, W2[e]) + b2[e]
            y = y + y_e * w_full[..., e, None]
        return y
    h = _L0_tok_ref(x, L0_tok_leaf_ids, L0_tok_op_ids, L0_tok_comp_emb, L0_tok_op_emb, L0_tok_W_bin, L0_tok_b_bin, L0_tok_gamma, L0_tok_beta)
    h = h + _L0_attn_ref(_layernorm(h, axis=-1), L0_attn_Wq, L0_attn_Wk, L0_attn_Wv, L0_attn_Wo, L0_attn_bo, L0_attn_g1, L0_attn_b1, L0_attn_W1, L0_attn_bf1, L0_attn_W2, L0_attn_bf2, L0_attn_g2, L0_attn_b2)
    h = h + _L0_ffn_ref(_layernorm(h, axis=-1), L0_ffn_ln_w, L0_ffn_ln_b, L0_ffn_W, L0_ffn_b)
    h = h + _L1_attn_ref(_layernorm(h, axis=-1), L1_attn_w_qkv, L1_attn_w_proj, L1_attn_b_proj, L1_attn_slopes)
    h = h + _L1_ffn_ref(_layernorm(h, axis=-1), L1_ffn_gamma, L1_ffn_beta, L1_ffn_Wr, L1_ffn_br, L1_ffn_W1, L1_ffn_b1, L1_ffn_W2, L1_ffn_b2)
    return h

_drawn_inputs = setup_inputs


def setup_inputs(seed=0):
    import zlib

    import numpy as np

    out = dict(_drawn_inputs(seed))
    spreads = {'L0_tok_b_bin': (0.0, 0.1),
     'L0_tok_gamma': (1.0, 0.2),
     'L0_tok_beta': (0.0, 0.1),
     'L0_attn_bo': (0.0, 0.1),
     'L0_attn_g1': (1.0, 0.6),
     'L0_attn_b1': (0.0, 0.8),
     'L0_attn_bf1': (0.0, 0.1),
     'L0_attn_bf2': (0.0, 0.1),
     'L0_attn_g2': (1.0, 0.6),
     'L0_attn_b2': (0.0, 0.8),
     'L0_ffn_ln_w': (1.0, 0.2),
     'L0_ffn_ln_b': (0.0, 0.1),
     'L1_attn_b_proj': (0.0, 0.345),
     'L1_ffn_br': (0.0, 0.8)}
    factors = {'L0_attn_Wq': 8.0,
     'L0_attn_Wk': 8.0,
     'L0_attn_Wv': 7.704,
     'L0_attn_Wo': 6.112,
     'L1_attn_w_qkv': 8.0,
     'L1_attn_w_proj': 8.0,
     'L1_attn_slopes': 8.0,
     'L1_ffn_gamma': 8.0,
     'L1_ffn_beta': 8.0,
     'L1_ffn_Wr': 8.0,
     'L1_ffn_W1': 8.0,
     'L1_ffn_b1': 39.166,
     'L1_ffn_W2': 8.0,
     'L1_ffn_b2': 57.274}
    for name, (base, spread) in spreads.items():
        noise = np.random.default_rng([zlib.crc32(name.encode()), seed]).standard_normal(out[name].shape)
        drawn = base * np.exp(spread * noise) if base else spread * noise
        out[name] = jnp.asarray(drawn.astype(out[name].dtype))
    for name, factor in factors.items():
        out[name] = (out[name] * factor).astype(out[name].dtype)
    return out
```

```python
from contextlib import ExitStack

import concourse.bass as bass
from concourse import mybir
import numpy as np

P = 128
D = 64
S = 2048
HALVES = 2
COLS = S // HALVES
CH = 512
NCH = COLS // CH
NB = COLS // P
NG = 4
GC = COLS // NG
NT = S // P
HEADS = 8
DH = D // HEADS
LAYERS = 4
FF = 256
ITERS = 30
E = 8
HID = 128
LEAVES = 8
SLOTS = 16
EPS = 1e-5
NORM_GAIN = 100.0

F32 = mybir.dt.float32
BF16 = mybir.dt.bfloat16
I32 = mybir.dt.int32
U32 = mybir.dt.uint32
ALU = mybir.AluOpType
ACT = mybir.ActivationFunctionType
AX = mybir.AxisListType

WEIGHTS = [
    ("comp", 2 * D), ("op", D), ("tok_gamma_row", D), ("tok_beta_row", D),
    ("wo_T", P), ("wl_T", P), ("wr_T", P), ("tok_b", 1), ("tok_gamma", 1), ("tok_beta", 1),
    ("ffn_wT", P), ("ffn_ln_w", 1), ("ffn_ln_b", 1), ("ffn_b", 1),
    ("dec_q", P), ("dec_k", P), ("dec_kv", 2 * P), ("dec_proj", P), ("dec_b", 1),
    ("slope_col", 1), ("slope_row", D), ("slope_heads", HEADS),
    ("moe_gamma", 1), ("moe_beta", 1), ("moe_wr", 2 * E), ("moe_br", 2 * E), ("moe_b1", E), ("moe_b2", E),
    ("moe_w2", E * D), ("moe_w1", HALVES * E * HID),
]
CONSTS = [
    ("center", P), ("mean", P), ("ident", P), ("swap", P), ("both", P), ("pe", COLS), ("head_block", D),
    ("head_mask", HALVES * HEADS), ("diff", P), ("causal", P), ("pos_row", P), ("pos_left", 1),
    ("vocab", 3), ("pick_expert", E * P), ("pick_block", NB), ("iota_e", E),
]
LAYER_A = [("wqv", 2 * P), ("wk", P), ("wo", D), ("g1", 1), ("b1", 1), ("bo", 1)]
LAYER_B = [("w1", HALVES * FF), ("w2", 2 * D), ("bf1", 2), ("bf2", 1), ("g2", 1), ("b2", 1)]


def offsets(table):
    out, at = {}, 0
    for name, width in table:
        out[name] = (at, width)
        at += width
    return out, at


W_AT, W_N = offsets(WEIGHTS)
C_AT, C_N = offsets(CONSTS)
A_AT, A_N = offsets(LAYER_A)
B_AT, B_N = offsets(LAYER_B)


LATE = W_AT["dec_q"][0]


def build(nc, token_idx, id_table, weights, consts, layer_a, layer_b, out):
    ctx = ExitStack()
    with ctx:
        def sb(name, shape, dt=F32):
            return ctx.enter_context(nc.sbuf_tensor(name, shape, dt))

        def sem(name):
            return ctx.enter_context(nc.semaphore(name))

        wt = sb("wt", [P, W_N])
        ct = sb("ct", [P, C_N])
        la = sb("la", [P, A_N])
        lb = sb("lb", [P, B_N])

        def W(name):
            at, n = W_AT[name]
            return wt[:, at:at + n]

        def C(name):
            at, n = C_AT[name]
            return ct[:, at:at + n]

        def A(name):
            at, n = A_AT[name]
            return la[:, at:at + n]

        def B(name):
            at, n = B_AT[name]
            return lb[:, at:at + n]

        def big(name):
            return sb(name, [P, COLS])

        def chunk(t, c):
            return t[:, c * CH:(c + 1) * CH]

        def group(t, g):
            return t[:, g * GC:(g + 1) * GC]

        ps = ctx.enter_context(nc.psum_tensor("ps", [P, 8, CH], F32))

        idx = sb("idx", [P, NT], I32)
        ids = sb("ids", [P, NT, SLOTS], I32)
        ids_b = sb("ids_b", [P, NT, SLOTS], BF16)
        ident_b = sb("ident_b", [P, P], BF16)
        keep_b = sb("keep_b", [P, P], BF16)
        eps_col = sb("eps_col", [P, 1])
        ids_T = sb("ids_T", [P, COLS], BF16)
        ids_wide = sb("ids_wide", [P, 3, CH], BF16)
        stats = sb("stats", [P, 2, 6])
        mv = sb("mv", [P, 2, 2])
        tab_rstd = sb("tab_rstd", [P, 2])
        comp_n = sb("comp_n", [P, 2, D])
        comp_T = sb("comp_T", [D, 2 * P])
        op_T = sb("op_T", [D, D])
        tree_w = sb("tree_w", [P, 3, P])
        tree_bias = sb("tree_bias", [P, 1])
        leaf_hi = sb("leaf_hi", [P, 2, P], BF16)
        leaf_mid = sb("leaf_mid", [P, 2, P], BF16)
        leaf_lo = sb("leaf_lo", [P, 2, P], BF16)
        op_hm = sb("op_hm", [P, D], BF16)
        op_lo = sb("op_lo", [P, D], BF16)
        leaf_rest = sb("leaf_rest", [P, 2, P])
        op_rest = sb("op_rest", [P, D])
        wide = sb("wide", [P, NT * HEADS * (D + DH)])
        node1 = [wide[:, k * COLS:(k + 1) * COLS] for k in range(4)]
        node2 = [wide[:, k * COLS:(k + 1) * COLS] for k in range(4, 6)]
        v_heads = wide[:, :].rearrange("p (n w) -> p n w", n=NT)
        space = sb("space", [P, 8, COLS])

        def view(k, inner=None):
            t = space[:, k, :]
            return t if inner is None else t.rearrange("p (n w) -> p n w", w=inner)

        onehot = space[:, 5:8, :].rearrange("p a b -> p (a b)").bitcast(BF16)[:, 0:2 * 5 * CH] \
            .rearrange("p (g r n) -> p g r n", g=2, r=5)


        hres = big("hres")
        x = big("x")
        hn = big("hn")
        norm_tmp = big("norm_tmp")
        squares = big("squares")
        logs = big("logs")
        rstd = big("rstd")

        k_exp = view(0)
        k_tok = view(1, P)
        v_tok = view(2, D)
        q_max = sb("q_max", [P, NT, HEADS])
        q_sh = view(3, D)
        q_e = view(4, D)
        q_sum = sb("q_sum", [P, NT, HEADS])
        q_inv = sb("q_inv", [P, NT, HEADS])
        q_n = view(5, D)
        q_T = view(6)
        k_part = sb("k_part", [P, 2])
        k_own = sb("k_own", [P, 1])
        k_neg = sb("k_neg", [P, 1])
        k_sums = sb("k_sums", [P, 2])
        k_half = sb("k_half", [P, 1])
        k_inv = sb("k_inv", [P, 1])
        ctx_T = sb("ctx_T", [P, D])
        mix = sb("mix", [P, P])
        act_h = sb("act_h", [P, 4, CH])

        f_state = view(0)
        f_tanh = view(1)
        f_mid = view(2)
        f_sig = view(3)
        f_gate = view(4)
        f_wt = sb("f_wt", [P, P])
        f_w = sb("f_w", [P, 2 * P])
        f_sumsq = sb("f_sumsq", [P, NG, 4])
        f_rstd_sb = sb("f_rstd_sb", [P, NG, 4])
        minus_half = sb("minus_half", [P, 4])
        f_squares = sb("f_squares", [P, NT, D + 1])
        f_tok = view(5)
        f_c = sb("f_c", [P, 1])
        f_c_gain = sb("f_c_gain", [P, 1])

        dq = view(0)
        dk = view(1)
        dqd = view(2)
        q_heads = sb("q_heads", [P, 2, HEADS, CH])
        kd_tok = view(3, D)
        dv_tok = view(4, D)
        slope_neg = sb("slope_neg", [P, 1])
        row_neg = sb("row_neg", [P, D])
        heads_neg = sb("heads_neg", [P, HEADS])
        q_decay = sb("q_decay", [P, P])
        k_decay = sb("k_decay", [P, D])
        block_decay = sb("block_decay", [P, 1])
        decay = sb("decay", [P, HEADS, P])
        updates = view(5, D)
        state = view(6, D)
        state_rows = sb("state_rows", [P, NT, D])
        scored = act_h
        d_out = view(7)

        xn = view(0)
        logits = sb("logits", [P, NT, E])
        top = sb("top", [P, NT, 8])
        top_i = sb("top_i", [P, NT, 8], U32)
        top_f = sb("top_f", [P, NT, 2])
        gap = sb("gap", [P, NT])
        gap_e = sb("gap_e", [P, NT])
        den = sb("den", [P, NT])
        w_1 = sb("w_1", [P, NT])
        w_2 = sb("w_2", [P, NT])
        pick_1 = sb("pick_1", [P, NT, E])
        pick_2 = sb("pick_2", [P, NT, E])
        share_1 = sb("share_1", [P, NT, E])
        share_2 = sb("share_2", [P, NT, E])
        share = sb("share", [P, NT, E])
        share_T = sb("share_T", [P, P])
        share_d = view(1, P)
        share_w = view(2, CH)
        y_part = view(3, CH)
        out_tok = view(4, P)

        weights_in = sem("weights_in")
        late_weights_in = sem("late_weights_in")
        row_stats = sem("row_stats")
        rows_summed = sem("rows_summed")
        hn_ready = sem("hn_ready")
        consts_in = sem("consts_in")
        idx_in = sem("idx_in")
        ids_in = sem("ids_in")
        layer_a_in = sem("layer_a_in")
        layer_b_in = sem("layer_b_in")
        pool_zeroed = sem("pool_zeroed")
        vec_order = sem("vec_order")
        act_order = sem("act_order")
        pe_prep = sem("pe_prep")
        vec_prep = sem("vec_prep")
        act_prep = sem("act_prep")
        ids_wide_ps = sem("ids_wide_ps")
        ids_wide_sb = sem("ids_wide_sb")
        onehot_ready = sem("onehot_ready")
        tree_sq = sem("tree_sq")
        tree_var = sem("tree_var")
        tree_rstd = sem("tree_rstd")
        tree_node = sem("tree_node")
        ln_in = sem("ln_in")
        ln_centered = sem("ln_centered")
        ln_squared = sem("ln_squared")
        ln_var = sem("ln_var")
        ln_rstd = sem("ln_rstd")
        qv_ready = sem("qv_ready")
        k_ready = sem("k_ready")
        k_max = sem("k_max")
        k_swapped = sem("k_swapped")
        k_negmax = sem("k_negmax")
        k_exped = sem("k_exped")
        k_turned = sem("k_turned")
        k_tok_ready = sem("k_tok_ready")
        v_tok_ready = sem("v_tok_ready")
        q_shifted = sem("q_shifted")
        q_exped = sem("q_exped")
        q_normed = sem("q_normed")
        q_turned = sem("q_turned")
        q_T_ready = sem("q_T_ready")
        k_summed = sem("k_summed")
        k_total = sem("k_total")
        ctx_ready = sem("ctx_ready")
        ctx_masked = sem("ctx_masked")
        mix_ps = sem("mix_ps")
        mix_ready = sem("mix_ready")
        attn_ready = sem("attn_ready")
        up_ready = sem("up_ready")
        gelu_ready = sem("gelu_ready")
        down_ready = sem("down_ready")
        f_state_ready = sem("f_state_ready")
        f_tanh_ready = sem("f_tanh_ready")
        f_mid_ready = sem("f_mid_ready")
        f_sig_ready = sem("f_sig_ready")
        f_gate_ready = sem("f_gate_ready")
        f_squared = sem("f_squared")
        f_rstd = sem("f_rstd")
        f_products = sem("f_products")
        f_summed = sem("f_summed")
        f_scaled = sem("f_scaled")
        f_turned = sem("f_turned")
        pool_order = sem("pool_order")
        d_qk_ps = sem("d_qk_ps")
        d_kv_ps = sem("d_kv_ps")
        d_q_ready = sem("d_q_ready")
        d_k_ready = sem("d_k_ready")
        d_kv_ready = sem("d_kv_ready")
        d_heads_ready = sem("d_heads_ready")
        d_upd_ps = sem("d_upd_ps")
        d_state_ready = sem("d_state_ready")
        d_scores = sem("d_scores")
        d_scored = sem("d_scored")
        d_block_out = sem("d_block_out")
        d_out_sb = sem("d_out_sb")
        d_proj = sem("d_proj")
        logits_ps = sem("logits_ps")
        gap_ready = sem("gap_ready")
        gap_exped = sem("gap_exped")
        share_ready = sem("share_ready")
        share_turned = sem("share_turned")
        share_d_ready = sem("share_d_ready")
        share_w_ps = sem("share_w_ps")
        share_w_ready = sem("share_w_ready")
        m_up = sem("m_up")
        m_gelu = sem("m_gelu")
        m_down = sem("m_down")
        m_added = sem("m_added")
        final_turned = sem("final_turned")
        final_tok = sem("final_tok")
        stored = sem("stored")

        class Order:

            def __init__(self, eng, s):
                self.eng, self.s, self.n, self.loop = eng, s, 0, None

            def did(self, ins):
                ins.then_inc(self.s, 1)
                self.n += 1

            def wait(self):
                n = self.n
                if self.loop is not None:
                    i, base, per = self.loop
                    n = i * per + n
                self.eng.wait_ge(self.s, n)

            def enter(self, i, per):
                self.loop = (i, self.n, per)

            def leave(self, count):
                _, base, per = self.loop
                assert self.n - base == per, self.n - base
                self.n = base + per * count
                self.loop = None

        UNITS = [(1, k, c) for k in range(4) for c in range(NCH)] \
            + [(2, k, c) for k in range(2) for c in range(NCH)] + [(3, 0, c) for c in range(NCH)]
        OP_SLOT = {1: LEAVES, 2: LEAVES + 4, 3: LEAVES + 6}
        KEEP_SLOT = SLOTS - 1
        GROUPS = [(n, half) for n in range(len(UNITS)) for half in range(HALVES)]

        def bank(n):
            return ps[:, n, :]

        def runs(s, back, ending, t):
            return back > t if ending else not (isinstance(s, int) and s < back)

        block = ctx.enter_context(nc.Block())

        @block.sync
        def _(sp):
            sp.dma_start(idx[:, :], token_idx).then_inc(idx_in, 16)
            sp.dma_start(wt[:, 0:LATE], weights[:, 0:LATE]).then_inc(weights_in, 16)
            sp.dma_start(la[:, :], layer_a[0]).then_inc(layer_a_in, 16)
            sp.dma_start(lb[:, :], layer_b[0]).then_inc(layer_b_in, 16)
            sp.dma_start(wt[:, LATE:W_N], weights[:, LATE:W_N]).then_inc(late_weights_in, 16)
            for i in range(1, LAYERS):
                sp.wait_ge(attn_ready, i * NCH)
                sp.wait_ge(ln_in, i * 2 * NCH + NCH)
                sp.dma_start(la[:, :], layer_a[i]).then_inc(layer_a_in, 16)
                sp.wait_ge(down_ready, i * NCH)
                sp.wait_ge(ln_in, i * 2 * NCH + 2 * NCH)
                sp.dma_start(lb[:, :], layer_b[i]).then_inc(layer_b_in, 16)
            sp.wait_ge(final_tok, NCH)
            for half in range(HALVES):
                sp.dma_start(out[0, half * COLS:(half + 1) * COLS, :].rearrange("(j p) d -> p j d", p=P),
                             out_tok[:, :, half * D:(half + 1) * D]).then_inc(stored, 16)
            sp.wait_ge(stored, 16 * HALVES)

        @block.gpsimd
        def _(pool):
            pool.wait_ge(idx_in, 16)
            for n in range(NT):
                pool.indirect_dma_start(ids[:, n, :], None, id_table,
                                        bass.IndirectOffsetOnAxis(ap=idx[:, n:n + 1], axis=0)).then_inc(ids_in, 16)
            nc.gpsimd.memset(mix[:, :], 0.0).then_inc(pool_zeroed, 1)
            nc.gpsimd.memset(ctx_T[:, :], 0.0).then_inc(pool_zeroed, 1)
            nc.gpsimd.memset(state_rows[:, :, :], 0.0).then_inc(pool_zeroed, 1)
            pool.wait_ge(ln_in, NCH)
            nc.gpsimd.memset(wide[:, :], 0.0).then_inc(pool_zeroed, 1)
            nc.gpsimd.memset(minus_half[:, :], -0.5).then_inc(pool_order, 1)
            nc.gpsimd.memset(f_squares[:, :, D:D + 1], EPS * NORM_GAIN ** 2 * D).then_inc(pool_order, 1)
            pool.wait_ge(pool_order, 2)
            with pool.Fori(0, ITERS) as i:
                for g in range(NG):
                    pool.wait_ge(f_summed, i * NG + (g + 1))
                    nc.gpsimd.tensor_tensor(f_rstd_sb[:, g, :], f_sumsq[:, g, :], minus_half[:, :], ALU.pow).then_inc(f_rstd, 1)

        @block.tensor
        def _(pe):
            def mm(o, l, r, start=True, stop=True, **kw):
                return nc.tensor.matmul(o, l, r, start=start, stop=stop, **kw)

            pe.wait_ge(weights_in, 16)
            pe.wait_ge(consts_in, 16)
            for k, name in enumerate(("wo_T", "wl_T", "wr_T")):
                mm(bank(0)[:, k * P:(k + 1) * P], W(name), C("center"))
            mm(bank(1)[:, 0:1], C("center"), W("tok_b")).then_inc(pe_prep, 1)
            pe.wait_ge(vec_prep, 1)
            for k in range(2):
                nc.tensor.transpose(bank(2)[0:D, k * P:(k + 1) * P], comp_n[:, k, :], C("ident"))
            nc.tensor.transpose(bank(2)[0:D, 2 * P:2 * P + D], W("op")[0:D, :], C("ident")[0:D, 0:D]).then_inc(pe_prep, 1)
            pe.wait_ge(vec_prep, 2)
            for j in range(NB):
                t = ps[:, 3, :].bitcast(BF16)[0:HALVES * SLOTS, j * P:(j + 1) * P]
                last = nc.tensor.transpose(t, ids_b[:, 2 * j:2 * j + 2, :].rearrange("p h s -> p (h s)"), ident_b[:, :])
            last.then_inc(pe_prep, 1)
            pe.wait_ge(vec_prep, 3)
            for k in range(2):
                for side in range(2):
                    mm(bank(4)[:, k * P + side * D:k * P + (side + 1) * D], comp_T[:, k * P:(k + 1) * P],
                       tree_w[0:D, 1 + side, 0:D])
            mm(bank(5)[0:D, 0:D], op_T[:, :], tree_w[0:D, 0, 0:D])
            mm(bank(5)[D:P, 0:D], op_T[:, :], tree_w[0:D, 0, 0:D]).then_inc(pe_prep, 1)

            pe.wait_ge(vec_prep, 5)
            pe.wait_ge(act_prep, 2)

            def spread(g):
                n, half = GROUPS[g]
                level, k, c = UNITS[n]
                if g >= 1:
                    pe.wait_ge(ids_wide_sb, g)
                slots = [2 * k, 2 * k + 1, OP_SLOT[1] + k] if level == 1 else [OP_SLOT[level] + k]
                for b, slot in enumerate(slots):
                    last = mm(bank(b), ident_b[:, half * SLOTS + slot:half * SLOTS + slot + 1].broadcast_to([P, P]), chunk(ids_T, c))
                last.then_inc(ids_wide_ps, 1)

            def gathered(g):
                n, half = GROUPS[g]
                level, k, c = UNITS[n]
                o = ps[half * D:(half + 1) * D, 3 + n % 2, :]
                pe.wait_ge(onehot_ready, g + 1)
                hot = onehot[:, g % 2, :, :]
                first = level == 1
                if level == 1:
                    for part in (leaf_hi, leaf_mid, leaf_lo):
                        for side in range(2):
                            for v in range(2):
                                mm(o, part[:, v, side * D:(side + 1) * D], hot[:, 2 * side + v, :], first, False,
                                   skip_group_check=True)
                                first = False
                mm(o, op_hm[:, :], hot[:, 4, :], False, False, skip_group_check=True)
                return mm(o, op_lo[:, :], hot[:, 4, :], False, True, skip_group_check=True)

            def variance(n):
                pe.wait_ge(tree_sq, n + 1)
                mm(bank(5 + n % 2), C("mean"), squares[:, (n % 2) * CH:(n % 2 + 1) * CH]).then_inc(tree_var, 1)

            spread(0)
            for g in range(len(GROUPS)):
                n, half = GROUPS[g]
                level, k, c = UNITS[n]
                if g + 1 < len(GROUPS):
                    spread(g + 1)
                if half == 0 and n >= 2:
                    pe.wait_ge(tree_node, n - 1)
                if half == 0 and level > 1:
                    src = node1 if level == 2 else node2
                    pe.wait_ge(tree_node, [m for m, u in enumerate(UNITS) if u == (level - 1, 2 * k + 1, c)][0] + 1)
                    mm(bank(3 + n % 2), tree_w[:, 1, :], chunk(src[2 * k], c), True, False, skip_group_check=True)
                    mm(bank(3 + n % 2), tree_w[:, 2, :], chunk(src[2 * k + 1], c), False, False, skip_group_check=True)
                gathered(g).then_inc(rows_summed, 1)
                if half == 1 and n >= 1:
                    variance(n - 1)
            variance(len(UNITS) - 1)
            pe.wait_ge(ids_wide_sb, len(GROUPS))
            for c in range(NCH):
                mm(bank(c), keep_b[:, :], chunk(ids_T, c)).then_inc(pe_prep, 1)

            mm(bank(7)[:, 0:P], C("center"), f_wt[:, :])
            mm(bank(7)[:, P:P + 1], W("ffn_wT"), W("ffn_ln_b")).then_inc(pe_prep, 1)

            def ln(n, n_in):
                for c in range(NCH):
                    pe.wait_ge(ln_in, n_in * NCH + (c + 1))
                    mm(bank(c), C("center"), chunk(x, c)).then_inc(ln_centered, 1)
                for c in range(NCH):
                    pe.wait_ge(ln_squared, n * NCH + (c + 1))
                    mm(bank(2 + c), C("mean"), chunk(squares, c)).then_inc(ln_var, 1)

            ln(0, 0)
            with pe.Fori(0, LAYERS) as i:
                ln(i * 2 + 1, i * 2 + 1)
                pe.wait_ge(layer_a_in, i * 16 + 16)
                for c in range(NCH):
                    pe.wait_ge(hn_ready, i * 2 * NCH + (c + 1))
                    mm(bank(c), A("wk"), chunk(hn, c)).then_inc(k_ready, 1)
                for j in range(NB):
                    last = mm(ps[:, 4 + j // 2, (j % 2) * 2 * P:(j % 2 + 1) * 2 * P], hn[:, j * P:(j + 1) * P], A("wqv"))
                    if j % 2 == 1:
                        last.then_inc(qv_ready, 1)
                pe.wait_ge(k_max, i + 1)
                mm(bank(2)[:, 0:1], C("swap"), k_own[:, :]).then_inc(k_swapped, 1)
                pe.wait_ge(k_negmax, i + 1)
                for c in range(NCH):
                    pe.wait_ge(k_exped, i * NCH + (c + 1))
                    for j in range(4 * c, 4 * c + 4):
                        last = nc.tensor.transpose(ps[:, 2 + c, (j % 4) * P:(j % 4 + 1) * P],
                                                   k_exp[:, j * P:(j + 1) * P], C("ident"))
                    last.then_inc(k_turned, 1)
                pe.wait_ge(v_tok_ready, i * 4 + 4)
                for n in range(NT):
                    j, half = n // 2, n % 2
                    if n % 8 == 0:
                        pe.wait_ge(k_tok_ready, i * NCH + (n // 8 + 1))
                    last = mm(ps[0:D, 0, 0:D], v_tok[:, n, :], k_tok[:, j, half * D:(half + 1) * D],
                              n == 0, n == NT - 1)
                last.then_inc(ctx_ready, 1)
                pe.wait_ge(k_summed, i + 1)
                mm(bank(1)[:, 0:1], C("both"), k_half[:, :]).then_inc(k_total, 1)
                pe.wait_ge(ctx_masked, i + 1)
                mm(ps[0:D, 2, 0:D], ctx_T[:, :], A("wo"))
                mm(ps[D:P, 2, 0:D], ctx_T[:, :], A("wo")).then_inc(mix_ps, 1)
                for c in range(NCH):
                    pe.wait_ge(q_normed, i * NCH + (c + 1))
                    for j in range(4 * c, 4 * c + 4):
                        last = nc.tensor.transpose(ps[:, 4 + c, (j % 4) * P:(j % 4 + 1) * P],
                                                   q_n[:, 2 * j:2 * j + 2, :].rearrange("p h d -> p (h d)"), C("ident"))
                    last.then_inc(q_turned, 1)
                pe.wait_ge(mix_ready, i + 1)
                for c in range(NCH):
                    pe.wait_ge(q_T_ready, i * NCH + (c + 1))
                    mm(bank(6 + c), mix[:, :], chunk(q_T, c)).then_inc(attn_ready, 1)
                ln(i * 2 + 2, i * 2 + 2)
                pe.wait_ge(layer_b_in, i * 16 + 16)
                ups = [(c, half, m) for c in range(NCH) for half in range(HALVES) for m in range(2)]

                def down(u):
                    c, half, m = ups[u]
                    pe.wait_ge(gelu_ready, i * len(ups) + (u + 1))
                    last = mm(ps[half * D:(half + 1) * D, c, :], B("w2")[:, m * D:(m + 1) * D], act_h[:, u % 4, :],
                              m == 0, m == 1)
                    if u % 4 == 3:
                        last.then_inc(down_ready, 1)

                for u, (c, half, m) in enumerate(ups):
                    if u % 4 == 0:
                        pe.wait_ge(hn_ready, i * 2 * NCH + (NCH + c + 1))
                    if u >= 4:
                        pe.wait_ge(gelu_ready, i * len(ups) + (u - 3))
                    mm(bank(4 + u % 4), B("w1")[:, (half * 2 + m) * P:(half * 2 + m + 1) * P], chunk(hn, c)).then_inc(up_ready, 1)
                    if u >= 2:
                        down(u - 2)
                down(len(ups) - 2)
                down(len(ups) - 1)

            N9 = 1 + 2 * LAYERS
            ln(N9, N9 + 1)
            for g in range(NG):
                pe.wait_ge(f_state_ready, g // 2 + 1)
                mm(bank(4 + g)[:, 0:GC], C("ident"), group(f_state, g)).then_inc(f_turned, 1)

            def slot(s, t, ending=False):
                if runs(s, 3, ending, t):
                    g = (t - 3) % NG
                    pe.wait_ge(f_scaled, s - 2)
                    for k in range(2):
                        j = 2 * g + k
                        last = nc.tensor.transpose(bank(4 + g)[:, k * P:(k + 1) * P], f_tok[:, j * P:(j + 1) * P], C("ident"))
                    last.then_inc(f_turned, 1)
                if not ending:
                    pe.wait_ge(f_gate_ready, s + 1)
                    for k in range(2):
                        j = 2 * t + k
                        last = mm(bank(t)[:, k * 2 * P:(k + 1) * 2 * P], f_gate[:, j * P:(j + 1) * P], f_w[:, :])
                    last.then_inc(f_products, 1)

            for t in range(NG):
                slot(t, t)
            with pe.Fori(1, ITERS) as i:
                for t in range(NG):
                    slot(i * NG + t, t)
            for t in range(3):
                slot(ITERS * NG + t, t, True)

            ln(N9 + 1, N9 + 2)
            pe.wait_ge(late_weights_in, 16)
            pe.wait_ge(hn_ready, (2 * LAYERS + 1) * NCH)
            for c in range(NCH):
                mm(bank(c), W("dec_q"), chunk(hn, c)).then_inc(d_qk_ps, 1)
            for c in range(NCH):
                mm(bank(2 + c), W("dec_k"), chunk(hn, c)).then_inc(d_qk_ps, 1)
            for j in range(NB):
                last = mm(ps[:, 4 + j // 2, (j % 2) * 2 * P:(j % 2 + 1) * 2 * P], hn[:, j * P:(j + 1) * P], W("dec_kv"))
                if j % 2 == 1:
                    last.then_inc(d_kv_ps, 1)
            pe.wait_ge(d_kv_ready, 4)
            for n in range(NT):
                mm(ps[0:D, 4 + n // 8, (n % 8) * D:(n % 8 + 1) * D], kd_tok[:, n, :], dv_tok[:, n, :])
                last = mm(ps[D:P, 4 + n // 8, (n % 8) * D:(n % 8 + 1) * D], kd_tok[:, n, :], dv_tok[:, n, :])
            last.then_inc(d_upd_ps, 1)
            score_units = [(j, half, g) for c in range(NCH) for half in range(HALVES)
                           for j in range(4 * c, 4 * c + 4) for g in range(2)]

            def score(u):
                j, half, g = score_units[u]
                quarter = u // 8
                if u % 8 == 0:
                    pe.wait_ge(d_heads_ready, (quarter + 1) * HEADS)
                if u >= 4:
                    pe.wait_ge(d_scored, u - 3)
                rhs = q_heads[:, quarter % 2, 4 * g:4 * g + 4, (j % 4) * P:(j % 4 + 1) * P]
                mm(bank(u % 4), dk[:, j * P:(j + 1) * P], rhs).then_inc(d_scores, 1)

            def spend(u):
                j, half, g = score_units[u]
                n = 2 * j + half
                o = ps[half * D:(half + 1) * D, 6 + j // 4, (j % 4) * P:(j % 4 + 1) * P]
                if g == 0:
                    mm(o, state_rows[:, n, :], dqd[:, j * P:(j + 1) * P], True, False)
                pe.wait_ge(d_scored, u + 1)
                for h in range(4):
                    last = mm(o, v_heads[:, n, (4 * g + h) * D:(4 * g + h + 1) * D], scored[:, u % 4, h * P:(h + 1) * P], False,
                              g == 1 and h == 3)
                last.then_inc(d_block_out, 1)

            pe.wait_ge(d_q_ready, NCH)
            pe.wait_ge(d_k_ready, NCH)
            score(0)
            score(1)
            pe.wait_ge(d_state_ready, 2)
            for u in range(len(score_units)):
                if u + 2 < len(score_units):
                    score(u + 2)
                spend(u)
            for c in range(NCH):
                pe.wait_ge(d_out_sb, c + 1)
                mm(bank(c), W("dec_proj"), chunk(d_out, c)).then_inc(d_proj, 1)

            ln(N9 + 2, N9 + 3)
            ln(N9 + 3, N9 + 4)
            pe.wait_ge(hn_ready, (2 * LAYERS + 2) * NCH)
            for j in range(NB):
                last = mm(bank(4)[:, j * 2 * E:(j + 1) * 2 * E], xn[:, j * P:(j + 1) * P], W("moe_wr"))
            last.then_inc(logits_ps, 1)
            units = [(e, c, half) for e in range(E) for c in range(NCH) for half in range(HALVES)]

            def up(u):
                e, c, half = units[u]
                if u >= 4:
                    pe.wait_ge(m_gelu, u - 3)
                mm(bank(u % 4), W("moe_w1")[:, (half * E + e) * P:(half * E + e + 1) * P], chunk(xn, c)).then_inc(m_up, 1)

            up(0)
            up(1)
            up(2)
            pe.wait_ge(share_ready, 1)
            nc.tensor.transpose(bank(5)[:, 0:P], share[:, :, :].rearrange("p n e -> p (n e)"), C("ident")).then_inc(share_turned, 1)
            pe.wait_ge(share_d_ready, 1)
            for u in range(len(units)):
                e, c, half = units[u]
                v = u // 2
                if half == 0:
                    if v >= 2:
                        pe.wait_ge(share_w_ready, v - 1)
                    mm(bank(6 + v % 2), C("pick_expert")[:, e * P:(e + 1) * P],
                       share_d[:, 4 * c:4 * c + 4, :].rearrange("p j t -> p (j t)")).then_inc(share_w_ps, 1)
                    if v >= 2:
                        pe.wait_ge(m_added, v - 1)
                if u + 3 < len(units):
                    up(u + 3)
                pe.wait_ge(m_gelu, u + 1)
                last = mm(ps[half * D:(half + 1) * D, 4 + v % 2, :], W("moe_w2")[:, e * D:(e + 1) * D], act_h[:, u % 4, :])
                if half == 1:
                    last.then_inc(m_down, 1)
            for c in range(NCH):
                pe.wait_ge(m_added, (E - 1) * NCH + c + 1)
                for j in range(4 * c, 4 * c + 4):
                    last = nc.tensor.transpose(ps[:, c, (j % 4) * P:(j % 4 + 1) * P], hres[:, j * P:(j + 1) * P], C("ident"))
                last.then_inc(final_turned, 1)

        @block.scalar
        def _(act):
            order = Order(act, act_order)
            A_ = nc.scalar.activation
            log_exp = "natural_log_exp_and_others"
            nc.scalar.preload_act_table_set(log_exp)
            act.dma_start(ct[:, :], consts).then_inc(consts_in, 16)
            act.wait_ge(weights_in, 16)
            act.wait_ge(row_stats, 4)
            order.did(A_(tab_rstd[:, :], mv[:, :, 1], ACT.Ln, bias=eps_col[:, 0:1]))
            order.wait()
            A_(tab_rstd[:, :], tab_rstd[:, :], ACT.Exp, scale=-0.5).then_inc(act_prep, 1)
            act.wait_ge(pe_prep, 3)
            act.wait_ge(vec_prep, 4)
            A_(ids_T[0:HALVES * SLOTS, :], ps[:, 3, :].bitcast(BF16)[0:HALVES * SLOTS, :], ACT.Copy).then_inc(act_prep, 1)

            def widen(g):
                n, half = GROUPS[g]
                level, k, c = UNITS[n]
                act.wait_ge(ids_wide_ps, g + 1)
                if g >= 1:
                    act.wait_ge(onehot_ready, g)
                w = 3 if level == 1 else 1
                A_(ids_wide[:, 0:w, :], ps[:, 0:w, :], ACT.Copy).then_inc(ids_wide_sb, 1)

            def root_mean(n):
                act.wait_ge(rows_summed, HALVES * (n + 1))
                if n >= 2:
                    act.wait_ge(tree_var, n - 1)
                sq = squares[:, (n % 2) * CH:(n % 2 + 1) * CH]
                A_(sq, bank(3 + n % 2), ACT.Square, bias=tree_bias[:, 0:1]).then_inc(tree_sq, 1)

            def root_rest(n):
                lg = logs[:, (n % 2) * CH:(n % 2 + 1) * CH]
                act.wait_ge(tree_var, n + 1)
                order.did(A_(lg, bank(5 + n % 2), ACT.Ln, bias=eps_col[:, 0:1]))
                if n >= 2:
                    act.wait_ge(tree_node, n - 1)
                order.wait()
                A_(rstd[:, (n % 2) * CH:(n % 2 + 1) * CH], lg, ACT.Exp, scale=-0.5).then_inc(tree_rstd, 1)

            widen(0)
            for g in range(len(GROUPS)):
                n, half = GROUPS[g]
                if g + 1 < len(GROUPS):
                    widen(g + 1)
                if half == 1:
                    root_mean(n)
                    if n >= 1:
                        root_rest(n - 1)
            root_rest(len(UNITS) - 1)

            def ln(n):
                for c in range(NCH):
                    act.wait_ge(ln_centered, n * NCH + (c + 1))
                    A_(chunk(squares, c), bank(c), ACT.Square).then_inc(ln_squared, 1)
                for c in range(NCH):
                    act.wait_ge(ln_var, n * NCH + (c + 1))
                    order.did(A_(chunk(logs, c), bank(2 + c), ACT.Ln, bias=eps_col[:, 0:1]))
                for c in range(NCH):
                    if c == 0:
                        order.wait()
                    A_(chunk(rstd, c), chunk(logs, c), ACT.Exp, scale=-0.5).then_inc(ln_rstd, 1)

            ln(0)
            with act.Fori(0, LAYERS) as i:
                nc.scalar.preload_act_table_set(log_exp)
                order.enter(i, 2 * NCH)
                ln(i * 2 + 1)
                act.wait_ge(k_negmax, i + 1)
                for c in range(NCH):
                    A_(chunk(k_exp, c), bank(c), ACT.Exp, bias=k_neg[:, 0:1],
                       accum_out=k_sums[:, c:c + 1]).then_inc(k_exped, 1)
                for c in range(NCH):
                    for b in range(2 * c, 2 * c + 2):
                        act.wait_ge(q_shifted, i * 4 + (b + 1))
                        A_(v_tok[:, 4 * b:4 * b + 4, :], bank(4 + b).rearrange("p (n w) -> p n w", n=4)[:, :, D:2 * D],
                           ACT.Copy).then_inc(v_tok_ready, 1)
                    A_(q_e[:, 8 * c:8 * c + 8, :], q_sh[:, 8 * c:8 * c + 8, :], ACT.Exp).then_inc(q_exped, 1)
                for c in range(NCH):
                    act.wait_ge(k_turned, i * NCH + (c + 1))
                    A_(k_tok[:, 4 * c:4 * c + 4, :], bank(2 + c).rearrange("p (j w) -> p j w", j=4),
                       ACT.Copy).then_inc(k_tok_ready, 1)
                for c in range(NCH):
                    act.wait_ge(q_turned, i * NCH + (c + 1))
                    A_(chunk(q_T, c), bank(4 + c), ACT.Copy).then_inc(q_T_ready, 1)
                ln(i * 2 + 2)
                act.wait_ge(layer_b_in, i * 16 + 16)
                for u in range(8):
                    act.wait_ge(up_ready, i * 8 + (u + 1))
                    if u == 4:
                        act.wait_ge(down_ready, i * NCH + 1)
                    A_(act_h[:, u % 4, :], bank(4 + u % 4), ACT.Gelu, bias=B("bf1")[:, u % 2:u % 2 + 1]).then_inc(gelu_ready, 1)
            order.leave(LAYERS)

            nc.scalar.preload_act_table_set(log_exp)
            ln(1 + 2 * LAYERS)
            nc.scalar.preload_act_table(ACT.Sigmoid)

            def slot(s, t, ending=False):
                if not ending:
                    act.wait_ge(f_turned, s + 1)
                    A_(group(f_tanh, t), bank(4 + t)[:, 0:GC], ACT.Tanh, bias=f_c[:, 0:1], scale=1.0 / NORM_GAIN).then_inc(f_tanh_ready, 1)
                    act.wait_ge(f_mid_ready, s + 1)
                    A_(group(f_sig, t), group(f_mid, t), ACT.Sigmoid, scale=1.0 / NORM_GAIN).then_inc(f_sig_ready, 1)
                if runs(s, 1, ending, t):
                    g = (t - 1) % NG
                    act.wait_ge(f_products, s)
                    A_(f_squares[:, 4 * g:4 * g + 4, 0:D].rearrange("p (j h) d -> p j h d", h=HALVES),
                       bank(g).rearrange("p (j w) -> p j w", w=2 * P)[:, :, P:2 * P].rearrange("p j (h d) -> p j h d", h=HALVES),
                       ACT.Square).then_inc(f_squared, 1)

            for t in range(NG):
                slot(t, t)
            with act.Fori(1, ITERS) as i:
                for t in range(NG):
                    slot(i * NG + t, t)
            for t in range(3):
                slot(ITERS * NG + t, t, True)

            nc.scalar.preload_act_table_set(log_exp)
            ln(2 + 2 * LAYERS)
            act.wait_ge(vec_prep, 6)
            A_(q_decay[:, :], C("pos_row"), ACT.Exp, scale=slope_neg[:, 0:1]).then_inc(act_prep, 1)
            A_(k_decay[:, :], row_neg[:, :], ACT.Exp, scale=C("pos_left")).then_inc(act_prep, 1)
            A_(block_decay[:, :], slope_neg[:, :], ACT.Exp, scale=float(P)).then_inc(act_prep, 1)
            for h in range(HEADS):
                A_(decay[:, h, :], C("diff"), ACT.Exp, scale=heads_neg[:, h:h + 1]).then_inc(act_prep, 1)
            for c in range(NCH):
                act.wait_ge(d_qk_ps, c + 1)
                A_(chunk(dq, c), bank(c), ACT.Copy, scale=DH ** -0.5).then_inc(d_q_ready, 1)
            for c in range(NCH):
                act.wait_ge(d_qk_ps, NCH + c + 1)
                A_(chunk(dk, c), bank(2 + c), ACT.Copy).then_inc(d_k_ready, 1)
            act.wait_ge(d_q_ready, NCH)
            for quarter in range(NCH * HALVES):
                c, half = quarter // 2, quarter % 2
                if quarter >= 2:
                    act.wait_ge(d_scores, (quarter - 1) * 8)
                for h in range(HEADS):
                    m = half * HEADS + h
                    A_(q_heads[:, quarter % 2, h, :], chunk(dq, c), ACT.Copy, scale=C("head_mask")[:, m:m + 1]).then_inc(d_heads_ready, 1)
            for c in range(NCH):
                act.wait_ge(d_block_out, (c + 1) * 16)
                A_(chunk(d_out, c), bank(6 + c), ACT.Copy).then_inc(d_out_sb, 1)

            ln(3 + 2 * LAYERS)
            ln(4 + 2 * LAYERS)
            act.wait_ge(gap_ready, 1)
            A_(gap_e[:, :], gap[:, :], ACT.Exp).then_inc(gap_exped, 1)
            for u in range(E * NCH * HALVES):
                e, v = u // (NCH * HALVES), u // HALVES
                act.wait_ge(m_up, u + 1)
                if u >= 4 and u % 2 == 0:
                    act.wait_ge(m_down, v - 1)
                A_(act_h[:, u % 4, :], bank(u % 4), ACT.Gelu, bias=W("moe_b1")[:, e:e + 1]).then_inc(m_gelu, 1)
                if u % 2 == 1:
                    act.wait_ge(share_w_ps, v + 1)
                    if v >= 2:
                        act.wait_ge(m_added, v - 1)
                    A_(share_w[:, v % 2, :], bank(6 + v % 2), ACT.Copy).then_inc(share_w_ready, 1)
            for c in range(NCH):
                act.wait_ge(final_turned, c + 1)
                A_(out_tok[:, 4 * c:4 * c + 4, :], bank(c).rearrange("p (j w) -> p j w", j=4), ACT.Copy).then_inc(final_tok, 1)

        @block.vector
        def _(dve):
            order = Order(dve, vec_order)
            V = nc.vector

            def TT(o, a, b, op):
                return V.tensor_tensor(o, a, b, op)

            def TS(o, a, s1, s2, op0, op1):
                return V.tensor_scalar(o, a, s1, s2, op0, op1)

            def STT(o, a, s, b, op0, op1):
                return V.scalar_tensor_tensor(out=o, in0=a, scalar=s, in1=b, op0=op0, op1=op1)

            order.did(V.memset(eps_col[:, :], EPS))
            dve.wait_ge(weights_in, 16)
            comp = W("comp").rearrange("p (k d) -> p k d", k=2)
            for k in range(2):
                V.bn_stats(stats[:, k, :], comp[:, k, :]).then_inc(row_stats, 1)
            dve.wait_ge(row_stats, 2)
            for k in range(2):
                V.bn_aggr(mv[:, k, :], stats[:, k, :]).then_inc(row_stats, 1)
            dve.wait_ge(act_prep, 1)
            for k in range(2):
                order.did(TS(comp_n[:, k, :], comp[:, k, :], mv[:, k, 0:1], tab_rstd[:, k:k + 1], ALU.subtract, ALU.mult))
            order.wait()
            for k in range(2):
                order.did(TT(comp_n[:, k, :], comp_n[:, k, :], W("tok_gamma_row"), ALU.mult))
            order.wait()
            last = TT(comp_n[:, 0, :], comp_n[:, 0, :], W("tok_beta_row"), ALU.add)
            order.did(last)
            TT(comp_n[:, 1, :], comp_n[:, 1, :], W("tok_beta_row"), ALU.add).then_inc(vec_prep, 1)
            order.wait()
            dve.wait_ge(consts_in, 16)
            order.did(V.tensor_copy(ident_b[:, :], C("ident")))
            order.did(V.memset(ids_T[:, :], 0.0))
            dve.wait_ge(ids_in, 16 * NT)
            order.did(V.tensor_copy(ids_b[:, :, :], ids[:, :, :]))
            order.wait()
            TS(ids_b[:, :, KEEP_SLOT], idx[:, :], 1.0, None, ALU.is_gt, ALU.bypass).then_inc(vec_prep, 1)
            dve.wait_ge(pe_prep, 2)
            order.did(V.tensor_copy(tree_w[:, :, :], bank(0)[:, 0:3 * P].rearrange("p (k n) -> p k n", k=3)))
            order.did(V.tensor_copy(tree_bias[:, :], bank(1)[:, 0:1]))
            order.did(V.tensor_copy(comp_T[:, :], bank(2)[0:D, 0:2 * P]))
            V.tensor_copy(op_T[:, :], bank(2)[0:D, 2 * P:2 * P + D]).then_inc(vec_prep, 1)
            order.did(V.tensor_copy(keep_b[:, 0:D], ident_b[:, KEEP_SLOT:KEEP_SLOT + 1].broadcast_to([P, D])))
            V.tensor_copy(keep_b[:, D:P], ident_b[:, SLOTS + KEEP_SLOT:SLOTS + KEEP_SLOT + 1].broadcast_to([P, D])).then_inc(vec_prep, 1)
            dve.wait_ge(pe_prep, 4)
            leaf = bank(4)[:, 0:2 * P].rearrange("p (k n) -> p k n", k=2)
            opp = bank(5)[:, 0:D]
            order.did(V.tensor_copy(leaf_hi[:, :, :], leaf))
            order.did(V.tensor_copy(op_hm[:, :], opp))
            order.wait()
            order.did(TT(leaf_rest[:, :, :], leaf, leaf_hi[:, :, :], ALU.subtract))
            order.did(TT(op_rest[:, :], opp, op_hm[:, :], ALU.subtract))
            order.wait()
            order.did(V.tensor_copy(leaf_mid[:, :, :], leaf_rest[:, :, :]))
            order.did(V.tensor_copy(op_lo[:, :], op_rest[:, :]))
            order.wait()
            order.did(TT(leaf_lo[:, :, :], leaf_rest[:, :, :], leaf_mid[:, :, :], ALU.subtract))
            order.did(V.tensor_copy(op_hm[D:P, :], op_lo[D:P, :]))
            order.wait()
            order.did(TT(op_rest[:, :], op_rest[:, :], op_lo[:, :], ALU.subtract))
            order.wait()
            order.did(V.tensor_copy(op_lo[0:D, :], op_rest[0:D, :]))
            order.did(V.memset(op_lo[D:P, :], 0.0))
            order.wait()
            TS(f_wt[:, :], W("ffn_wT"), W("ffn_ln_w"), None, ALU.mult, ALU.bypass).then_inc(vec_prep, 1)

            def compare(g):
                n, half = GROUPS[g]
                level, k, c = UNITS[n]
                dve.wait_ge(ids_wide_sb, g + 1)
                if g >= 2:
                    dve.wait_ge(rows_summed, g - 1)
                hot = onehot[:, g % 2, :, :]
                if level == 1:
                    for side in range(2):
                        for v in range(2):
                            TS(hot[:, 2 * side + v, :], ids_wide[:, side, :], C("vocab")[:, v:v + 1], None,
                               ALU.is_equal, ALU.bypass)
                TS(hot[:, 4, :], ids_wide[:, 2 if level == 1 else 0, :], C("vocab")[:, 2:3], None,
                   ALU.is_equal, ALU.bypass).then_inc(onehot_ready, 1)

            def normal(n):
                level, k, c = UNITS[n]
                dve.wait_ge(tree_rstd, n + 1)
                o = chunk(norm_tmp, n % 2)
                r = chunk(rstd, n % 2)
                order.did(STT(o, bank(3 + n % 2), tree_bias[:, 0:1], r, ALU.add, ALU.mult))
                order.wait()
                dst = node1[k] if level == 1 else node2[k] if level == 2 else hres
                TS(chunk(dst, c), o, W("tok_gamma"), W("tok_beta"), ALU.mult, ALU.add).then_inc(tree_node, 1)

            compare(0)
            for g in range(len(GROUPS)):
                n, half = GROUPS[g]
                if g + 1 < len(GROUPS):
                    compare(g + 1)
                if half == 1 and n >= 1:
                    normal(n - 1)
            normal(len(UNITS) - 1)
            dve.wait_ge(tree_node, len(UNITS))
            for c in range(NCH):
                dve.wait_ge(pe_prep, 5 + c)
                order.did(TT(chunk(hres, c), chunk(hres, c), bank(c), ALU.mult))
            order.wait()
            for c in range(NCH):
                V.tensor_copy(chunk(x, c), chunk(hres, c)).then_inc(ln_in, 1)
            dve.wait_ge(pe_prep, 7)
            dve.wait_ge(late_weights_in, 16)
            order.did(V.tensor_copy(f_w[:, P:2 * P], C("center")))
            order.did(TS(f_w[:, 0:P], bank(7)[:, 0:P], NORM_GAIN * D ** 0.5, None, ALU.mult, ALU.bypass))
            order.did(TT(f_c[:, :], bank(7)[:, P:P + 1], W("ffn_b"), ALU.add))
            order.did(TS(slope_neg[:, :], W("slope_col"), -1.0, None, ALU.mult, ALU.bypass))
            order.did(TS(row_neg[:, :], W("slope_row"), -1.0, None, ALU.mult, ALU.bypass))
            order.did(TS(heads_neg[:, :], W("slope_heads"), -1.0, None, ALU.mult, ALU.bypass))
            order.wait()
            TS(f_c_gain[:, :], f_c[:, :], NORM_GAIN, None, ALU.mult, ALU.bypass).then_inc(vec_prep, 1)

            def ln(n, c, dst, inc, gamma=None, beta=None, plus=None, post=None):
                dve.wait_ge(ln_rstd, n * NCH + (c + 1))
                if gamma is None and plus is None:
                    TT(chunk(dst, c), bank(c), chunk(rstd, c), ALU.mult).then_inc(inc, 1)
                    return
                order.did(TT(chunk(norm_tmp, c), bank(c), chunk(rstd, c), ALU.mult))
                order.wait()
                if plus is not None:
                    TT(chunk(dst, c), chunk(norm_tmp, c), chunk(plus, c), ALU.add).then_inc(inc, 1)
                else:
                    TS(chunk(dst, c), chunk(norm_tmp, c), gamma, beta, ALU.mult, ALU.add).then_inc(inc, 1)

            for c in range(NCH):
                ln(0, c, x, ln_in, plus=C("pe"))
            with dve.Fori(0, LAYERS) as i:
                order.enter(i, 16)
                dve.wait_ge(layer_a_in, i * 16 + 16)
                for c in range(NCH):
                    ln(i * 2 + 1, c, hn, hn_ready, gamma=A("g1"), beta=A("b1"))
                for c in range(NCH):
                    dve.wait_ge(k_ready, i * NCH + (c + 1))
                    order.did(V.tensor_reduce(k_part[:, c:c + 1], bank(c), AX.X, ALU.max))
                order.wait()
                TT(k_own[:, :], k_part[:, 0:1], k_part[:, 1:2], ALU.max).then_inc(k_max, 1)
                for b in range(4):
                    dve.wait_ge(qv_ready, i * 4 + (b + 1))
                    q = bank(4 + b).rearrange("p (n w) -> p n w", n=4)[:, :, 0:D].rearrange("p n (h d) -> p n h d", h=HEADS)
                    order.did(V.tensor_reduce(q_max[:, 4 * b:4 * b + 4, :], q, AX.X, ALU.max))
                    if b == 0:
                        dve.wait_ge(k_swapped, i + 1)
                        dve.wait_ge(k_max, i + 1)
                        TS(k_neg[:, :], bank(2)[:, 0:1], k_own[:, 0:1], -1.0, ALU.max, ALU.mult).then_inc(k_negmax, 1)
                    order.wait()
                    ins = TT(q_sh[:, 4 * b:4 * b + 4, :].rearrange("p n (h d) -> p n h d", h=HEADS), q,
                             q_max[:, 4 * b:4 * b + 4, :].unsqueeze(3).broadcast_to([P, 4, HEADS, DH]), ALU.subtract)
                    ins.then_inc(q_shifted, 1)
                for c in range(NCH):
                    t = slice(8 * c, 8 * c + 8)
                    dve.wait_ge(q_exped, i * NCH + (c + 1))
                    order.did(V.tensor_reduce(q_sum[:, t, :], q_e[:, t, :].rearrange("p n (h d) -> p n h d", h=HEADS), AX.X, ALU.add))
                    order.wait()
                    order.did(V.reciprocal(q_inv[:, t, :], q_sum[:, t, :]))
                    order.wait()
                    TT(q_n[:, t, :].rearrange("p n (h d) -> p n h d", h=HEADS),
                       q_e[:, t, :].rearrange("p n (h d) -> p n h d", h=HEADS),
                       q_inv[:, t, :].unsqueeze(3).broadcast_to([P, 8, HEADS, DH]), ALU.mult).then_inc(q_normed, 1)
                dve.wait_ge(k_exped, i * NCH + NCH)
                TT(k_half[:, :], k_sums[:, 0:1], k_sums[:, 1:2], ALU.add).then_inc(k_summed, 1)
                dve.wait_ge(ctx_ready, i + 1)
                dve.wait_ge(pool_zeroed, 3)
                TT(ctx_T[0:D, :], ps[0:D, 0, 0:D], C("head_block")[0:D, :], ALU.mult).then_inc(ctx_masked, 1)
                dve.wait_ge(k_total, i + 1)
                order.did(V.reciprocal(k_inv[:, :], bank(1)[:, 0:1]))
                order.wait()
                dve.wait_ge(mix_ps, i + 1)
                order.did(TS(mix[0:D, 0:D], ps[0:D, 2, 0:D], k_inv[0:D, 0:1], DH ** -0.5, ALU.mult, ALU.mult))
                order.wait()
                TS(mix[D:P, D:P], ps[D:P, 2, 0:D], k_inv[D:P, 0:1], DH ** -0.5, ALU.mult, ALU.mult).then_inc(mix_ready, 1)
                for c in range(NCH):
                    dve.wait_ge(attn_ready, i * NCH + (c + 1))
                    STT(chunk(x, c), bank(6 + c), A("bo"), chunk(x, c), ALU.add, ALU.add).then_inc(ln_in, 1)
                dve.wait_ge(layer_b_in, i * 16 + 16)
                for c in range(NCH):
                    ln(i * 2 + 2, c, hn, hn_ready, gamma=B("g2"), beta=B("b2"))
                for c in range(NCH):
                    dve.wait_ge(down_ready, i * NCH + (c + 1))
                    dve.wait_ge(ln_in, (i * 2 + 3) * NCH)
                    STT(chunk(x, c), bank(c), B("bf2"), chunk(x, c), ALU.add, ALU.add).then_inc(ln_in, 1)
            order.leave(LAYERS)
            N9 = 1 + 2 * LAYERS

            def residual(c, src):
                order.did(TT(chunk(hres, c), chunk(hres, c), src, ALU.add))
                order.wait()
                V.tensor_copy(chunk(x, c), chunk(hres, c)).then_inc(ln_in, 1)

            dve.wait_ge(ln_in, (N9 + 1) * NCH)
            for c in range(NCH):
                residual(c, chunk(x, c))

            dve.wait_ge(pool_order, 2)
            for c in range(NCH):
                dve.wait_ge(ln_rstd, N9 * NCH + (c + 1))
                order.did(TT(chunk(norm_tmp, c), bank(c), chunk(rstd, c), ALU.mult))
                order.wait()
                TS(chunk(f_state, c), chunk(norm_tmp, c), NORM_GAIN, f_c_gain[:, 0:1], ALU.mult, ALU.subtract).then_inc(f_state_ready, 1)

            def slot(s, t, ending=False):
                if not ending:
                    dve.wait_ge(f_tanh_ready, s + 1)
                    STT(group(f_mid, t), bank(4 + t)[:, 0:GC], f_c_gain[:, 0:1], group(f_tanh, t), ALU.add, ALU.add).then_inc(f_mid_ready, 1)
                if runs(s, 3, ending, t):
                    g = (t - 3) % NG
                    dve.wait_ge(f_rstd, s - 2)
                    TT(group(f_tok, g).rearrange("p (j h d) -> p j h d", j=2, h=HALVES),
                       bank(g).rearrange("p (j w) -> p j w", w=2 * P)[:, :, 0:P].rearrange("p j (h d) -> p j h d", h=HALVES),
                       f_rstd_sb[:, g, :].rearrange("p (j h) -> p j h", j=2).unsqueeze(3).broadcast_to([P, 2, HALVES, D]), ALU.mult).then_inc(f_scaled, 1)
                if not ending:
                    dve.wait_ge(f_sig_ready, s + 1)
                    TT(group(f_gate, t), group(f_mid, t), group(f_sig, t), ALU.mult).then_inc(f_gate_ready, 1)
                if runs(s, 1, ending, t):
                    g = (t - 1) % NG
                    dve.wait_ge(f_squared, s)
                    V.tensor_reduce(f_sumsq[:, g, :], f_squares[:, 4 * g:4 * g + 4, :], AX.X, ALU.add).then_inc(f_summed, 1)

            for t in range(NG):
                slot(t, t)
            with dve.Fori(1, ITERS) as i:
                for t in range(NG):
                    slot(i * NG + t, t)
            for t in range(3):
                slot(ITERS * NG + t, t, True)
            for c in range(NCH):
                dve.wait_ge(f_turned, ITERS * NG + 2 * c + 2)
                for g in (2 * c, 2 * c + 1):
                    order.did(TS(group(norm_tmp, g), bank(4 + g)[:, 0:GC], 1.0 / NORM_GAIN, f_c[:, 0:1], ALU.mult, ALU.add))
                order.wait()
                residual(c, chunk(norm_tmp, c))

            for c in range(NCH):
                ln(N9 + 1, c, hn, hn_ready)
            dve.wait_ge(act_prep, 13)
            dve.wait_ge(pool_zeroed, 4)
            for h in range(HEADS):
                last = TT(decay[:, h, :], decay[:, h, :], C("causal"), ALU.mult)
                order.did(last)
            dve.wait_ge(pool_zeroed, 4)
            for b in range(4):
                dve.wait_ge(d_kv_ps, b + 1)
                kv = bank(4 + b).rearrange("p (n w) -> p n w", n=4)
                order.did(TT(kd_tok[:, 4 * b:4 * b + 4, :], kv[:, :, 0:D],
                             k_decay[:, :].unsqueeze(1).broadcast_to([P, 4, D]), ALU.mult))
                order.did(V.tensor_copy(dv_tok[:, 4 * b:4 * b + 4, :], kv[:, :, D:2 * D]))
                V.tensor_copy(v_heads[:, 4 * b:4 * b + 4, :].rearrange("p n (h w) -> p n h w", h=HEADS)[:, :, :, 0:DH],
                              kv[:, :, D:2 * D].rearrange("p n (h d) -> p n h d", h=HEADS)).then_inc(d_kv_ready, 1)
            dve.wait_ge(d_q_ready, NCH)
            order.did(TT(dqd[:, :].rearrange("p (j t) -> p j t", j=NB), dq[:, :].rearrange("p (j t) -> p j t", j=NB),
                         q_decay[:, :].unsqueeze(1).broadcast_to([P, NB, P]), ALU.mult))
            dve.wait_ge(d_upd_ps, 1)
            order.did(TT(updates[:, :, :], ps[:, 4:6, :].rearrange("p b (n d) -> p (b n) d", d=D),
                         C("head_block").unsqueeze(1).broadcast_to([P, NT, D]), ALU.mult))
            order.did(V.memset(state[:, 0, :], 0.0))
            order.wait()
            tiles = [2 * j + half for half in range(HALVES) for j in range(NB)]
            for s in range(1, NT):
                order.did(STT(state[:, s, :], state[:, s - 1, :], block_decay[:, 0:1], updates[:, tiles[s - 1], :],
                              ALU.mult, ALU.add))
                order.wait()
            for half in range(HALVES):
                rows = slice(half * D, (half + 1) * D)
                V.tensor_copy(state_rows[rows, :, :].rearrange("p (j h) d -> p j h d", h=HALVES)[:, :, half, :],
                              state[rows, half * NB:(half + 1) * NB, :]).then_inc(d_state_ready, 1)
            for u in range(2 * NT):
                g = u % 2
                dve.wait_ge(d_scores, u + 1)
                if u >= 4:
                    dve.wait_ge(d_block_out, u - 3)
                TT(scored[:, u % 4, :], bank(u % 4), decay[:, 4 * g:4 * g + 4, :].rearrange("p h t -> p (h t)"),
                   ALU.mult).then_inc(d_scored, 1)
            for c in range(NCH):
                dve.wait_ge(d_proj, c + 1)
                order.did(TS(chunk(norm_tmp, c), bank(c), W("dec_b"), None, ALU.add, ALU.bypass))
                order.wait()
                residual(c, chunk(norm_tmp, c))

            for c in range(NCH):
                ln(N9 + 2, c, x, ln_in)
            for c in range(NCH):
                ln(N9 + 3, c, xn, hn_ready, gamma=W("moe_gamma"), beta=W("moe_beta"))
            dve.wait_ge(logits_ps, 1)
            order.did(TT(logits[:, :, :], bank(4)[:, 0:NT * E].rearrange("p (n e) -> p n e", e=E),
                         W("moe_br")[:, 0:E].unsqueeze(1).broadcast_to([P, NT, E]), ALU.add))
            order.wait()
            for n in range(NT):
                order.did(V.max(top[:, n, :], logits[:, n, :]))
            order.wait()
            for n in range(NT):
                order.did(V.max_index(top_i[:, n, :], top[:, n, :], logits[:, n, :]))
            TT(gap[:, :], top[:, :, 1], top[:, :, 0], ALU.subtract).then_inc(gap_ready, 1)
            order.wait()
            order.did(V.tensor_copy(top_f[:, :, :], top_i[:, :, 0:2]))
            order.wait()
            iota = C("iota_e").unsqueeze(1).broadcast_to([P, NT, E])
            order.did(TT(pick_1[:, :, :], iota, top_f[:, :, 0:1].broadcast_to([P, NT, E]), ALU.is_equal))
            order.did(TT(pick_2[:, :, :], iota, top_f[:, :, 1:2].broadcast_to([P, NT, E]), ALU.is_equal))
            dve.wait_ge(gap_exped, 1)
            order.did(TS(den[:, :], gap_e[:, :], 1.0, None, ALU.add, ALU.bypass))
            order.wait()
            order.did(V.reciprocal(w_1[:, :], den[:, :]))
            order.wait()
            order.did(TT(w_2[:, :], gap_e[:, :], w_1[:, :], ALU.mult))
            order.did(TT(share_1[:, :, :], pick_1[:, :, :], w_1[:, :].unsqueeze(2).broadcast_to([P, NT, E]), ALU.mult))
            order.wait()
            order.did(TT(share_2[:, :, :], pick_2[:, :, :], w_2[:, :].unsqueeze(2).broadcast_to([P, NT, E]), ALU.mult))
            order.wait()
            TT(share[:, :, :], share_1[:, :, :], share_2[:, :, :], ALU.add).then_inc(share_ready, 1)
            dve.wait_ge(share_turned, 1)
            order.did(V.tensor_copy(share_T[:, :], bank(5)[:, 0:P]))
            order.wait()
            for j in range(NB):
                ins = TS(share_d[:, j, :], share_T[:, :], C("pick_block")[:, j:j + 1], None, ALU.mult, ALU.bypass)
            ins.then_inc(share_d_ready, 1)
            for v in range(E * NCH):
                e, c = v // 2, v % 2
                dve.wait_ge(m_down, v + 1)
                dve.wait_ge(share_w_ready, v + 1)
                order.did(STT(y_part[:, v % 2, :], bank(4 + v % 2), W("moe_b2")[:, e:e + 1], share_w[:, v % 2, :], ALU.add, ALU.mult))
                order.wait()
                if v >= 2:
                    dve.wait_ge(m_added, v - 1)
                TT(chunk(hres, c), chunk(hres, c), y_part[:, v % 2, :], ALU.add).then_inc(m_added, 1)


def pack(table, columns, n):
    at, width = offsets(table)
    out = np.zeros(n + (P, width), np.float32)
    for name, (a, w) in at.items():
        v = np.asarray(columns[name])
        out[..., a:a + w] = v
    return out


def twice(v):
    return np.concatenate([v, v]).reshape(P, 1)


def diagonal(*blocks):
    a, b = blocks
    out = np.zeros(a.shape[:-2] + (P, a.shape[-1] + b.shape[-1]), np.float32)
    out[..., :D, :a.shape[-1]] = a
    out[..., D:, a.shape[-1]:] = b
    return out


def make_consts():
    c = {}
    eye = np.eye(P, dtype=np.float32)
    same = np.kron(np.eye(HALVES), np.ones((D, D)))
    p = np.arange(P)
    c["center"] = eye - same / D
    c["mean"] = same / D
    c["ident"] = eye
    c["swap"] = eye[(p + D) % P]
    c["both"] = eye + c["swap"]
    pos = np.arange(S, dtype=np.float32)[:, None]
    div = np.exp(np.arange(0, D, 2, dtype=np.float32) * np.float32(-np.log(10000.0) / D)).astype(np.float32)
    table = np.zeros((S, D), np.float32)
    table[:, 0::2] = np.sin((pos * div).astype(np.float32))
    table[:, 1::2] = np.cos((pos * div).astype(np.float32))
    c["pe"] = table.reshape(HALVES, COLS, D).transpose(0, 2, 1).reshape(P, COLS)
    f = p % D
    c["head_block"] = (f[:, None] // DH == np.arange(D)[None, :] // DH)
    c["head_mask"] = (p[:, None] // DH == np.arange(HALVES * HEADS)[None, :])
    c["diff"] = np.maximum(p[None, :] - p[:, None], 0)
    c["causal"] = p[None, :] >= p[:, None]
    c["pos_row"] = np.broadcast_to(p[None, :], (P, P))
    c["pos_left"] = (P - p)[:, None]
    c["vocab"] = np.stack([p, p + P, f], 1)
    c["pick_block"] = p[:, None] // (HALVES * E) == np.arange(NB)[None, :]
    c["pick_expert"] = np.concatenate([(p[:, None] % E == e) & (p[:, None] // E % HALVES == p[None, :] // D)
                                       for e in range(E)], 1)
    c["iota_e"] = np.broadcast_to(np.arange(E)[None, :], (P, E))
    return pack(CONSTS, c, ())


def kernel(**inputs):
    import concourse.bacc as bacc
    from concourse.bass_utils import run_bass_kernel_spmd

    a = {k: np.asarray(v) for k, v in inputs.items()}
    tok = {k[7:]: v for k, v in a.items() if k.startswith("L0_tok_")}
    att = {k[8:]: v for k, v in a.items() if k.startswith("L0_attn_")}
    ffn = {k[7:]: v for k, v in a.items() if k.startswith("L0_ffn_")}
    dec = {k[8:]: v for k, v in a.items() if k.startswith("L1_attn_")}
    moe = {k[7:]: v for k, v in a.items() if k.startswith("L1_ffn_")}

    w = {}
    w["comp"] = tok["comp_emb"].reshape(2, P, D).transpose(1, 0, 2).reshape(P, 2 * D)
    w["op"] = np.concatenate([tok["op_emb"], np.zeros((D, D), np.float32)])
    w["tok_gamma_row"] = np.broadcast_to(tok["gamma"], (P, D))
    w["tok_beta_row"] = np.broadcast_to(tok["beta"], (P, D))
    for k, name in enumerate(("wo_T", "wl_T", "wr_T")):
        t = tok["W_bin"][k * D:(k + 1) * D].T
        w[name] = diagonal(t, t)
    w["tok_b"], w["tok_gamma"], w["tok_beta"] = twice(tok["b_bin"]), twice(tok["gamma"]), twice(tok["beta"])
    w["ffn_wT"] = diagonal(ffn["W"].T, ffn["W"].T)
    w["ffn_ln_w"], w["ffn_ln_b"], w["ffn_b"] = twice(ffn["ln_w"]), twice(ffn["ln_b"]), twice(ffn["b"])
    wq, wk, wv = (dec["w_qkv"][:, k * D:(k + 1) * D] for k in range(3))
    w["dec_q"], w["dec_k"] = diagonal(wq, wq), diagonal(wk, wk)
    kv = np.concatenate([wk, wv], 1)
    w["dec_kv"] = diagonal(kv, kv)
    w["dec_proj"] = diagonal(dec["w_proj"], dec["w_proj"])
    w["dec_b"] = twice(dec["b_proj"])
    w["slope_col"] = twice(np.repeat(dec["slopes"], DH))
    w["slope_row"] = np.broadcast_to(np.repeat(dec["slopes"], DH), (P, D))
    w["slope_heads"] = np.broadcast_to(dec["slopes"], (P, HEADS))
    w["moe_gamma"], w["moe_beta"] = twice(moe["gamma"]), twice(moe["beta"])
    w["moe_wr"] = diagonal(moe["Wr"], moe["Wr"])
    w["moe_br"] = np.broadcast_to(np.concatenate([moe["br"], moe["br"]]), (P, 2 * E))
    w["moe_b1"] = moe["b1"].T
    w["moe_b2"] = np.concatenate([moe["b2"].T, moe["b2"].T])
    w["moe_w2"] = moe["W2"].transpose(1, 0, 2).reshape(HID, E * D)
    up = np.zeros((P, HALVES, E, HID), np.float32)
    for half in range(HALVES):
        up[half * D:(half + 1) * D, half] = moe["W1"].transpose(1, 0, 2)
    w["moe_w1"] = up.reshape(P, HALVES * E * HID)

    def column(v):
        return np.concatenate([v, v], 1)[:, :, None]

    la = {"wk": diagonal(att["Wk"], att["Wk"]), "wo": np.concatenate([att["Wo"], att["Wo"]], 1),
          "g1": column(att["g1"]), "b1": column(att["b1"]), "bo": column(att["bo"])}
    qv = np.concatenate([att["Wq"], att["Wv"]], 2)
    la["wqv"] = diagonal(qv, qv)
    lb = {"w1": diagonal(att["W1"], att["W1"]), "w2": att["W2"].reshape(LAYERS, 2, P, D).transpose(0, 2, 1, 3).reshape(LAYERS, P, 2 * D),
          "bf1": att["bf1"].reshape(LAYERS, 2, P).transpose(0, 2, 1), "bf2": column(att["bf2"]),
          "g2": column(att["g2"]), "b2": column(att["b2"])}

    table = np.zeros((tok["leaf_ids"].shape[0], SLOTS), np.int32)
    table[:, :LEAVES] = tok["leaf_ids"]
    table[:, LEAVES:2 * LEAVES - 1] = tok["op_ids"]
    arrays = {
        "token_idx": np.ascontiguousarray(a["x"].reshape(HALVES, NB, P).transpose(2, 1, 0).reshape(P, NT)),
        "id_table": table,
        "weights": pack(WEIGHTS, w, ()),
        "consts": make_consts(),
        "layer_a": pack(LAYER_A, la, (LAYERS,)),
        "layer_b": pack(LAYER_B, lb, (LAYERS,)),
    }
    nc = bacc.Bacc("TRN2", target_bir_lowering=False, num_devices=1)
    args = [nc.dram_tensor(name, v.shape, mybir.dt.from_np(v.dtype), kind="ExternalInput").ap() for name, v in arrays.items()]
    out = nc.dram_tensor("out", (1, S, D), F32, kind="ExternalOutput").ap()
    build(nc, *args, out)
    r = run_bass_kernel_spmd(nc, [arrays], core_ids=[0])
    return r.results[0]["out"]
```

```python
from contextlib import ExitStack

import concourse.bass as bass
from concourse import mybir
import numpy as np

P = 128
D = 64
S = 2048
HALVES = 2
COLS = S // HALVES
CH = 512
NCH = COLS // CH
NB = COLS // P
NG = 4
GC = COLS // NG
NT = S // P
HEADS = 8
DH = D // HEADS
LAYERS = 4
FF = 256
ITERS = 30
E = 8
HID = 128
LEAVES = 8
SLOTS = 16
EPS = 1e-5
NORM_GAIN = 100.0
HOT_BUFS = 4

F32 = mybir.dt.float32
BF16 = mybir.dt.bfloat16
I32 = mybir.dt.int32
U32 = mybir.dt.uint32
ALU = mybir.AluOpType
ACT = mybir.ActivationFunctionType
AX = mybir.AxisListType

WEIGHTS = [
    ("comp", 2 * D), ("op", D), ("tok_gamma_row", D), ("tok_beta_row", D),
    ("wo_T", P), ("wl_T", P), ("wr_T", P), ("tok_b", 1), ("tok_gamma", 1), ("tok_beta", 1),
    ("ffn_wT", P), ("ffn_ln_w", 1), ("ffn_ln_b", 1), ("ffn_b", 1),
    ("dec_q", P), ("dec_k", P), ("dec_kv", 2 * P), ("dec_proj", P), ("dec_b", 1),
    ("slope_col", 1), ("slope_row", D), ("slope_heads", HEADS),
    ("moe_gamma", 1), ("moe_beta", 1), ("moe_wr", 2 * E), ("moe_br", 2 * E), ("moe_b1", E), ("moe_b2", E),
    ("moe_w2", E * D), ("moe_w1", HALVES * E * HID),
]
CONSTS = [
    ("center", P), ("mean", P), ("ident", P), ("swap", P), ("both", P), ("pe", COLS), ("head_block", D),
    ("head_mask", HALVES * HEADS), ("diff", P), ("causal", P), ("pos_row", P), ("pos_left", 1),
    ("vocab", 3), ("pick_expert", E * P), ("iota_e", E),
]
LAYER_A = [("wqv", 2 * P), ("wk", P), ("wo", D), ("g1", 1), ("b1", 1), ("bo", 1)]
LAYER_B = [("w1", HALVES * FF), ("w2", 2 * D), ("bf1", 2), ("bf2", 1), ("g2", 1), ("b2", 1)]


def offsets(table):
    out, at = {}, 0
    for name, width in table:
        out[name] = (at, width)
        at += width
    return out, at


W_AT, W_N = offsets(WEIGHTS)
C_AT, C_N = offsets(CONSTS)
A_AT, A_N = offsets(LAYER_A)
B_AT, B_N = offsets(LAYER_B)


LATE = W_AT["dec_q"][0]


def build(nc, token_idx, id_table, weights, consts, layer_a, layer_b, out):
    ctx = ExitStack()
    with ctx:
        def sb(name, shape, dt=F32):
            return ctx.enter_context(nc.sbuf_tensor(name, shape, dt))

        def sem(name):
            return ctx.enter_context(nc.semaphore(name))

        wt = sb("wt", [P, W_N])
        ct = sb("ct", [P, C_N])
        la = sb("la", [P, A_N])
        lb = sb("lb", [P, B_N])

        def W(name):
            at, n = W_AT[name]
            return wt[:, at:at + n]

        def C(name):
            at, n = C_AT[name]
            return ct[:, at:at + n]

        def A(name):
            at, n = A_AT[name]
            return la[:, at:at + n]

        def B(name):
            at, n = B_AT[name]
            return lb[:, at:at + n]

        def big(name):
            return sb(name, [P, COLS])

        def chunk(t, c):
            return t[:, c * CH:(c + 1) * CH]

        def group(t, g):
            return t[:, g * GC:(g + 1) * GC]

        ps = ctx.enter_context(nc.psum_tensor("ps", [P, 8, CH], F32))

        idx = sb("idx", [P, NT], I32)
        ids = sb("ids", [P, NT, SLOTS], I32)
        ids_b = sb("ids_b", [P, NT, SLOTS], BF16)
        ident_b = sb("ident_b", [P, P], BF16)
        keep_b = sb("keep_b", [P, P], BF16)
        eps_col = sb("eps_col", [P, 1])
        ids_T = sb("ids_T", [P, COLS], BF16)
        stats = sb("stats", [P, 2, 6])
        mv = sb("mv", [P, 2, 2])
        tab_rstd = sb("tab_rstd", [P, 2])
        comp_n = sb("comp_n", [P, 2, D])
        comp_T = sb("comp_T", [D, 2 * P])
        op_T = sb("op_T", [D, D])
        tree_w = sb("tree_w", [P, 3, P])
        tree_bias = sb("tree_bias", [P, 1])
        leaf_hi = sb("leaf_hi", [P, 2, P], BF16)
        leaf_mid = sb("leaf_mid", [P, 2, P], BF16)
        leaf_lo = sb("leaf_lo", [P, 2, P], BF16)
        op_hm = sb("op_hm", [P, D], BF16)
        op_lo = sb("op_lo", [P, D], BF16)
        leaf_rest = sb("leaf_rest", [P, 2, P])
        op_rest = sb("op_rest", [P, D])
        wide = sb("wide", [P, NT * HEADS * (D + DH)])
        node1 = [wide[:, k * COLS:(k + 1) * COLS] for k in range(4)]
        node2 = [wide[:, k * COLS:(k + 1) * COLS] for k in range(4, 6)]
        v_heads = wide[:, :].rearrange("p (n w) -> p n w", n=NT)
        space = sb("space", [P, 8, COLS])

        def view(k, inner=None):
            t = space[:, k, :]
            return t if inner is None else t.rearrange("p (n w) -> p n w", w=inner)

        onehot = space[:, 3:8, :].rearrange("p a b -> p (a b)").bitcast(BF16) \
            .rearrange("p (g r n) -> p g r n", g=HOT_BUFS, r=5)
        ids_wide = space[:, 1:3, :].rearrange("p a b -> p (a b)").bitcast(BF16)[:, 0:2 * 3 * CH] \
            .rearrange("p (g r n) -> p g r n", g=2, r=3)

        hres = big("hres")
        x = big("x")
        hn = big("hn")
        norm_tmp = big("norm_tmp")
        squares = big("squares")
        logs = big("logs")
        rstd = big("rstd")

        k_exp = view(0)
        k_tok = view(1, P)
        v_tok = view(2, D)
        q_max = sb("q_max", [P, NT, HEADS])
        q_sh = view(3, D)
        q_e = view(4, D)
        q_sum = sb("q_sum", [P, NT, HEADS])
        q_inv = sb("q_inv", [P, NT, HEADS])
        q_n = view(5, D)
        q_T = view(6)
        k_part = sb("k_part", [P, 2])
        k_own = sb("k_own", [P, 1])
        k_neg = sb("k_neg", [P, 1])
        k_sums = sb("k_sums", [P, 2])
        k_half = sb("k_half", [P, 1])
        k_inv = sb("k_inv", [P, 1])
        ctx_T = sb("ctx_T", [P, D])
        mix = sb("mix", [P, P])
        act_h = sb("act_h", [P, 4, CH])

        f_state = view(0)
        f_tanh = view(1)
        f_mid = view(2)
        f_sig = view(3)
        f_gate = view(4)
        f_wt = sb("f_wt", [P, P])
        f_w = sb("f_w", [P, 2 * P])
        f_sumsq = sb("f_sumsq", [P, NG, 4])
        f_rstd_sb = sb("f_rstd_sb", [P, NG, 4])
        minus_half = sb("minus_half", [P, 4])
        f_squares = sb("f_squares", [P, NT, D + 1])
        f_tok = view(5)
        f_c = sb("f_c", [P, 1])
        f_c_gain = sb("f_c_gain", [P, 1])

        dq = view(0)
        dk = view(1)
        dqd = view(2)
        q_heads = sb("q_heads", [P, 2, HALVES, HEADS, 2 * P])
        kd_tok = view(3, D)
        dv_tok = view(4, D)
        pick_b = sb("pick_b", [P, E * P], BF16)
        slope_neg = sb("slope_neg", [P, 1])
        row_neg = sb("row_neg", [P, D])
        heads_neg = sb("heads_neg", [P, HEADS])
        q_decay = sb("q_decay", [P, P])
        k_decay = sb("k_decay", [P, D])
        block_decay = sb("block_decay", [P, 1])
        decay = sb("decay", [P, HEADS, P])
        updates = view(5, D)
        state = view(6, D)
        state_rows = sb("state_rows", [P, NT, D])
        scored = act_h
        d_out = view(7)

        xn = view(0)
        logits = sb("logits", [P, NT, E])
        top = sb("top", [P, NT, 8])
        top_i = sb("top_i", [P, NT, 8], U32)
        top_f = sb("top_f", [P, NT, 2])
        gap = sb("gap", [P, NT])
        gap_e = sb("gap_e", [P, NT])
        den = sb("den", [P, NT])
        w_1 = sb("w_1", [P, NT])
        w_2 = sb("w_2", [P, NT])
        pick_1 = sb("pick_1", [P, NT, E])
        pick_2 = sb("pick_2", [P, NT, E])
        share_1 = sb("share_1", [P, NT, E])
        share_2 = sb("share_2", [P, NT, E])
        share = sb("share", [P, NT, E])
        share_rest = sb("share_rest", [P, NB, HALVES * E])
        share_parts = sb("share_parts", [P, NB, 3, HALVES * E], BF16)
        share_T = view(1).bitcast(BF16)[:, 0:COLS]
        share_w = view(2, CH)
        y_part = view(3, CH)
        out_tok = view(4, P)

        weights_in = sem("weights_in")
        late_weights_in = sem("late_weights_in")
        row_stats = sem("row_stats")
        rows_summed = sem("rows_summed")
        hn_ready = sem("hn_ready")
        consts_in = sem("consts_in")
        idx_in = sem("idx_in")
        ids_in = sem("ids_in")
        layer_a_in = sem("layer_a_in")
        layer_b_in = sem("layer_b_in")
        pool_zeroed = sem("pool_zeroed")
        slopes_ready = sem("slopes_ready")
        decay_masked = sem("decay_masked")
        v_heads_ready = sem("v_heads_ready")
        d_stated = sem("d_stated")
        vec_order = sem("vec_order")
        act_order = sem("act_order")
        pe_prep = sem("pe_prep")
        vec_prep = sem("vec_prep")
        act_prep = sem("act_prep")
        ids_wide_ps = sem("ids_wide_ps")
        ids_wide_sb = sem("ids_wide_sb")
        onehot_ready = sem("onehot_ready")
        tree_sq = sem("tree_sq")
        tree_var = sem("tree_var")
        tree_rstd = sem("tree_rstd")
        tree_node = sem("tree_node")
        ln_in = sem("ln_in")
        ln_centered = sem("ln_centered")
        ln_squared = sem("ln_squared")
        ln_var = sem("ln_var")
        ln_rstd = sem("ln_rstd")
        qv_ready = sem("qv_ready")
        k_ready = sem("k_ready")
        k_max = sem("k_max")
        k_swapped = sem("k_swapped")
        k_negmax = sem("k_negmax")
        k_exped = sem("k_exped")
        k_turned = sem("k_turned")
        k_tok_ready = sem("k_tok_ready")
        v_tok_ready = sem("v_tok_ready")
        q_shifted = sem("q_shifted")
        q_exped = sem("q_exped")
        q_normed = sem("q_normed")
        q_turned = sem("q_turned")
        q_T_ready = sem("q_T_ready")
        k_summed = sem("k_summed")
        k_total = sem("k_total")
        ctx_ready = sem("ctx_ready")
        ctx_masked = sem("ctx_masked")
        mix_ps = sem("mix_ps")
        mix_ready = sem("mix_ready")
        attn_ready = sem("attn_ready")
        up_ready = sem("up_ready")
        gelu_ready = sem("gelu_ready")
        down_ready = sem("down_ready")
        f_state_ready = sem("f_state_ready")
        f_tanh_ready = sem("f_tanh_ready")
        f_mid_ready = sem("f_mid_ready")
        f_sig_ready = sem("f_sig_ready")
        f_gate_ready = sem("f_gate_ready")
        f_squared = sem("f_squared")
        f_rstd = sem("f_rstd")
        f_products = sem("f_products")
        f_summed = sem("f_summed")
        f_scaled = sem("f_scaled")
        f_turned = sem("f_turned")
        pool_order = sem("pool_order")
        d_qk_ps = sem("d_qk_ps")
        d_kv_ps = sem("d_kv_ps")
        d_q_ready = sem("d_q_ready")
        d_k_ready = sem("d_k_ready")
        d_kv_ready = sem("d_kv_ready")
        d_heads_ready = sem("d_heads_ready")
        d_upd_ps = sem("d_upd_ps")
        d_state_ready = sem("d_state_ready")
        d_scores = sem("d_scores")
        d_scored = sem("d_scored")
        d_block_out = sem("d_block_out")
        d_out_sb = sem("d_out_sb")
        d_proj = sem("d_proj")
        logits_ps = sem("logits_ps")
        gap_ready = sem("gap_ready")
        gap_exped = sem("gap_exped")
        share_ready = sem("share_ready")
        share_turned = sem("share_turned")
        share_T_ready = sem("share_T_ready")
        share_w_ps = sem("share_w_ps")
        share_w_ready = sem("share_w_ready")
        m_up = sem("m_up")
        m_gelu = sem("m_gelu")
        m_down = sem("m_down")
        m_added = sem("m_added")
        final_turned = sem("final_turned")
        final_tok = sem("final_tok")
        stored = sem("stored")

        class Order:

            def __init__(self, eng, s):
                self.eng, self.s, self.n, self.loop = eng, s, 0, None

            def did(self, ins):
                ins.then_inc(self.s, 1)
                self.n += 1

            def wait(self):
                n = self.n
                if self.loop is not None:
                    i, base, per = self.loop
                    n = i * per + n
                self.eng.wait_ge(self.s, n)

            def enter(self, i, per):
                self.loop = (i, self.n, per)

            def leave(self, count):
                _, base, per = self.loop
                assert self.n - base == per, self.n - base
                self.n = base + per * count
                self.loop = None

        UNITS = [(1, k, c) for k in range(4) for c in range(NCH)] \
            + [(2, k, c) for k in range(2) for c in range(NCH)] + [(3, 0, c) for c in range(NCH)]
        OP_SLOT = {1: LEAVES, 2: LEAVES + 4, 3: LEAVES + 6}
        KEEP_SLOT = SLOTS - 1
        GROUPS = [(n, half) for n in range(len(UNITS)) for half in range(HALVES)]

        def bank(n):
            return ps[:, n, :]

        def runs(s, back, ending, t):
            return back > t if ending else not (isinstance(s, int) and s < back)

        block = ctx.enter_context(nc.Block())

        @block.sync
        def _(sp):
            sp.dma_start(idx[:, :], token_idx).then_inc(idx_in, 16)
            sp.dma_start(wt[:, 0:LATE], weights[:, 0:LATE]).then_inc(weights_in, 16)
            sp.dma_start(la[:, :], layer_a[0]).then_inc(layer_a_in, 16)
            sp.dma_start(lb[:, :], layer_b[0]).then_inc(layer_b_in, 16)
            sp.dma_start(wt[:, LATE:W_N], weights[:, LATE:W_N]).then_inc(late_weights_in, 16)
            for i in range(1, LAYERS):
                sp.wait_ge(attn_ready, i * NCH)
                sp.wait_ge(ln_in, i * 2 * NCH + NCH)
                sp.dma_start(la[:, :], layer_a[i]).then_inc(layer_a_in, 16)
                sp.wait_ge(down_ready, i * 8)
                sp.wait_ge(ln_in, i * 2 * NCH + 2 * NCH)
                sp.dma_start(lb[:, :], layer_b[i]).then_inc(layer_b_in, 16)
            sp.wait_ge(final_tok, NCH)
            for half in range(HALVES):
                sp.dma_start(out[0, half * COLS:(half + 1) * COLS, :].rearrange("(j p) d -> p j d", p=P),
                             out_tok[:, :, half * D:(half + 1) * D]).then_inc(stored, 16)
            sp.wait_ge(stored, 16 * HALVES)

        @block.gpsimd
        def _(pool):
            pool.wait_ge(idx_in, 16)
            for n in range(NT):
                pool.indirect_dma_start(ids[:, n, :], None, id_table,
                                        bass.IndirectOffsetOnAxis(ap=idx[:, n:n + 1], axis=0)).then_inc(ids_in, 16)
            nc.gpsimd.memset(mix[:, :], 0.0).then_inc(pool_zeroed, 1)
            nc.gpsimd.memset(state_rows[:, :, :], 0.0).then_inc(pool_zeroed, 1)
            for h in range(HEADS):
                pool.wait_ge(act_prep, h + 3)
                nc.gpsimd.tensor_tensor(decay[:, h, :], decay[:, h, :], C("causal"), ALU.mult).then_inc(decay_masked, 1)
            pool.wait_ge(ln_in, NCH)
            nc.gpsimd.memset(wide[:, :], 0.0).then_inc(pool_zeroed, 1)
            nc.gpsimd.memset(minus_half[:, :], -0.5).then_inc(pool_order, 1)
            nc.gpsimd.memset(f_squares[:, :, D:D + 1], EPS * NORM_GAIN ** 2 * D).then_inc(pool_order, 1)
            pool.wait_ge(pool_order, 2)
            with pool.Fori(0, ITERS) as i:
                for g in range(NG):
                    pool.wait_ge(f_summed, i * NG + (g + 1))
                    nc.gpsimd.tensor_tensor(f_rstd_sb[:, g, :], f_sumsq[:, g, :], minus_half[:, :], ALU.pow).then_inc(f_rstd, 1)

        @block.tensor
        def _(pe):
            def mm(o, l, r, start=True, stop=True, **kw):
                return nc.tensor.matmul(o, l, r, start=start, stop=stop, **kw)

            pe.wait_ge(weights_in, 16)
            pe.wait_ge(consts_in, 16)
            for k, name in enumerate(("wo_T", "wl_T", "wr_T")):
                mm(bank(0)[:, k * P:(k + 1) * P], W(name), C("center"))
            mm(bank(1)[:, 0:1], C("center"), W("tok_b")).then_inc(pe_prep, 1)
            pe.wait_ge(vec_prep, 1)
            for k in range(2):
                nc.tensor.transpose(bank(2)[0:D, k * P:(k + 1) * P], comp_n[:, k, :], C("ident"))
            nc.tensor.transpose(bank(2)[0:D, 2 * P:2 * P + D], W("op")[0:D, :], C("ident")[0:D, 0:D]).then_inc(pe_prep, 1)
            pe.wait_ge(vec_prep, 2)
            for j in range(NB):
                t = ps[:, 3, :].bitcast(BF16)[0:HALVES * SLOTS, j * P:(j + 1) * P]
                last = nc.tensor.transpose(t, ids_b[:, 2 * j:2 * j + 2, :].rearrange("p h s -> p (h s)"), ident_b[:, :])
            last.then_inc(pe_prep, 1)
            pe.wait_ge(vec_prep, 3)
            for k in range(2):
                for side in range(2):
                    mm(bank(4)[:, k * P + side * D:k * P + (side + 1) * D], comp_T[:, k * P:(k + 1) * P],
                       tree_w[0:D, 1 + side, 0:D])
            mm(bank(5)[0:D, 0:D], op_T[:, :], tree_w[0:D, 0, 0:D])
            mm(bank(5)[D:P, 0:D], op_T[:, :], tree_w[0:D, 0, 0:D]).then_inc(pe_prep, 1)

            pe.wait_ge(vec_prep, 5)
            pe.wait_ge(act_prep, 2)

            def spread(g):
                n, half = GROUPS[g]
                level, k, c = UNITS[n]
                if g >= 1:
                    pe.wait_ge(ids_wide_sb, g)
                slots = [2 * k, 2 * k + 1, OP_SLOT[1] + k] if level == 1 else [OP_SLOT[level] + k]
                for b, slot in enumerate(slots):
                    last = mm(bank(b), ident_b[:, half * SLOTS + slot:half * SLOTS + slot + 1].broadcast_to([P, P]), chunk(ids_T, c))
                last.then_inc(ids_wide_ps, 1)

            def passes(n):
                level = UNITS[n][0]
                out = []
                if level == 1:
                    out = [(part[:, v, side * D:(side + 1) * D], 2 * side + v)
                           for part in (leaf_hi, leaf_mid, leaf_lo) for side in range(2) for v in range(2)]
                return out + [(op_hm[:, :], 4), (op_lo[:, :], 4)]

            def gather(n, some, ending):
                for q, (part, row) in enumerate(some):
                    for half in range(HALVES):
                        last = mm(ps[half * D:(half + 1) * D, 3 + n % 2, :], part, onehot[:, (2 * n + half) % HOT_BUFS, row, :],
                                  UNITS[n][0] == 1 and not ending and q == 0, ending and q == len(some) - 1,
                                  skip_group_check=True)
                        if ending and q == len(some) - 1:
                            last.then_inc(rows_summed, 1)

            def variance(n):
                pe.wait_ge(tree_sq, n + 1)
                mm(bank(5 + n % 2), C("mean"), squares[:, (n % 2) * CH:(n % 2 + 1) * CH]).then_inc(tree_var, 1)

            for g in range(HALVES):
                spread(g)
            for n, (level, k, c) in enumerate(UNITS):
                if n + 1 < len(UNITS):
                    spread(2 * n + 2)
                if n >= 2:
                    pe.wait_ge(tree_node, n - 1)
                if level > 1:
                    src = node1 if level == 2 else node2
                    pe.wait_ge(tree_node, UNITS.index((level - 1, 2 * k + 1, c)) + 1)
                    mm(bank(3 + n % 2), tree_w[:, 1, :], chunk(src[2 * k], c), True, False, skip_group_check=True)
                    mm(bank(3 + n % 2), tree_w[:, 2, :], chunk(src[2 * k + 1], c), False, False, skip_group_check=True)
                pe.wait_ge(onehot_ready, 2 * n + 2)
                todo = passes(n)
                cut = 4 if level == 1 else 0
                gather(n, todo[:cut], False)
                if n >= 1:
                    variance(n - 1)
                if n + 1 < len(UNITS):
                    spread(2 * n + 3)
                gather(n, todo[cut:], True)
            variance(len(UNITS) - 1)
            pe.wait_ge(ids_wide_sb, len(GROUPS))
            for c in range(NCH):
                mm(bank(c), keep_b[:, :], chunk(ids_T, c)).then_inc(pe_prep, 1)

            mm(bank(7)[:, 0:P], C("center"), f_wt[:, :])
            mm(bank(7)[:, P:P + 1], W("ffn_wT"), W("ffn_ln_b")).then_inc(pe_prep, 1)

            def centre(n, c):
                pe.wait_ge(ln_in, n * NCH + (c + 1))
                mm(bank(c), C("center"), chunk(x, c)).then_inc(ln_centered, 1)

            def mean_square(n, c):
                pe.wait_ge(ln_squared, n * NCH + (c + 1))
                mm(bank(2 + c), C("mean"), chunk(squares, c)).then_inc(ln_var, 1)

            def ln(n):
                for c in range(NCH):
                    centre(n, c)
                for c in range(NCH):
                    mean_square(n, c)

            ln(0)
            ln(1)
            with pe.Fori(0, LAYERS) as i:
                pe.wait_ge(layer_a_in, i * 16 + 16)
                for c in range(NCH):
                    pe.wait_ge(hn_ready, i * 2 * NCH + (c + 1))
                    mm(bank(c), A("wk"), chunk(hn, c)).then_inc(k_ready, 1)
                    for j in range(4 * c, 4 * c + 4):
                        last = mm(ps[:, 4 + j // 2, (j % 2) * 2 * P:(j % 2 + 1) * 2 * P], hn[:, j * P:(j + 1) * P], A("wqv"))
                        if j % 2 == 1:
                            last.then_inc(qv_ready, 1)
                pe.wait_ge(k_max, i + 1)
                mm(bank(2)[:, 0:1], C("swap"), k_own[:, :]).then_inc(k_swapped, 1)
                pe.wait_ge(k_negmax, i + 1)
                for c in range(NCH):
                    pe.wait_ge(k_exped, i * NCH + (c + 1))
                    for j in range(4 * c, 4 * c + 4):
                        last = nc.tensor.transpose(ps[:, 2 + c, (j % 4) * P:(j % 4 + 1) * P],
                                                   k_exp[:, j * P:(j + 1) * P], C("ident"))
                    last.then_inc(k_turned, 1)

                def turn_queries(c):
                    pe.wait_ge(q_normed, i * NCH + (c + 1))
                    for j in range(4 * c, 4 * c + 4):
                        last = nc.tensor.transpose(ps[:, 4 + c, (j % 4) * P:(j % 4 + 1) * P],
                                                   q_n[:, 2 * j:2 * j + 2, :].rearrange("p h d -> p (h d)"), C("ident"))
                    last.then_inc(q_turned, 1)

                for c in range(NCH):
                    pe.wait_ge(v_tok_ready, i * 4 + (2 * c + 2))
                    pe.wait_ge(k_tok_ready, i * NCH + (c + 1))
                    for n in range(8 * c, 8 * c + 8):
                        j, half = n // 2, n % 2
                        last = mm(ps[half * D:(half + 1) * D, 0, 0:D], v_tok[:, n, :], k_tok[:, j, half * D:(half + 1) * D],
                                  j == 0, j == NB - 1)
                        if n == NT - 2:
                            last.then_inc(ctx_ready, 1)
                    if c == 0:
                        turn_queries(0)
                last.then_inc(ctx_ready, 1)
                pe.wait_ge(k_summed, i + 1)
                mm(bank(1)[:, 0:1], C("both"), k_half[:, :]).then_inc(k_total, 1)
                pe.wait_ge(ctx_masked, i + 1)
                mm(ps[0:D, 2, 0:D], ctx_T[:, :], A("wo"))
                mm(ps[D:P, 2, 0:D], ctx_T[:, :], A("wo")).then_inc(mix_ps, 1)
                turn_queries(1)
                pe.wait_ge(mix_ready, i + 1)
                for c in range(NCH):
                    pe.wait_ge(q_T_ready, i * NCH + (c + 1))
                    mm(bank(6 + c), mix[:, :], chunk(q_T, c)).then_inc(attn_ready, 1)
                ln(i * 2 + 2)
                pe.wait_ge(layer_b_in, i * 16 + 16)
                ups = [(c, half, m) for c in range(NCH) for m in range(2) for half in range(HALVES)]

                def up(u):
                    c, half, m = ups[u]
                    if u % 4 == 0:
                        pe.wait_ge(hn_ready, i * 2 * NCH + (NCH + c + 1))
                    if u >= 4:
                        pe.wait_ge(gelu_ready, i * len(ups) + (u - 3))
                    mm(bank(4 + u % 4), B("w1")[:, (half * 2 + m) * P:(half * 2 + m + 1) * P], chunk(hn, c)).then_inc(up_ready, 1)

                def down_pair(u):
                    pe.wait_ge(gelu_ready, i * len(ups) + (u + 2))
                    for v in (u, u + 1):
                        c, half, m = ups[v]
                        last = mm(ps[half * D:(half + 1) * D, c, :], B("w2")[:, m * D:(m + 1) * D], act_h[:, v % 4, :],
                                  m == 0, m == 1)
                        last.then_inc(down_ready, 1)

                for u in (0, 2, 4, 6):
                    up(u)
                    up(u + 1)
                    if u == 4:
                        down_pair(0)
                        down_pair(2)
                centre(i * 2 + 3, 0)
                down_pair(4)
                down_pair(6)
                mean_square(i * 2 + 3, 0)
                centre(i * 2 + 3, 1)
                mean_square(i * 2 + 3, 1)

            N9 = 1 + 2 * LAYERS
            for g in range(NG):
                pe.wait_ge(f_state_ready, g // 2 + 1)
                mm(bank(4 + g)[:, 0:GC], C("ident"), group(f_state, g)).then_inc(f_turned, 1)

            def slot(s, t, ending=False):
                if runs(s, 3, ending, t):
                    g = (t - 3) % NG
                    pe.wait_ge(f_scaled, s - 2)
                    for k in range(2):
                        j = 2 * g + k
                        last = nc.tensor.transpose(bank(4 + g)[:, k * P:(k + 1) * P], f_tok[:, j * P:(j + 1) * P], C("ident"))
                    last.then_inc(f_turned, 1)
                if not ending:
                    pe.wait_ge(f_gate_ready, s + 1)
                    for k in range(2):
                        j = 2 * t + k
                        last = mm(bank(t)[:, k * 2 * P:(k + 1) * 2 * P], f_gate[:, j * P:(j + 1) * P], f_w[:, :])
                    last.then_inc(f_products, 1)

            for t in range(NG):
                slot(t, t)
            with pe.Fori(1, ITERS) as i:
                for t in range(NG):
                    slot(i * NG + t, t)
            for t in range(3):
                slot(ITERS * NG + t, t, True)

            ln(N9 + 1)
            pe.wait_ge(late_weights_in, 16)
            for c in range(NCH):
                pe.wait_ge(hn_ready, 2 * LAYERS * NCH + (c + 1))
                mm(bank(c), W("dec_q"), chunk(hn, c)).then_inc(d_qk_ps, 1)
                for j in range(4 * c, 4 * c + 4):
                    last = mm(ps[:, 4 + j // 2, (j % 2) * 2 * P:(j % 2 + 1) * 2 * P], hn[:, j * P:(j + 1) * P], W("dec_kv"))
                    if j % 2 == 1:
                        last.then_inc(d_kv_ps, 1)
            for c in range(NCH):
                mm(bank(2 + c), W("dec_k"), chunk(hn, c)).then_inc(d_qk_ps, 1)
            pe.wait_ge(d_kv_ready, 4)
            for n in range(NT):
                mm(ps[0:D, 4 + n // 8, (n % 8) * D:(n % 8 + 1) * D], kd_tok[:, n, :], dv_tok[:, n, :])
                last = mm(ps[D:P, 4 + n // 8, (n % 8) * D:(n % 8 + 1) * D], kd_tok[:, n, :], dv_tok[:, n, :])
            last.then_inc(d_upd_ps, 1)
            score_units = [(j, g, half) for j in range(NB) for g in range(2) for half in range(HALVES)]

            def score(u):
                j, g, half = score_units[u]
                quarter = j // 2
                if u % 8 == 0:
                    pe.wait_ge(d_heads_ready, (quarter + 1) * HALVES * HEADS)
                if u >= 4:
                    pe.wait_ge(d_scored, u - 3)
                rhs = q_heads[:, quarter % 2, half, 4 * g:4 * g + 4, (j % 2) * P:(j % 2 + 1) * P]
                mm(bank(u % 4), dk[:, j * P:(j + 1) * P], rhs).then_inc(d_scores, 1)

            def spend_pair(u):
                j, g, _ = score_units[u]
                o = [ps[half * D:(half + 1) * D, 6 + j // 4, (j % 4) * P:(j % 4 + 1) * P] for half in range(HALVES)]
                pe.wait_ge(d_scored, u + 2)
                for h in range(4):
                    for half in range(HALVES):
                        last = mm(o[half], v_heads[:, 2 * j + half, (4 * g + h) * D:(4 * g + h + 1) * D],
                                  scored[:, (u + half) % 4, h * P:(h + 1) * P], g == 0 and h == 0, False)
                        if h == 3:
                            last.then_inc(d_block_out, 1)
                if g == 1:
                    if j == 0:
                        pe.wait_ge(d_state_ready, 2)
                    for half in range(HALVES):
                        mm(o[half], state_rows[:, 2 * j + half, :], dqd[:, j * P:(j + 1) * P], False, True).then_inc(d_stated, 1)

            pe.wait_ge(d_k_ready, NCH)
            score(0)
            score(1)
            for u in range(0, len(score_units), 2):
                if u + 2 < len(score_units):
                    score(u + 2)
                    score(u + 3)
                if u == 0:
                    pe.wait_ge(v_heads_ready, 2)
                spend_pair(u)
            for c in range(NCH):
                pe.wait_ge(d_out_sb, c + 1)
                mm(bank(c), W("dec_proj"), chunk(d_out, c)).then_inc(d_proj, 1)

            ln(N9 + 2)
            ln(N9 + 3)
            pe.wait_ge(hn_ready, (2 * LAYERS + 2) * NCH)
            for j in range(NB):
                last = mm(bank(4)[:, j * 2 * E:(j + 1) * 2 * E], xn[:, j * P:(j + 1) * P], W("moe_wr"))
            last.then_inc(logits_ps, 1)
            units = [(e, c, half) for e in range(E) for c in range(NCH) for half in range(HALVES)]

            def up(u):
                e, c, half = units[u]
                if u >= 4:
                    pe.wait_ge(m_gelu, u - 3)
                mm(bank(u % 4), W("moe_w1")[:, (half * E + e) * P:(half * E + e + 1) * P], chunk(xn, c)).then_inc(m_up, 1)

            up(0)
            up(1)
            up(2)
            pe.wait_ge(share_ready, 1)
            for j in range(NB):
                last = nc.tensor.transpose(ps[:, 5, :].bitcast(BF16)[0:3 * 2 * E, j * P:(j + 1) * P],
                                           share_parts[:, j, :, :].rearrange("p k e -> p (k e)"), ident_b[:, :])
            last.then_inc(share_turned, 1)
            pe.wait_ge(share_T_ready, 2)
            for u in range(len(units)):
                e, c, half = units[u]
                v = u // 2
                if half == 0:
                    if v >= 2:
                        pe.wait_ge(share_w_ready, v - 1)
                    mm(bank(6 + v % 2), pick_b[:, e * P:(e + 1) * P], chunk(share_T, c)).then_inc(share_w_ps, 1)
                    if v >= 2:
                        pe.wait_ge(m_added, v - 1)
                if u + 3 < len(units):
                    up(u + 3)
                pe.wait_ge(m_gelu, u + 1)
                last = mm(ps[half * D:(half + 1) * D, 4 + v % 2, :], W("moe_w2")[:, e * D:(e + 1) * D], act_h[:, u % 4, :])
                if half == 1:
                    last.then_inc(m_down, 1)
            for c in range(NCH):
                pe.wait_ge(m_added, (E - 1) * NCH + c + 1)
                for j in range(4 * c, 4 * c + 4):
                    last = nc.tensor.transpose(ps[:, c, (j % 4) * P:(j % 4 + 1) * P], hres[:, j * P:(j + 1) * P], C("ident"))
                last.then_inc(final_turned, 1)

        @block.scalar
        def _(act):
            order = Order(act, act_order)
            A_ = nc.scalar.activation
            log_exp = "natural_log_exp_and_others"
            nc.scalar.preload_act_table_set(log_exp)
            act.dma_start(ct[:, :], consts).then_inc(consts_in, 16)
            act.wait_ge(weights_in, 16)
            act.wait_ge(row_stats, 4)
            order.did(A_(tab_rstd[:, :], mv[:, :, 1], ACT.Ln, bias=eps_col[:, 0:1]))
            order.wait()
            A_(tab_rstd[:, :], tab_rstd[:, :], ACT.Exp, scale=-0.5).then_inc(act_prep, 1)
            act.wait_ge(pe_prep, 3)
            act.wait_ge(vec_prep, 4)
            A_(ids_T[0:HALVES * SLOTS, :], ps[:, 3, :].bitcast(BF16)[0:HALVES * SLOTS, :], ACT.Copy).then_inc(act_prep, 1)

            def widen(g):
                n, half = GROUPS[g]
                level, k, c = UNITS[n]
                act.wait_ge(ids_wide_ps, g + 1)
                if g >= 2:
                    act.wait_ge(onehot_ready, g - 1)
                w = 3 if level == 1 else 1
                A_(ids_wide[:, g % 2, 0:w, :], ps[:, 0:w, :], ACT.Copy).then_inc(ids_wide_sb, 1)

            def root_mean(n):
                act.wait_ge(rows_summed, HALVES * (n + 1))
                if n >= 2:
                    act.wait_ge(tree_var, n - 1)
                sq = squares[:, (n % 2) * CH:(n % 2 + 1) * CH]
                A_(sq, bank(3 + n % 2), ACT.Square, bias=tree_bias[:, 0:1]).then_inc(tree_sq, 1)

            def root_rest(n):
                lg = logs[:, (n % 2) * CH:(n % 2 + 1) * CH]
                act.wait_ge(tree_var, n + 1)
                order.did(A_(lg, bank(5 + n % 2), ACT.Ln, bias=eps_col[:, 0:1]))
                if n >= 2:
                    act.wait_ge(tree_node, n - 1)
                order.wait()
                A_(rstd[:, (n % 2) * CH:(n % 2 + 1) * CH], lg, ACT.Exp, scale=-0.5).then_inc(tree_rstd, 1)

            decays = [(decay[:, h, :], C("diff"), heads_neg[:, h:h + 1]) for h in range(HEADS)] \
                + [(q_decay[:, :], C("pos_row"), slope_neg[:, 0:1]), (k_decay[:, :], row_neg[:, :], C("pos_left")),
                   (block_decay[:, :], slope_neg[:, :], float(P))]
            for g in range(HALVES):
                widen(g)
            for n in range(len(UNITS)):
                if n + 1 < len(UNITS):
                    widen(2 * n + 2)
                if n >= 1:
                    root_rest(n - 1)
                if n + 1 < len(UNITS):
                    widen(2 * n + 3)
                root_mean(n)
                if n == 5:
                    act.wait_ge(slopes_ready, 3)
                for dst, src, scale in decays[2 * (n - 5):2 * (n - 4)] if n >= 5 else []:
                    A_(dst, src, ACT.Exp, scale=scale).then_inc(act_prep, 1)
            root_rest(len(UNITS) - 1)

            def ln_square(n, c):
                act.wait_ge(ln_centered, n * NCH + (c + 1))
                A_(chunk(squares, c), bank(c), ACT.Square).then_inc(ln_squared, 1)

            def ln_root(n, c):
                act.wait_ge(ln_var, n * NCH + (c + 1))
                order.did(A_(chunk(logs, c), bank(2 + c), ACT.Ln, bias=eps_col[:, 0:1]))
                order.wait()
                A_(chunk(rstd, c), chunk(logs, c), ACT.Exp, scale=-0.5).then_inc(ln_rstd, 1)

            def ln(n):
                for c in range(NCH):
                    ln_square(n, c)
                for c in range(NCH):
                    ln_root(n, c)

            ln(0)
            ln(1)
            with act.Fori(0, LAYERS) as i:
                order.enter(i, 2 * NCH)
                act.wait_ge(k_negmax, i + 1)
                for c in range(NCH):
                    A_(chunk(k_exp, c), bank(c), ACT.Exp, bias=k_neg[:, 0:1],
                       accum_out=k_sums[:, c:c + 1]).then_inc(k_exped, 1)
                for c in range(NCH):
                    for b in range(2 * c, 2 * c + 2):
                        act.wait_ge(q_shifted, i * 4 + (b + 1))
                        A_(v_tok[:, 4 * b:4 * b + 4, :], bank(4 + b).rearrange("p (n w) -> p n w", n=4)[:, :, D:2 * D],
                           ACT.Copy).then_inc(v_tok_ready, 1)
                    A_(q_e[:, 8 * c:8 * c + 8, :], q_sh[:, 8 * c:8 * c + 8, :], ACT.Exp).then_inc(q_exped, 1)
                for c in range(NCH):
                    act.wait_ge(k_turned, i * NCH + (c + 1))
                    A_(k_tok[:, 4 * c:4 * c + 4, :], bank(2 + c).rearrange("p (j w) -> p j w", j=4),
                       ACT.Copy).then_inc(k_tok_ready, 1)
                for c in range(NCH):
                    act.wait_ge(q_turned, i * NCH + (c + 1))
                    A_(chunk(q_T, c), bank(4 + c), ACT.Copy).then_inc(q_T_ready, 1)
                ln(i * 2 + 2)
                act.wait_ge(layer_b_in, i * 16 + 16)
                for u in range(8):
                    act.wait_ge(up_ready, i * 8 + (u + 1))
                    if u == 4:
                        act.wait_ge(down_ready, i * 8 + 4)
                    m = u // 2 % 2
                    A_(act_h[:, u % 4, :], bank(4 + u % 4), ACT.Gelu, bias=B("bf1")[:, m:m + 1]).then_inc(gelu_ready, 1)
                nc.scalar.preload_act_table_set(log_exp)
                for c in range(NCH):
                    ln_square(i * 2 + 3, c)
                    ln_root(i * 2 + 3, c)
            order.leave(LAYERS)
            nc.scalar.preload_act_table(ACT.Sigmoid)

            def slot(s, t, ending=False):
                if not ending:
                    act.wait_ge(f_turned, s + 1)
                    A_(group(f_tanh, t), bank(4 + t)[:, 0:GC], ACT.Tanh, bias=f_c[:, 0:1], scale=1.0 / NORM_GAIN).then_inc(f_tanh_ready, 1)
                    act.wait_ge(f_mid_ready, s + 1)
                    A_(group(f_sig, t), group(f_mid, t), ACT.Sigmoid, scale=1.0 / NORM_GAIN).then_inc(f_sig_ready, 1)
                if runs(s, 1, ending, t):
                    g = (t - 1) % NG
                    act.wait_ge(f_products, s)
                    A_(f_squares[:, 4 * g:4 * g + 4, 0:D].rearrange("p (j h) d -> p j h d", h=HALVES),
                       bank(g).rearrange("p (j w) -> p j w", w=2 * P)[:, :, P:2 * P].rearrange("p j (h d) -> p j h d", h=HALVES),
                       ACT.Square).then_inc(f_squared, 1)

            for t in range(NG):
                slot(t, t)
            with act.Fori(1, ITERS) as i:
                for t in range(NG):
                    slot(i * NG + t, t)
            for t in range(3):
                slot(ITERS * NG + t, t, True)

            nc.scalar.preload_act_table_set(log_exp)
            ln(2 + 2 * LAYERS)
            for c in range(NCH):
                act.wait_ge(d_qk_ps, c + 1)
                A_(chunk(dq, c), bank(c), ACT.Copy, scale=DH ** -0.5).then_inc(d_q_ready, 1)
            for c in range(NCH):
                act.wait_ge(d_qk_ps, NCH + c + 1)
                A_(chunk(dk, c), bank(2 + c), ACT.Copy).then_inc(d_k_ready, 1)
            act.wait_ge(d_q_ready, NCH)
            for quarter in range(NB // 2):
                if quarter >= 2:
                    act.wait_ge(d_scores, (quarter - 1) * 8)
                for half in range(HALVES):
                    for h in range(HEADS):
                        m = half * HEADS + h
                        A_(q_heads[:, quarter % 2, half, h, :], dq[:, quarter * 2 * P:(quarter + 1) * 2 * P], ACT.Copy,
                           scale=C("head_mask")[:, m:m + 1]).then_inc(d_heads_ready, 1)
            for c in range(NCH):
                act.wait_ge(d_stated, (c + 1) * NB)
                A_(chunk(d_out, c), bank(6 + c), ACT.Copy).then_inc(d_out_sb, 1)

            ln(3 + 2 * LAYERS)
            ln(4 + 2 * LAYERS)
            act.wait_ge(gap_ready, 1)
            A_(gap_e[:, :], gap[:, :], ACT.Exp).then_inc(gap_exped, 1)
            for u in range(E * NCH * HALVES):
                e, v = u // (NCH * HALVES), u // HALVES
                act.wait_ge(m_up, u + 1)
                if u >= 4 and u % 2 == 0:
                    act.wait_ge(m_down, v - 1)
                A_(act_h[:, u % 4, :], bank(u % 4), ACT.Gelu, bias=W("moe_b1")[:, e:e + 1]).then_inc(m_gelu, 1)
                if u % 2 == 1:
                    act.wait_ge(share_w_ps, v + 1)
                    if v >= 2:
                        act.wait_ge(m_added, v - 1)
                    A_(share_w[:, v % 2, :], bank(6 + v % 2), ACT.Copy).then_inc(share_w_ready, 1)
            for c in range(NCH):
                act.wait_ge(final_turned, c + 1)
                A_(out_tok[:, 4 * c:4 * c + 4, :], bank(c).rearrange("p (j w) -> p j w", j=4), ACT.Copy).then_inc(final_tok, 1)

        @block.vector
        def _(dve):
            order = Order(dve, vec_order)
            V = nc.vector

            def TT(o, a, b, op):
                return V.tensor_tensor(o, a, b, op)

            def TS(o, a, s1, s2, op0, op1):
                return V.tensor_scalar(o, a, s1, s2, op0, op1)

            def STT(o, a, s, b, op0, op1):
                return V.scalar_tensor_tensor(out=o, in0=a, scalar=s, in1=b, op0=op0, op1=op1)

            order.did(V.memset(eps_col[:, :], EPS))
            dve.wait_ge(weights_in, 16)
            comp = W("comp").rearrange("p (k d) -> p k d", k=2)
            for k in range(2):
                V.bn_stats(stats[:, k, :], comp[:, k, :]).then_inc(row_stats, 1)
            dve.wait_ge(row_stats, 2)
            for k in range(2):
                V.bn_aggr(mv[:, k, :], stats[:, k, :]).then_inc(row_stats, 1)
            dve.wait_ge(act_prep, 1)
            for k in range(2):
                order.did(TS(comp_n[:, k, :], comp[:, k, :], mv[:, k, 0:1], tab_rstd[:, k:k + 1], ALU.subtract, ALU.mult))
            order.wait()
            for k in range(2):
                order.did(TT(comp_n[:, k, :], comp_n[:, k, :], W("tok_gamma_row"), ALU.mult))
            order.wait()
            last = TT(comp_n[:, 0, :], comp_n[:, 0, :], W("tok_beta_row"), ALU.add)
            order.did(last)
            TT(comp_n[:, 1, :], comp_n[:, 1, :], W("tok_beta_row"), ALU.add).then_inc(vec_prep, 1)
            order.wait()
            dve.wait_ge(consts_in, 16)
            order.did(V.tensor_copy(ident_b[:, :], C("ident")))
            order.did(V.memset(ids_T[:, :], 0.0))
            dve.wait_ge(ids_in, 16 * NT)
            order.did(V.tensor_copy(ids_b[:, :, :], ids[:, :, :]))
            order.wait()
            TS(ids_b[:, :, KEEP_SLOT], idx[:, :], 1.0, None, ALU.is_gt, ALU.bypass).then_inc(vec_prep, 1)
            dve.wait_ge(pe_prep, 2)
            order.did(V.tensor_copy(tree_w[:, :, :], bank(0)[:, 0:3 * P].rearrange("p (k n) -> p k n", k=3)))
            order.did(V.tensor_copy(tree_bias[:, :], bank(1)[:, 0:1]))
            order.did(V.tensor_copy(comp_T[:, :], bank(2)[0:D, 0:2 * P]))
            V.tensor_copy(op_T[:, :], bank(2)[0:D, 2 * P:2 * P + D]).then_inc(vec_prep, 1)
            order.did(V.tensor_copy(keep_b[:, 0:D], ident_b[:, KEEP_SLOT:KEEP_SLOT + 1].broadcast_to([P, D])))
            V.tensor_copy(keep_b[:, D:P], ident_b[:, SLOTS + KEEP_SLOT:SLOTS + KEEP_SLOT + 1].broadcast_to([P, D])).then_inc(vec_prep, 1)
            dve.wait_ge(pe_prep, 4)
            leaf = bank(4)[:, 0:2 * P].rearrange("p (k n) -> p k n", k=2)
            opp = bank(5)[:, 0:D]
            order.did(V.tensor_copy(leaf_hi[:, :, :], leaf))
            order.did(V.tensor_copy(op_hm[:, :], opp))
            order.wait()
            order.did(TT(leaf_rest[:, :, :], leaf, leaf_hi[:, :, :], ALU.subtract))
            order.did(TT(op_rest[:, :], opp, op_hm[:, :], ALU.subtract))
            order.wait()
            order.did(V.tensor_copy(leaf_mid[:, :, :], leaf_rest[:, :, :]))
            order.did(V.tensor_copy(op_lo[:, :], op_rest[:, :]))
            order.wait()
            order.did(TT(leaf_lo[:, :, :], leaf_rest[:, :, :], leaf_mid[:, :, :], ALU.subtract))
            order.did(V.tensor_copy(op_hm[D:P, :], op_lo[D:P, :]))
            order.wait()
            order.did(TT(op_rest[:, :], op_rest[:, :], op_lo[:, :], ALU.subtract))
            order.wait()
            order.did(V.tensor_copy(op_lo[0:D, :], op_rest[0:D, :]))
            order.did(V.memset(op_lo[D:P, :], 0.0))
            order.wait()
            TS(f_wt[:, :], W("ffn_wT"), W("ffn_ln_w"), None, ALU.mult, ALU.bypass).then_inc(vec_prep, 1)

            def compare(g):
                n, half = GROUPS[g]
                level, k, c = UNITS[n]
                dve.wait_ge(ids_wide_sb, g + 1)
                if g >= HOT_BUFS:
                    dve.wait_ge(rows_summed, HALVES * (g // 2 - 1))
                hot = onehot[:, g % HOT_BUFS, :, :]
                if level == 1:
                    for side in range(2):
                        for v in range(2):
                            TS(hot[:, 2 * side + v, :], ids_wide[:, g % 2, side, :], C("vocab")[:, v:v + 1], None,
                               ALU.is_equal, ALU.bypass)
                TS(hot[:, 4, :], ids_wide[:, g % 2, 2 if level == 1 else 0, :], C("vocab")[:, 2:3], None,
                   ALU.is_equal, ALU.bypass).then_inc(onehot_ready, 1)

            def normal(n):
                level, k, c = UNITS[n]
                dve.wait_ge(tree_rstd, n + 1)
                o = chunk(norm_tmp, n % 2)
                r = chunk(rstd, n % 2)
                order.did(STT(o, bank(3 + n % 2), tree_bias[:, 0:1], r, ALU.add, ALU.mult))
                order.wait()
                dst = node1[k] if level == 1 else node2[k] if level == 2 else hres
                TS(chunk(dst, c), o, W("tok_gamma"), W("tok_beta"), ALU.mult, ALU.add).then_inc(tree_node, 1)

            for g in range(HALVES):
                compare(g)
            for n in range(len(UNITS)):
                if n + 1 < len(UNITS):
                    compare(2 * n + 2)
                if n >= 1:
                    normal(n - 1)
                if n + 1 < len(UNITS):
                    compare(2 * n + 3)
                if n == 4:
                    dve.wait_ge(late_weights_in, 16)
                    TS(slope_neg[:, :], W("slope_col"), -1.0, None, ALU.mult, ALU.bypass).then_inc(slopes_ready, 1)
                    TS(row_neg[:, :], W("slope_row"), -1.0, None, ALU.mult, ALU.bypass).then_inc(slopes_ready, 1)
                    TS(heads_neg[:, :], W("slope_heads"), -1.0, None, ALU.mult, ALU.bypass).then_inc(slopes_ready, 1)
                    V.tensor_copy(pick_b[:, :], C("pick_expert")).then_inc(slopes_ready, 1)
            normal(len(UNITS) - 1)
            dve.wait_ge(tree_node, len(UNITS))
            for c in range(NCH):
                dve.wait_ge(pe_prep, 5 + c)
                order.did(TT(chunk(hres, c), chunk(hres, c), bank(c), ALU.mult))
            order.wait()
            for c in range(NCH):
                V.tensor_copy(chunk(x, c), chunk(hres, c)).then_inc(ln_in, 1)
            dve.wait_ge(pe_prep, 7)
            dve.wait_ge(late_weights_in, 16)
            order.did(V.tensor_copy(f_w[:, P:2 * P], C("center")))
            order.did(TS(f_w[:, 0:P], bank(7)[:, 0:P], NORM_GAIN * D ** 0.5, None, ALU.mult, ALU.bypass))
            order.did(TT(f_c[:, :], bank(7)[:, P:P + 1], W("ffn_b"), ALU.add))
            order.wait()
            TS(f_c_gain[:, :], f_c[:, :], NORM_GAIN, None, ALU.mult, ALU.bypass).then_inc(vec_prep, 1)

            def ln(n, c, dst, inc, gamma=None, beta=None, plus=None, post=None):
                dve.wait_ge(ln_rstd, n * NCH + (c + 1))
                if gamma is None and plus is None:
                    TT(chunk(dst, c), bank(c), chunk(rstd, c), ALU.mult).then_inc(inc, 1)
                    return
                order.did(TT(chunk(norm_tmp, c), bank(c), chunk(rstd, c), ALU.mult))
                order.wait()
                if plus is not None:
                    TT(chunk(dst, c), chunk(norm_tmp, c), chunk(plus, c), ALU.add).then_inc(inc, 1)
                else:
                    TS(chunk(dst, c), chunk(norm_tmp, c), gamma, beta, ALU.mult, ALU.add).then_inc(inc, 1)

            for c in range(NCH):
                ln(0, c, x, ln_in, plus=C("pe"))
            def residual(c, src):
                order.did(TT(chunk(hres, c), chunk(hres, c), src, ALU.add))
                order.wait()
                V.tensor_copy(chunk(x, c), chunk(hres, c)).then_inc(ln_in, 1)

            def layer(i, last=False):
                dve.wait_ge(layer_a_in, i * 16 + 16)
                for c in range(NCH):
                    ln(i * 2 + 1, c, hn, hn_ready, gamma=A("g1"), beta=A("b1"))
                for c in range(NCH):
                    dve.wait_ge(k_ready, i * NCH + (c + 1))
                    order.did(V.tensor_reduce(k_part[:, c:c + 1], bank(c), AX.X, ALU.max))
                order.wait()
                TT(k_own[:, :], k_part[:, 0:1], k_part[:, 1:2], ALU.max).then_inc(k_max, 1)
                for b in range(4):
                    dve.wait_ge(qv_ready, i * 4 + (b + 1))
                    q = bank(4 + b).rearrange("p (n w) -> p n w", n=4)[:, :, 0:D].rearrange("p n (h d) -> p n h d", h=HEADS)
                    order.did(V.tensor_reduce(q_max[:, 4 * b:4 * b + 4, :], q, AX.X, ALU.max))
                    if b == 0:
                        dve.wait_ge(k_swapped, i + 1)
                        dve.wait_ge(k_max, i + 1)
                        TS(k_neg[:, :], bank(2)[:, 0:1], k_own[:, 0:1], -1.0, ALU.max, ALU.mult).then_inc(k_negmax, 1)
                    order.wait()
                    ins = TT(q_sh[:, 4 * b:4 * b + 4, :].rearrange("p n (h d) -> p n h d", h=HEADS), q,
                             q_max[:, 4 * b:4 * b + 4, :].unsqueeze(3).broadcast_to([P, 4, HEADS, DH]), ALU.subtract)
                    ins.then_inc(q_shifted, 1)
                for c in range(NCH):
                    t = slice(8 * c, 8 * c + 8)
                    dve.wait_ge(q_exped, i * NCH + (c + 1))
                    order.did(V.tensor_reduce(q_sum[:, t, :], q_e[:, t, :].rearrange("p n (h d) -> p n h d", h=HEADS), AX.X, ALU.add))
                    order.wait()
                    order.did(V.reciprocal(q_inv[:, t, :], q_sum[:, t, :]))
                    order.wait()
                    TT(q_n[:, t, :].rearrange("p n (h d) -> p n h d", h=HEADS),
                       q_e[:, t, :].rearrange("p n (h d) -> p n h d", h=HEADS),
                       q_inv[:, t, :].unsqueeze(3).broadcast_to([P, 8, HEADS, DH]), ALU.mult).then_inc(q_normed, 1)
                dve.wait_ge(k_exped, i * NCH + NCH)
                TT(k_half[:, :], k_sums[:, 0:1], k_sums[:, 1:2], ALU.add).then_inc(k_summed, 1)
                dve.wait_ge(ctx_ready, i * 2 + 2)
                dve.wait_ge(pool_zeroed, 2)
                TT(ctx_T[:, :], ps[:, 0, 0:D], C("head_block"), ALU.mult).then_inc(ctx_masked, 1)
                dve.wait_ge(k_total, i + 1)
                order.did(V.reciprocal(k_inv[:, :], bank(1)[:, 0:1]))
                order.wait()
                dve.wait_ge(mix_ps, i + 1)
                order.did(TS(mix[0:D, 0:D], ps[0:D, 2, 0:D], k_inv[0:D, 0:1], DH ** -0.5, ALU.mult, ALU.mult))
                order.wait()
                TS(mix[D:P, D:P], ps[D:P, 2, 0:D], k_inv[D:P, 0:1], DH ** -0.5, ALU.mult, ALU.mult).then_inc(mix_ready, 1)
                for c in range(NCH):
                    dve.wait_ge(attn_ready, i * NCH + (c + 1))
                    STT(chunk(x, c), bank(6 + c), A("bo"), chunk(x, c), ALU.add, ALU.add).then_inc(ln_in, 1)
                dve.wait_ge(layer_b_in, i * 16 + 16)
                for c in range(NCH):
                    ln(i * 2 + 2, c, hn, hn_ready, gamma=B("g2"), beta=B("b2"))
                for c in range(NCH):
                    dve.wait_ge(down_ready, i * 8 + (4 * c + 4))
                    dve.wait_ge(ln_in, (i * 2 + 3) * NCH)
                    layer_out = STT(chunk(x, c), bank(c), B("bf2"), chunk(x, c), ALU.add, ALU.add)
                    if last:
                        order.did(layer_out)
                        order.wait()
                        residual(c, chunk(x, c))
                    else:
                        layer_out.then_inc(ln_in, 1)

            with dve.Fori(0, LAYERS - 1) as i:
                order.enter(i, 16)
                layer(i)
            order.leave(LAYERS - 1)
            layer(LAYERS - 1, True)
            N9 = 1 + 2 * LAYERS


            dve.wait_ge(pool_order, 2)
            for c in range(NCH):
                dve.wait_ge(ln_rstd, N9 * NCH + (c + 1))
                order.did(TT(chunk(norm_tmp, c), bank(c), chunk(rstd, c), ALU.mult))
                order.wait()
                TS(chunk(f_state, c), chunk(norm_tmp, c), NORM_GAIN, f_c_gain[:, 0:1], ALU.mult, ALU.subtract).then_inc(f_state_ready, 1)

            def slot(s, t, ending=False):
                if not ending:
                    dve.wait_ge(f_tanh_ready, s + 1)
                    STT(group(f_mid, t), bank(4 + t)[:, 0:GC], f_c_gain[:, 0:1], group(f_tanh, t), ALU.add, ALU.add).then_inc(f_mid_ready, 1)
                if runs(s, 3, ending, t):
                    g = (t - 3) % NG
                    dve.wait_ge(f_rstd, s - 2)
                    TT(group(f_tok, g).rearrange("p (j h d) -> p j h d", j=2, h=HALVES),
                       bank(g).rearrange("p (j w) -> p j w", w=2 * P)[:, :, 0:P].rearrange("p j (h d) -> p j h d", h=HALVES),
                       f_rstd_sb[:, g, :].rearrange("p (j h) -> p j h", j=2).unsqueeze(3).broadcast_to([P, 2, HALVES, D]), ALU.mult).then_inc(f_scaled, 1)
                if not ending:
                    dve.wait_ge(f_sig_ready, s + 1)
                    TT(group(f_gate, t), group(f_mid, t), group(f_sig, t), ALU.mult).then_inc(f_gate_ready, 1)
                if runs(s, 1, ending, t):
                    g = (t - 1) % NG
                    dve.wait_ge(f_squared, s)
                    V.tensor_reduce(f_sumsq[:, g, :], f_squares[:, 4 * g:4 * g + 4, :], AX.X, ALU.add).then_inc(f_summed, 1)

            for t in range(NG):
                slot(t, t)
            with dve.Fori(1, ITERS) as i:
                for t in range(NG):
                    slot(i * NG + t, t)
            for t in range(3):
                slot(ITERS * NG + t, t, True)
            for c in range(NCH):
                dve.wait_ge(f_turned, ITERS * NG + 2 * c + 2)
                for g in (2 * c, 2 * c + 1):
                    order.did(TS(group(norm_tmp, g), bank(4 + g)[:, 0:GC], 1.0 / NORM_GAIN, f_c[:, 0:1], ALU.mult, ALU.add))
                order.wait()
                residual(c, chunk(norm_tmp, c))

            for c in range(NCH):
                ln(N9 + 1, c, hn, hn_ready)
            dve.wait_ge(act_prep, 13)
            for b in range(4):
                dve.wait_ge(d_kv_ps, b + 1)
                kv = bank(4 + b).rearrange("p (n w) -> p n w", n=4)
                order.did(TT(kd_tok[:, 4 * b:4 * b + 4, :], kv[:, :, 0:D],
                             k_decay[:, :].unsqueeze(1).broadcast_to([P, 4, D]), ALU.mult))
                V.tensor_copy(dv_tok[:, 4 * b:4 * b + 4, :], kv[:, :, D:2 * D]).then_inc(d_kv_ready, 1)
            dve.wait_ge(pool_zeroed, 3)
            dve.wait_ge(d_kv_ready, 4)
            for part in range(2):
                t = slice(part * NB, part * NB + NB)
                V.tensor_copy(v_heads[:, t, :].rearrange("p n (h w) -> p n h w", h=HEADS)[:, :, :, 0:DH],
                              dv_tok[:, t, :].rearrange("p n (h d) -> p n h d", h=HEADS)).then_inc(v_heads_ready, 1)
            dve.wait_ge(d_q_ready, NCH)
            order.did(TT(dqd[:, :].rearrange("p (j t) -> p j t", j=NB), dq[:, :].rearrange("p (j t) -> p j t", j=NB),
                         q_decay[:, :].unsqueeze(1).broadcast_to([P, NB, P]), ALU.mult))
            dve.wait_ge(d_upd_ps, 1)
            order.did(TT(updates[:, :, :], ps[:, 4:6, :].rearrange("p b (n d) -> p (b n) d", d=D),
                         C("head_block").unsqueeze(1).broadcast_to([P, NT, D]), ALU.mult))
            order.did(V.memset(state[:, 0, :], 0.0))
            order.wait()
            tiles = [2 * j + half for half in range(HALVES) for j in range(NB)]
            for s in range(1, NT):
                order.did(STT(state[:, s, :], state[:, s - 1, :], block_decay[:, 0:1], updates[:, tiles[s - 1], :],
                              ALU.mult, ALU.add))
                order.wait()
            for half in range(HALVES):
                rows = slice(half * D, (half + 1) * D)
                V.tensor_copy(state_rows[rows, :, :].rearrange("p (j h) d -> p j h d", h=HALVES)[:, :, half, :],
                              state[rows, half * NB:(half + 1) * NB, :]).then_inc(d_state_ready, 1)
            dve.wait_ge(decay_masked, HEADS)
            for u in range(2 * NT):
                g = u // 2 % 2
                dve.wait_ge(d_scores, u + 1)
                if u >= 4:
                    dve.wait_ge(d_block_out, u - 3)
                TT(scored[:, u % 4, :], bank(u % 4), decay[:, 4 * g:4 * g + 4, :].rearrange("p h t -> p (h t)"),
                   ALU.mult).then_inc(d_scored, 1)
            for c in range(NCH):
                dve.wait_ge(d_proj, c + 1)
                order.did(TS(chunk(norm_tmp, c), bank(c), W("dec_b"), None, ALU.add, ALU.bypass))
                order.wait()
                residual(c, chunk(norm_tmp, c))

            for c in range(NCH):
                ln(N9 + 2, c, x, ln_in)
            for c in range(NCH):
                ln(N9 + 3, c, xn, hn_ready, gamma=W("moe_gamma"), beta=W("moe_beta"))
            dve.wait_ge(logits_ps, 1)
            order.did(TT(logits[:, :, :], bank(4)[:, 0:NT * E].rearrange("p (n e) -> p n e", e=E),
                         W("moe_br")[:, 0:E].unsqueeze(1).broadcast_to([P, NT, E]), ALU.add))
            order.wait()
            for n in range(NT):
                order.did(V.max(top[:, n, :], logits[:, n, :]))
            order.wait()
            for n in range(NT):
                order.did(V.max_index(top_i[:, n, :], top[:, n, :], logits[:, n, :]))
            TT(gap[:, :], top[:, :, 1], top[:, :, 0], ALU.subtract).then_inc(gap_ready, 1)
            order.wait()
            order.did(V.tensor_copy(top_f[:, :, :], top_i[:, :, 0:2]))
            order.wait()
            iota = C("iota_e").unsqueeze(1).broadcast_to([P, NT, E])
            order.did(TT(pick_1[:, :, :], iota, top_f[:, :, 0:1].broadcast_to([P, NT, E]), ALU.is_equal))
            order.did(TT(pick_2[:, :, :], iota, top_f[:, :, 1:2].broadcast_to([P, NT, E]), ALU.is_equal))
            dve.wait_ge(gap_exped, 1)
            order.did(TS(den[:, :], gap_e[:, :], 1.0, None, ALU.add, ALU.bypass))
            order.wait()
            order.did(V.reciprocal(w_1[:, :], den[:, :]))
            order.wait()
            order.did(TT(w_2[:, :], gap_e[:, :], w_1[:, :], ALU.mult))
            order.did(TT(share_1[:, :, :], pick_1[:, :, :], w_1[:, :].unsqueeze(2).broadcast_to([P, NT, E]), ALU.mult))
            order.wait()
            order.did(TT(share_2[:, :, :], pick_2[:, :, :], w_2[:, :].unsqueeze(2).broadcast_to([P, NT, E]), ALU.mult))
            order.wait()
            order.did(TT(share[:, :, :], share_1[:, :, :], share_2[:, :, :], ALU.add))
            order.wait()
            whole = share[:, :, :].rearrange("p (j h) e -> p j (h e)", h=HALVES)
            rest = share_rest[:, :, :]
            order.did(V.tensor_copy(share_parts[:, :, 0, :], whole))
            order.wait()
            order.did(TT(rest, whole, share_parts[:, :, 0, :], ALU.subtract))
            order.wait()
            order.did(V.tensor_copy(share_parts[:, :, 1, :], rest))
            order.wait()
            TT(share_parts[:, :, 2, :], rest, share_parts[:, :, 1, :], ALU.subtract).then_inc(share_ready, 1)
            V.memset(share_T[:, :], 0.0).then_inc(share_T_ready, 1)
            dve.wait_ge(share_turned, 1)
            dve.wait_ge(share_T_ready, 1)
            V.tensor_copy(share_T[0:3 * 2 * E, :], ps[:, 5, :].bitcast(BF16)[0:3 * 2 * E, :]).then_inc(share_T_ready, 1)
            for v in range(E * NCH):
                e, c = v // 2, v % 2
                dve.wait_ge(m_down, v + 1)
                dve.wait_ge(share_w_ready, v + 1)
                order.did(STT(y_part[:, v % 2, :], bank(4 + v % 2), W("moe_b2")[:, e:e + 1], share_w[:, v % 2, :], ALU.add, ALU.mult))
                order.wait()
                if v >= 2:
                    dve.wait_ge(m_added, v - 1)
                TT(chunk(hres, c), chunk(hres, c), y_part[:, v % 2, :], ALU.add).then_inc(m_added, 1)


def pack(table, columns, n):
    at, width = offsets(table)
    out = np.zeros(n + (P, width), np.float32)
    for name, (a, w) in at.items():
        v = np.asarray(columns[name])
        out[..., a:a + w] = v
    return out


def twice(v):
    return np.concatenate([v, v]).reshape(P, 1)


def diagonal(*blocks):
    a, b = blocks
    out = np.zeros(a.shape[:-2] + (P, a.shape[-1] + b.shape[-1]), np.float32)
    out[..., :D, :a.shape[-1]] = a
    out[..., D:, a.shape[-1]:] = b
    return out


def make_consts():
    c = {}
    eye = np.eye(P, dtype=np.float32)
    same = np.kron(np.eye(HALVES), np.ones((D, D)))
    p = np.arange(P)
    c["center"] = eye - same / D
    c["mean"] = same / D
    c["ident"] = eye
    c["swap"] = eye[(p + D) % P]
    c["both"] = eye + c["swap"]
    pos = np.arange(S, dtype=np.float32)[:, None]
    div = np.exp(np.arange(0, D, 2, dtype=np.float32) * np.float32(-np.log(10000.0) / D)).astype(np.float32)
    table = np.zeros((S, D), np.float32)
    table[:, 0::2] = np.sin((pos * div).astype(np.float32))
    table[:, 1::2] = np.cos((pos * div).astype(np.float32))
    c["pe"] = table.reshape(HALVES, COLS, D).transpose(0, 2, 1).reshape(P, COLS)
    f = p % D
    c["head_block"] = (f[:, None] // DH == np.arange(D)[None, :] // DH)
    c["head_mask"] = (p[:, None] // DH == np.arange(HALVES * HEADS)[None, :])
    c["diff"] = np.maximum(p[None, :] - p[:, None], 0)
    c["causal"] = p[None, :] >= p[:, None]
    c["pos_row"] = np.broadcast_to(p[None, :], (P, P))
    c["pos_left"] = (P - p)[:, None]
    c["vocab"] = np.stack([p, p + P, f], 1)
    c["pick_expert"] = np.concatenate([(p[:, None] % E == e) & (p[:, None] // E % HALVES == p[None, :] // D)
                                       & (p[:, None] < 3 * HALVES * E) for e in range(E)], 1)
    c["iota_e"] = np.broadcast_to(np.arange(E)[None, :], (P, E))
    return pack(CONSTS, c, ())


def kernel(**inputs):
    import concourse.bacc as bacc
    from concourse.bass_utils import run_bass_kernel_spmd

    a = {k: np.asarray(v) for k, v in inputs.items()}
    tok = {k[7:]: v for k, v in a.items() if k.startswith("L0_tok_")}
    att = {k[8:]: v for k, v in a.items() if k.startswith("L0_attn_")}
    ffn = {k[7:]: v for k, v in a.items() if k.startswith("L0_ffn_")}
    dec = {k[8:]: v for k, v in a.items() if k.startswith("L1_attn_")}
    moe = {k[7:]: v for k, v in a.items() if k.startswith("L1_ffn_")}

    w = {}
    w["comp"] = tok["comp_emb"].reshape(2, P, D).transpose(1, 0, 2).reshape(P, 2 * D)
    w["op"] = np.concatenate([tok["op_emb"], np.zeros((D, D), np.float32)])
    w["tok_gamma_row"] = np.broadcast_to(tok["gamma"], (P, D))
    w["tok_beta_row"] = np.broadcast_to(tok["beta"], (P, D))
    for k, name in enumerate(("wo_T", "wl_T", "wr_T")):
        t = tok["W_bin"][k * D:(k + 1) * D].T
        w[name] = diagonal(t, t)
    w["tok_b"], w["tok_gamma"], w["tok_beta"] = twice(tok["b_bin"]), twice(tok["gamma"]), twice(tok["beta"])
    w["ffn_wT"] = diagonal(ffn["W"].T, ffn["W"].T)
    w["ffn_ln_w"], w["ffn_ln_b"], w["ffn_b"] = twice(ffn["ln_w"]), twice(ffn["ln_b"]), twice(ffn["b"])
    wq, wk, wv = (dec["w_qkv"][:, k * D:(k + 1) * D] for k in range(3))
    w["dec_q"], w["dec_k"] = diagonal(wq, wq), diagonal(wk, wk)
    kv = np.concatenate([wk, wv], 1)
    w["dec_kv"] = diagonal(kv, kv)
    w["dec_proj"] = diagonal(dec["w_proj"], dec["w_proj"])
    w["dec_b"] = twice(dec["b_proj"])
    w["slope_col"] = twice(np.repeat(dec["slopes"], DH))
    w["slope_row"] = np.broadcast_to(np.repeat(dec["slopes"], DH), (P, D))
    w["slope_heads"] = np.broadcast_to(dec["slopes"], (P, HEADS))
    w["moe_gamma"], w["moe_beta"] = twice(moe["gamma"]), twice(moe["beta"])
    w["moe_wr"] = diagonal(moe["Wr"], moe["Wr"])
    w["moe_br"] = np.broadcast_to(np.concatenate([moe["br"], moe["br"]]), (P, 2 * E))
    w["moe_b1"] = moe["b1"].T
    w["moe_b2"] = np.concatenate([moe["b2"].T, moe["b2"].T])
    w["moe_w2"] = moe["W2"].transpose(1, 0, 2).reshape(HID, E * D)
    up = np.zeros((P, HALVES, E, HID), np.float32)
    for half in range(HALVES):
        up[half * D:(half + 1) * D, half] = moe["W1"].transpose(1, 0, 2)
    w["moe_w1"] = up.reshape(P, HALVES * E * HID)

    def column(v):
        return np.concatenate([v, v], 1)[:, :, None]

    la = {"wk": diagonal(att["Wk"], att["Wk"]), "wo": np.concatenate([att["Wo"], att["Wo"]], 1),
          "g1": column(att["g1"]), "b1": column(att["b1"]), "bo": column(att["bo"])}
    qv = np.concatenate([att["Wq"], att["Wv"]], 2)
    la["wqv"] = diagonal(qv, qv)
    lb = {"w1": diagonal(att["W1"], att["W1"]), "w2": att["W2"].reshape(LAYERS, 2, P, D).transpose(0, 2, 1, 3).reshape(LAYERS, P, 2 * D),
          "bf1": att["bf1"].reshape(LAYERS, 2, P).transpose(0, 2, 1), "bf2": column(att["bf2"]),
          "g2": column(att["g2"]), "b2": column(att["b2"])}

    table = np.zeros((tok["leaf_ids"].shape[0], SLOTS), np.int32)
    table[:, :LEAVES] = tok["leaf_ids"]
    table[:, LEAVES:2 * LEAVES - 1] = tok["op_ids"]
    arrays = {
        "token_idx": np.ascontiguousarray(a["x"].reshape(HALVES, NB, P).transpose(2, 1, 0).reshape(P, NT)),
        "id_table": table,
        "weights": pack(WEIGHTS, w, ()),
        "consts": make_consts(),
        "layer_a": pack(LAYER_A, la, (LAYERS,)),
        "layer_b": pack(LAYER_B, lb, (LAYERS,)),
    }
    nc = bacc.Bacc("TRN2", target_bir_lowering=False, num_devices=1)
    args = [nc.dram_tensor(name, v.shape, mybir.dt.from_np(v.dtype), kind="ExternalInput").ap() for name, v in arrays.items()]
    out = nc.dram_tensor("out", (1, S, D), F32, kind="ExternalOutput").ap()
    build(nc, *args, out)
    r = run_bass_kernel_spmd(nc, [arrays], core_ids=[0])
    return r.results[0]["out"]
```

```python
from contextlib import ExitStack

import concourse.bass as bass
from concourse import mybir
import numpy as np

P = 128
D = 64
S = 2048
HALVES = 2
COLS = S // HALVES
CH = 512
NCH = COLS // CH
NB = COLS // P
NG = 4
GC = COLS // NG
NT = S // P
HEADS = 8
DH = D // HEADS
LAYERS = 4
FF = 256
ITERS = 30
E = 8
HID = 128
LEAVES = 8
SLOTS = 16
EPS = 1e-5
NORM_GAIN = 100.0
HOT_BUFS = 4

F32 = mybir.dt.float32
BF16 = mybir.dt.bfloat16
I32 = mybir.dt.int32
U32 = mybir.dt.uint32
ALU = mybir.AluOpType
ACT = mybir.ActivationFunctionType
AX = mybir.AxisListType

WEIGHTS = [
    ("comp", 2 * D), ("op", D), ("tok_gamma_row", D), ("tok_beta_row", D),
    ("wo_T", P), ("wl_T", P), ("wr_T", P), ("tok_b", 1), ("tok_gamma", 1), ("tok_beta", 1),
    ("ffn_wT", P), ("ffn_ln_w", 1), ("ffn_ln_b", 1), ("ffn_b", 1),
    ("dec_q", P), ("dec_k", P), ("dec_kv", 2 * P), ("dec_proj", P), ("dec_b", 1),
    ("slope_col", 1), ("slope_row", D), ("slope_heads", HEADS),
    ("moe_gamma", 1), ("moe_beta", 1), ("moe_wr", 2 * E), ("moe_br", 2 * E), ("moe_b1", E), ("moe_b2", E),
    ("moe_w2", E * D), ("moe_w1", HALVES * E * HID),
]
CONSTS = [
    ("center", P), ("mean", P), ("ident", P), ("swap", P), ("both", P), ("pe", COLS), ("head_block", D),
    ("head_mask", HALVES * HEADS), ("diff", P), ("causal", P), ("pos_row", P), ("pos_left", 1),
    ("vocab", 3), ("pick_expert", E * P), ("iota_e", E),
]
LAYER_A = [("wqv", 2 * P), ("wk", P), ("wo", D), ("g1", 1), ("b1", 1), ("bo", 1)]
LAYER_B = [("w1", HALVES * FF), ("w2", 2 * D), ("bf1", 2), ("bf2", 1), ("g2", 1), ("b2", 1)]


def offsets(table):
    out, at = {}, 0
    for name, width in table:
        out[name] = (at, width)
        at += width
    return out, at


W_AT, W_N = offsets(WEIGHTS)
C_AT, C_N = offsets(CONSTS)
A_AT, A_N = offsets(LAYER_A)
B_AT, B_N = offsets(LAYER_B)


LATE = W_AT["dec_q"][0]


def build(nc, token_idx, id_table, weights, consts, layer_a, layer_b, out):
    ctx = ExitStack()
    with ctx:
        def sb(name, shape, dt=F32):
            return ctx.enter_context(nc.sbuf_tensor(name, shape, dt))

        def sem(name):
            return ctx.enter_context(nc.semaphore(name))

        wt = sb("wt", [P, W_N])
        ct = sb("ct", [P, C_N])
        la = sb("la", [P, A_N])
        lb = sb("lb", [P, B_N])

        def W(name):
            at, n = W_AT[name]
            return wt[:, at:at + n]

        def C(name):
            at, n = C_AT[name]
            return ct[:, at:at + n]

        def A(name):
            at, n = A_AT[name]
            return la[:, at:at + n]

        def B(name):
            at, n = B_AT[name]
            return lb[:, at:at + n]

        def big(name):
            return sb(name, [P, COLS])

        def chunk(t, c):
            return t[:, c * CH:(c + 1) * CH]

        def group(t, g):
            return t[:, g * GC:(g + 1) * GC]

        ps = ctx.enter_context(nc.psum_tensor("ps", [P, 8, CH], F32))

        idx = sb("idx", [P, NT], I32)
        ids = sb("ids", [P, NT, SLOTS], I32)
        ids_b = sb("ids_b", [P, NT, SLOTS], BF16)
        ident_b = sb("ident_b", [P, P], BF16)
        keep_b = sb("keep_b", [P, P], BF16)
        eps_col = sb("eps_col", [P, 1])
        ids_T = sb("ids_T", [P, COLS], BF16)
        stats = sb("stats", [P, 2, 6])
        mv = sb("mv", [P, 2, 2])
        tab_rstd = sb("tab_rstd", [P, 2])
        comp_n = sb("comp_n", [P, 2, D])
        comp_T = sb("comp_T", [D, 2 * P])
        op_T = sb("op_T", [D, D])
        tree_w = sb("tree_w", [P, 3, P])
        tree_bias = sb("tree_bias", [P, 1])
        leaf_hi = sb("leaf_hi", [P, 2, P], BF16)
        leaf_mid = sb("leaf_mid", [P, 2, P], BF16)
        leaf_lo = sb("leaf_lo", [P, 2, P], BF16)
        op_hm = sb("op_hm", [P, D], BF16)
        op_lo = sb("op_lo", [P, D], BF16)
        leaf_rest = sb("leaf_rest", [P, 2, P])
        op_rest = sb("op_rest", [P, D])
        wide = sb("wide", [P, NT * HEADS * (D + DH)])
        node1 = [wide[:, k * COLS:(k + 1) * COLS] for k in range(4)]
        node2 = [wide[:, k * COLS:(k + 1) * COLS] for k in range(4, 6)]
        v_heads = wide[:, :].rearrange("p (n w) -> p n w", n=NT)
        space = sb("space", [P, 8, COLS])

        def view(k, inner=None):
            t = space[:, k, :]
            return t if inner is None else t.rearrange("p (n w) -> p n w", w=inner)

        onehot = space[:, 3:8, :].rearrange("p a b -> p (a b)").bitcast(BF16) \
            .rearrange("p (g r n) -> p g r n", g=HOT_BUFS, r=5)
        upper_hot = onehot.rearrange("p g r n -> p (g r) n")
        ids_wide = space[:, 1:3, :].rearrange("p a b -> p (a b)").bitcast(BF16)[:, 0:2 * 3 * CH] \
            .rearrange("p (g r n) -> p g r n", g=2, r=3)

        hres = big("hres")
        x = big("x")
        hn = big("hn")
        norm_tmp = big("norm_tmp")
        squares = big("squares")
        logs = big("logs")
        rstd = big("rstd")

        k_exp = view(0)
        k_tok = view(1, P)
        v_tok = view(2, D)
        q_max = sb("q_max", [P, NT, HEADS])
        q_sh = view(3, D)
        q_e = view(4, D)
        q_sum = sb("q_sum", [P, NT, HEADS])
        q_inv = sb("q_inv", [P, NT, HEADS])
        q_n = view(5, D)
        q_T = view(6)
        k_part = sb("k_part", [P, 2])
        k_own = sb("k_own", [P, 1])
        k_neg = sb("k_neg", [P, 1])
        k_sums = sb("k_sums", [P, 2])
        k_half = sb("k_half", [P, 1])
        k_inv = sb("k_inv", [P, 1])
        ctx_T = sb("ctx_T", [P, D])
        mix = sb("mix", [P, P])
        act_h = sb("act_h", [P, 4, CH])

        f_state = view(0)
        f_tanh = view(1)
        f_mid = view(2)
        f_gate = view(4)
        f_wt = sb("f_wt", [P, P])
        f_w = sb("f_w", [P, P])
        f_sumsq = sb("f_sumsq", [P, NG, 4])
        f_rstd_sb = sb("f_rstd_sb", [P, NG, 4])
        minus_half = sb("minus_half", [P, 4])
        f_squares = sb("f_squares", [P, NT, D + 1])
        f_tok = view(5)
        f_c = sb("f_c", [P, 1])
        f_c_gain = sb("f_c_gain", [P, 1])

        dq = view(0)
        dk = view(1)
        dqd = view(2)
        q_heads = sb("q_heads", [P, 2, HALVES, HEADS, 2 * P])
        kd_tok = view(3, D)
        dv_tok = view(4, D)
        pick_b = sb("pick_b", [P, E * P], BF16)
        slope_neg = sb("slope_neg", [P, 1])
        row_neg = sb("row_neg", [P, D])
        heads_neg = sb("heads_neg", [P, HEADS])
        q_decay = sb("q_decay", [P, P])
        k_decay = sb("k_decay", [P, D])
        block_decay = sb("block_decay", [P, 1])
        decay = sb("decay", [P, HEADS, P])
        updates = view(5, D)
        state = view(6, D)
        state_rows = sb("state_rows", [P, NT, D])
        scored = act_h
        d_out = view(7)
        d_state_out = squares[:, 0:CH]

        xn = view(0)
        logits = sb("logits", [P, NT, E])
        top = sb("top", [P, NT, 8])
        top_i = sb("top_i", [P, NT, 8], U32)
        top_f = sb("top_f", [P, NT, 2])
        gap = sb("gap", [P, NT])
        gap_e = sb("gap_e", [P, NT])
        den = sb("den", [P, NT])
        w_1 = sb("w_1", [P, NT])
        w_2 = sb("w_2", [P, NT])
        pick_1 = sb("pick_1", [P, NT, E])
        pick_2 = sb("pick_2", [P, NT, E])
        share_1 = sb("share_1", [P, NT, E])
        share_2 = sb("share_2", [P, NT, E])
        share = sb("share", [P, NT, E])
        share_rest = sb("share_rest", [P, NB, HALVES * E])
        share_parts = sb("share_parts", [P, NB, 3, HALVES * E], BF16)
        share_T = view(1).bitcast(BF16)[:, 0:COLS]
        share_w = view(2, CH)
        y_part = view(3, CH)
        out_tok = view(4, P)

        weights_in = sem("weights_in")
        late_weights_in = sem("late_weights_in")
        row_stats = sem("row_stats")
        rows_summed = sem("rows_summed")
        hn_ready = sem("hn_ready")
        consts_in = sem("consts_in")
        idx_in = sem("idx_in")
        ids_in = [sem("ids_in_0"), sem("ids_in_1")]
        ids_b_ready = sem("ids_b_ready")
        ids_turned = sem("ids_turned")
        ids_T_ready = sem("ids_T_ready")
        layer_a_in = sem("layer_a_in")
        layer_b_in = sem("layer_b_in")
        pool_zeroed = sem("pool_zeroed")
        slopes_ready = sem("slopes_ready")
        decay_masked = sem("decay_masked")
        v_heads_ready = sem("v_heads_ready")
        d_stated = sem("d_stated")
        d_state_sb = sem("d_state_sb")
        vec_order = sem("vec_order")
        act_order = sem("act_order")
        pe_prep = sem("pe_prep")
        vec_prep = sem("vec_prep")
        act_prep = sem("act_prep")
        ids_wide_ps = sem("ids_wide_ps")
        ids_wide_sb = sem("ids_wide_sb")
        onehot_ready = sem("onehot_ready")
        tree_sq = sem("tree_sq")
        tree_var = sem("tree_var")
        tree_rstd = sem("tree_rstd")
        tree_node = sem("tree_node")
        ln_in = sem("ln_in")
        ln_centered = sem("ln_centered")
        ln_squared = sem("ln_squared")
        ln_var = sem("ln_var")
        ln_rstd = sem("ln_rstd")
        qv_ready = sem("qv_ready")
        k_ready = sem("k_ready")
        k_max = sem("k_max")
        k_swapped = sem("k_swapped")
        k_negmax = sem("k_negmax")
        k_exped = sem("k_exped")
        k_turned = sem("k_turned")
        k_tok_ready = sem("k_tok_ready")
        v_tok_ready = sem("v_tok_ready")
        q_shifted = sem("q_shifted")
        q_exped = sem("q_exped")
        q_normed = sem("q_normed")
        q_turned = sem("q_turned")
        q_T_ready = sem("q_T_ready")
        k_summed = sem("k_summed")
        k_total = sem("k_total")
        ctx_ready = sem("ctx_ready")
        ctx_masked = sem("ctx_masked")
        mix_ps = sem("mix_ps")
        mix_ready = sem("mix_ready")
        attn_ready = sem("attn_ready")
        up_ready = sem("up_ready")
        gelu_ready = sem("gelu_ready")
        down_ready = sem("down_ready")
        f_state_ready = sem("f_state_ready")
        f_tanh_ready = sem("f_tanh_ready")
        f_mid_ready = sem("f_mid_ready")
        f_gate_ready = sem("f_gate_ready")
        f_squared = sem("f_squared")
        f_rstd = sem("f_rstd")
        f_centred = sem("f_centred")
        f_mapped = sem("f_mapped")
        f_summed = sem("f_summed")
        f_scaled = sem("f_scaled")
        f_turned = sem("f_turned")
        pool_order = sem("pool_order")
        d_qk_ps = sem("d_qk_ps")
        d_kv_ps = sem("d_kv_ps")
        d_q_ready = sem("d_q_ready")
        d_k_ready = sem("d_k_ready")
        d_kv_ready = sem("d_kv_ready")
        d_heads_ready = sem("d_heads_ready")
        d_upd_ps = sem("d_upd_ps")
        d_state_ready = sem("d_state_ready")
        d_scores = sem("d_scores")
        d_scored = sem("d_scored")
        d_block_out = sem("d_block_out")
        d_out_sb = sem("d_out_sb")
        d_proj = sem("d_proj")
        logits_ps = sem("logits_ps")
        gap_ready = sem("gap_ready")
        gap_exped = sem("gap_exped")
        share_ready = sem("share_ready")
        share_turned = sem("share_turned")
        share_T_ready = sem("share_T_ready")
        share_w_ps = sem("share_w_ps")
        share_w_ready = sem("share_w_ready")
        m_up = sem("m_up")
        m_gelu = sem("m_gelu")
        m_down = sem("m_down")
        m_added = sem("m_added")
        final_turned = sem("final_turned")
        final_tok = sem("final_tok")
        stored = sem("stored")

        class Order:

            def __init__(self, eng, s):
                self.eng, self.s, self.n, self.loop = eng, s, 0, None

            def did(self, ins):
                ins.then_inc(self.s, 1)
                self.n += 1

            def wait(self):
                n = self.n
                if self.loop is not None:
                    i, base, per = self.loop
                    n = i * per + n
                self.eng.wait_ge(self.s, n)

            def enter(self, i, per):
                self.loop = (i, self.n, per)

            def leave(self, count):
                _, base, per = self.loop
                assert self.n - base == per, self.n - base
                self.n = base + per * count
                self.loop = None

        UNITS = [(1, k, c) for c in range(NCH) for k in range(4)] \
            + [(2, k, c) for c in range(NCH) for k in range(2)] + [(3, 0, c) for c in range(NCH)]
        OP_SLOT = {1: LEAVES, 2: LEAVES + 4, 3: LEAVES + 6}
        KEEP_SLOT = SLOTS - 1
        LEAF_STEPS = [(n, half) for n, u in enumerate(UNITS) if u[0] == 1 for half in range(HALVES)]
        UPPER = [(n, half) for n, u in enumerate(UNITS) if u[0] > 1 for half in range(HALVES)]
        STEPS = len(LEAF_STEPS) + len(UPPER) // 3
        UPPER_FROM = len(LEAF_STEPS) // HALVES

        def sources(step):
            if step < len(LEAF_STEPS):
                n, half = LEAF_STEPS[step]
                _, k, c = UNITS[n]
                return [(slot, half, c) for slot in (2 * k, 2 * k + 1, OP_SLOT[1] + k)]
            q = 3 * (step - len(LEAF_STEPS))
            return [(OP_SLOT[UNITS[n][0]] + UNITS[n][1], half, UNITS[n][2]) for n, half in UPPER[q:q + 3]]

        def steps_for(n):
            return HALVES * (n + 1) if n < UPPER_FROM else len(LEAF_STEPS) + (HALVES * (n - UPPER_FROM) + 1) // 3 + 1

        def hot_row(n, half, row):
            if n < UPPER_FROM:
                return onehot[:, (HALVES * n + half) % HOT_BUFS, row, :]
            return upper_hot[:, HALVES * (n - UPPER_FROM) + half, :]

        def bank(n):
            return ps[:, n, :]

        SUM_BANKS = 3

        def sum_bank(n):
            return bank((3, 4, 7)[n % SUM_BANKS])

        def centred(g):
            return ps[:, g, 0:GC]

        def mapped(g):
            return ps[:, (g + NG - 1) % NG, GC:2 * GC]

        def runs(s, back, ending, t):
            return back > t if ending else not (isinstance(s, int) and s < back)

        block = ctx.enter_context(nc.Block())

        @block.sync
        def _(sp):
            sp.dma_start(idx[:, :], token_idx).then_inc(idx_in, 16)
            sp.dma_start(wt[:, 0:LATE], weights[:, 0:LATE]).then_inc(weights_in, 16)
            sp.dma_start(la[:, :], layer_a[0]).then_inc(layer_a_in, 16)
            sp.dma_start(lb[:, :], layer_b[0]).then_inc(layer_b_in, 16)
            sp.dma_start(wt[:, LATE:W_N], weights[:, LATE:W_N]).then_inc(late_weights_in, 16)
            for i in range(1, LAYERS):
                sp.wait_ge(attn_ready, i * NCH)
                sp.wait_ge(ln_in, i * 2 * NCH + NCH)
                sp.dma_start(la[:, :], layer_a[i]).then_inc(layer_a_in, 16)
                sp.wait_ge(down_ready, i * 8)
                sp.wait_ge(ln_in, i * 2 * NCH + 2 * NCH)
                sp.dma_start(lb[:, :], layer_b[i]).then_inc(layer_b_in, 16)
            sp.wait_ge(final_tok, NCH)
            for half in range(HALVES):
                sp.dma_start(out[0, half * COLS:(half + 1) * COLS, :].rearrange("(j p) d -> p j d", p=P),
                             out_tok[:, :, half * D:(half + 1) * D]).then_inc(stored, 16)
            sp.wait_ge(stored, 16 * HALVES)

        @block.gpsimd
        def _(pool):
            pool.wait_ge(idx_in, 16)
            for n in range(NT):
                pool.indirect_dma_start(ids[:, n, :], None, id_table,
                                        bass.IndirectOffsetOnAxis(ap=idx[:, n:n + 1], axis=0)) \
                    .then_inc(ids_in[n // (NT // NCH)], 16)
            nc.gpsimd.memset(mix[:, :], 0.0).then_inc(pool_zeroed, 1)
            nc.gpsimd.memset(state_rows[:, :, :], 0.0).then_inc(pool_zeroed, 1)
            for h in range(HEADS):
                pool.wait_ge(act_prep, h + 2)
                nc.gpsimd.tensor_tensor(decay[:, h, :], decay[:, h, :], C("causal"), ALU.mult).then_inc(decay_masked, 1)
            pool.wait_ge(ln_in, NCH)
            nc.gpsimd.memset(wide[:, :], 0.0).then_inc(pool_zeroed, 1)
            nc.gpsimd.memset(minus_half[:, :], -0.5).then_inc(pool_order, 1)
            nc.gpsimd.memset(f_squares[:, :, D:D + 1], EPS * D).then_inc(pool_order, 1)
            pool.wait_ge(pool_order, 2)
            with pool.Fori(0, ITERS) as i:
                for g in range(NG):
                    pool.wait_ge(f_summed, i * NG + (g + 1))
                    nc.gpsimd.tensor_tensor(f_rstd_sb[:, g, :], f_sumsq[:, g, :], minus_half[:, :], ALU.pow).then_inc(f_rstd, 1)

        @block.tensor
        def _(pe):
            def mm(o, l, r, start=True, stop=True, **kw):
                return nc.tensor.matmul(o, l, r, start=start, stop=stop, **kw)

            pe.wait_ge(weights_in, 16)
            pe.wait_ge(consts_in, 16)
            for k, name in enumerate(("wo_T", "wl_T", "wr_T")):
                mm(bank(0)[:, k * P:(k + 1) * P], W(name), C("center"))
            mm(bank(1)[:, 0:1], C("center"), W("tok_b")).then_inc(pe_prep, 1)
            pe.wait_ge(vec_prep, 1)
            for k in range(2):
                nc.tensor.transpose(bank(2)[0:D, k * P:(k + 1) * P], comp_n[:, k, :], C("ident"))
            nc.tensor.transpose(bank(2)[0:D, 2 * P:2 * P + D], W("op")[0:D, :], C("ident")[0:D, 0:D]).then_inc(pe_prep, 1)
            pe.wait_ge(vec_prep, 2)
            for k in range(2):
                for side in range(2):
                    mm(bank(4)[:, k * P + side * D:k * P + (side + 1) * D], comp_T[:, k * P:(k + 1) * P],
                       tree_w[0:D, 1 + side, 0:D])
            mm(bank(5)[0:D, 0:D], op_T[:, :], tree_w[0:D, 0, 0:D])
            mm(bank(5)[D:P, 0:D], op_T[:, :], tree_w[0:D, 0, 0:D]).then_inc(pe_prep, 1)
            def turn_ids(c):
                pe.wait_ge(ids_b_ready, c + 1)
                for j in range(4 * c, 4 * c + 4):
                    t = ps[:, 7, :].bitcast(BF16)[0:HALVES * SLOTS, j * P:(j + 1) * P]
                    last = nc.tensor.transpose(t, ids_b[:, 2 * j:2 * j + 2, :].rearrange("p h s -> p (h s)"), ident_b[:, :])
                last.then_inc(ids_turned, 1)

            pe.wait_ge(vec_prep, 4)
            turn_ids(0)
            pe.wait_ge(ids_T_ready, 1)

            def spread(g):
                if g >= 1:
                    pe.wait_ge(ids_wide_sb, g)
                for b, (slot, half, c) in enumerate(sources(g)):
                    last = mm(bank(b), ident_b[:, half * SLOTS + slot:half * SLOTS + slot + 1].broadcast_to([P, P]), chunk(ids_T, c))
                last.then_inc(ids_wide_ps, 1)

            def passes(n):
                level = UNITS[n][0]
                out = []
                if level == 1:
                    out = [(part[:, v, side * D:(side + 1) * D], 2 * side + v)
                           for part in (leaf_hi, leaf_mid, leaf_lo) for side in range(2) for v in range(2)]
                return out + [(op_hm[:, :], 4), (op_lo[:, :], 4)]

            def gather(n, some, ending):
                for q, (part, row) in enumerate(some):
                    for half in range(HALVES):
                        last = mm(sum_bank(n)[half * D:(half + 1) * D, :], part, hot_row(n, half, row),
                                  UNITS[n][0] == 1 and not ending and q == 0, ending and q == len(some) - 1,
                                  skip_group_check=True)
                        if ending and q == len(some) - 1:
                            last.then_inc(rows_summed, 1)

            def variance(n):
                pe.wait_ge(tree_sq, n + 1)
                mm(bank(5 + n % 2), C("mean"), squares[:, (n % 2) * CH:(n % 2 + 1) * CH]).then_inc(tree_var, 1)

            for g in range(HALVES):
                spread(g)
            for n, (level, k, c) in enumerate(UNITS):
                if 2 * n + 2 < STEPS:
                    spread(2 * n + 2)
                if n == 1:
                    turn_ids(1)
                if n == 2:
                    pe.wait_ge(ids_T_ready, 2)
                if n >= SUM_BANKS:
                    pe.wait_ge(tree_node, n - SUM_BANKS + 1)
                if level > 1:
                    src = node1 if level == 2 else node2
                    pe.wait_ge(tree_node, UNITS.index((level - 1, 2 * k + 1, c)) + 1)
                    mm(sum_bank(n), tree_w[:, 1, :], chunk(src[2 * k], c), True, False, skip_group_check=True)
                    mm(sum_bank(n), tree_w[:, 2, :], chunk(src[2 * k + 1], c), False, False, skip_group_check=True)
                pe.wait_ge(onehot_ready, steps_for(n))
                todo = passes(n)
                cut = 4 if level == 1 else 0
                gather(n, todo[:cut], False)
                if n >= 1:
                    variance(n - 1)
                if 2 * n + 3 < STEPS:
                    spread(2 * n + 3)
                gather(n, todo[cut:], True)
            variance(len(UNITS) - 1)
            pe.wait_ge(ids_wide_sb, STEPS)
            for c in range(NCH):
                mm(bank(c), keep_b[:, :], chunk(ids_T, c)).then_inc(pe_prep, 1)

            mm(bank(7)[:, 0:P], C("center"), f_wt[:, :])
            mm(bank(7)[:, P:P + 1], W("ffn_wT"), W("ffn_ln_b")).then_inc(pe_prep, 1)

            def centre(n, c, src=x):
                pe.wait_ge(ln_in, n * NCH + (c + 1))
                mm(bank(c), C("center"), chunk(src, c)).then_inc(ln_centered, 1)

            def mean_square(n, c):
                pe.wait_ge(ln_squared, n * NCH + (c + 1))
                mm(bank(2 + c), C("mean"), chunk(squares, c)).then_inc(ln_var, 1)

            def ln(n, src=x):
                for c in range(NCH):
                    centre(n, c, src)
                for c in range(NCH):
                    mean_square(n, c)

            ln(0)
            ln(1)
            with pe.Fori(0, LAYERS) as i:
                pe.wait_ge(layer_a_in, i * 16 + 16)
                for c in range(NCH):
                    pe.wait_ge(hn_ready, i * 2 * NCH + (c + 1))
                    mm(bank(c), A("wk"), chunk(hn, c)).then_inc(k_ready, 1)
                    for j in range(4 * c, 4 * c + 4):
                        last = mm(ps[:, 4 + j // 2, (j % 2) * 2 * P:(j % 2 + 1) * 2 * P], hn[:, j * P:(j + 1) * P], A("wqv"))
                        if j % 2 == 1:
                            last.then_inc(qv_ready, 1)
                pe.wait_ge(k_max, i + 1)
                mm(bank(2)[:, 0:1], C("swap"), k_own[:, :]).then_inc(k_swapped, 1)
                pe.wait_ge(k_negmax, i + 1)
                for c in range(NCH):
                    pe.wait_ge(k_exped, i * NCH + (c + 1))
                    for j in range(4 * c, 4 * c + 4):
                        last = nc.tensor.transpose(ps[:, 2 + c, (j % 4) * P:(j % 4 + 1) * P],
                                                   k_exp[:, j * P:(j + 1) * P], C("ident"))
                    last.then_inc(k_turned, 1)

                def turn_queries(c):
                    pe.wait_ge(q_normed, i * NCH + (c + 1))
                    for j in range(4 * c, 4 * c + 4):
                        last = nc.tensor.transpose(ps[:, 4 + c, (j % 4) * P:(j % 4 + 1) * P],
                                                   q_n[:, 2 * j:2 * j + 2, :].rearrange("p h d -> p (h d)"), C("ident"))
                    last.then_inc(q_turned, 1)

                for c in range(NCH):
                    pe.wait_ge(v_tok_ready, i * 4 + (2 * c + 2))
                    pe.wait_ge(k_tok_ready, i * NCH + (c + 1))
                    for n in range(8 * c, 8 * c + 8):
                        j, half = n // 2, n % 2
                        last = mm(ps[half * D:(half + 1) * D, 0, 0:D], v_tok[:, n, :], k_tok[:, j, half * D:(half + 1) * D],
                                  j == 0, j == NB - 1)
                        if n == NT - 2:
                            last.then_inc(ctx_ready, 1)
                    if c == 0:
                        turn_queries(0)
                last.then_inc(ctx_ready, 1)
                pe.wait_ge(k_summed, i + 1)
                mm(bank(1)[:, 0:1], C("both"), k_half[:, :]).then_inc(k_total, 1)
                pe.wait_ge(ctx_masked, i + 1)
                mm(ps[0:D, 2, 0:D], ctx_T[:, :], A("wo"))
                mm(ps[D:P, 2, 0:D], ctx_T[:, :], A("wo")).then_inc(mix_ps, 1)
                turn_queries(1)
                pe.wait_ge(mix_ready, i * 2 + 2)
                for c in range(NCH):
                    pe.wait_ge(q_T_ready, i * NCH + (c + 1))
                    mm(bank(6 + c), mix[:, :], chunk(q_T, c)).then_inc(attn_ready, 1)
                ln(i * 2 + 2)
                pe.wait_ge(layer_b_in, i * 16 + 16)
                ups = [(c, half, m) for c in range(NCH) for m in range(2) for half in range(HALVES)]

                def up(u):
                    c, half, m = ups[u]
                    if u % 4 == 0:
                        pe.wait_ge(hn_ready, i * 2 * NCH + (NCH + c + 1))
                    if u >= 4:
                        pe.wait_ge(gelu_ready, i * len(ups) + (u - 3))
                    mm(bank(4 + u % 4), B("w1")[:, (half * 2 + m) * P:(half * 2 + m + 1) * P], chunk(hn, c)).then_inc(up_ready, 1)

                def down_pair(u):
                    pe.wait_ge(gelu_ready, i * len(ups) + (u + 2))
                    for v in (u, u + 1):
                        c, half, m = ups[v]
                        last = mm(ps[half * D:(half + 1) * D, c, :], B("w2")[:, m * D:(m + 1) * D], act_h[:, v % 4, :],
                                  m == 0, m == 1)
                        last.then_inc(down_ready, 1)

                for u in (0, 2, 4, 6):
                    up(u)
                    up(u + 1)
                    if u == 4:
                        down_pair(0)
                        down_pair(2)
                centre(i * 2 + 3, 0)
                down_pair(4)
                down_pair(6)
                mean_square(i * 2 + 3, 0)
                centre(i * 2 + 3, 1)
                mean_square(i * 2 + 3, 1)

            N9 = 1 + 2 * LAYERS
            for g in range(NG):
                pe.wait_ge(f_state_ready, g // 2 + 1)
                mm(bank(4 + g)[:, 0:GC], C("ident"), group(f_state, g)).then_inc(f_turned, 1)

            def slot(s, t, ending=False):
                if runs(s, 1, ending, t):
                    g = (t - 1) % NG
                    pe.wait_ge(f_gate_ready, s)
                    for k in range(2):
                        j = 2 * g + k
                        last = mm(centred(g)[:, k * P:(k + 1) * P], f_gate[:, j * P:(j + 1) * P], C("center"))
                    last.then_inc(f_centred, 1)
                    if runs(s, 2, ending, t):
                        pe.wait_ge(f_squared, s - 1)
                    for k in range(2):
                        j = 2 * g + k
                        last = mm(mapped(g)[:, k * P:(k + 1) * P], f_gate[:, j * P:(j + 1) * P], f_w[:, :])
                    last.then_inc(f_mapped, 1)
                if runs(s, 3, ending, t):
                    g = (t - 3) % NG
                    pe.wait_ge(f_scaled, s - 2)
                    for k in range(2):
                        j = 2 * g + k
                        last = nc.tensor.transpose(bank(4 + g)[:, k * P:(k + 1) * P], f_tok[:, j * P:(j + 1) * P], C("ident"))
                    last.then_inc(f_turned, 1)

            for t in range(NG):
                slot(t, t)
            with pe.Fori(1, ITERS) as i:
                for t in range(NG):
                    slot(i * NG + t, t)
            for t in range(3):
                slot(ITERS * NG + t, t, True)

            ln(N9 + 1, hres)
            pe.wait_ge(late_weights_in, 16)
            for c in range(NCH):
                pe.wait_ge(hn_ready, 2 * LAYERS * NCH + (c + 1))
                mm(bank(c), W("dec_q"), chunk(hn, c)).then_inc(d_qk_ps, 1)
                for j in range(4 * c, 4 * c + 4):
                    last = mm(ps[:, 4 + j // 2, (j % 2) * 2 * P:(j % 2 + 1) * 2 * P], hn[:, j * P:(j + 1) * P], W("dec_kv"))
                    if j % 2 == 1:
                        last.then_inc(d_kv_ps, 1)
            for c in range(NCH):
                mm(bank(2 + c), W("dec_k"), chunk(hn, c)).then_inc(d_qk_ps, 1)
            pe.wait_ge(d_kv_ready, 4)
            for n in range(NT):
                mm(ps[0:D, 4 + n // 8, (n % 8) * D:(n % 8 + 1) * D], kd_tok[:, n, :], dv_tok[:, n, :])
                last = mm(ps[D:P, 4 + n // 8, (n % 8) * D:(n % 8 + 1) * D], kd_tok[:, n, :], dv_tok[:, n, :])
            last.then_inc(d_upd_ps, 1)
            score_units = [(j, g, half) for j in range(NB) for g in range(2) for half in range(HALVES)]

            def score(u):
                j, g, half = score_units[u]
                quarter = j // 2
                if u % 8 < 4:
                    pe.wait_ge(d_heads_ready, quarter * HALVES * HEADS + (u % 8 + 1) * 4)
                if u in (0, 3):
                    pe.wait_ge(d_k_ready, 1 if u == 0 else NCH)
                if u >= 4:
                    pe.wait_ge(d_scored, u - 3)
                rhs = q_heads[:, quarter % 2, half, 4 * g:4 * g + 4, (j % 2) * P:(j % 2 + 1) * P]
                mm(bank(u % 4), dk[:, j * P:(j + 1) * P], rhs).then_inc(d_scores, 1)

            def spend_pair(u):
                j, g, _ = score_units[u]
                o = [ps[half * D:(half + 1) * D, 6 + j // 4, (j % 4) * P:(j % 4 + 1) * P] for half in range(HALVES)]
                pe.wait_ge(d_scored, u + 2)
                for h in range(4):
                    for half in range(HALVES):
                        last = mm(o[half], v_heads[:, 2 * j + half, (4 * g + h) * D:(4 * g + h + 1) * D],
                                  scored[:, (u + half) % 4, h * P:(h + 1) * P], g == 0 and h == 0,
                                  j < NB // 2 and g == 1 and h == 3)
                        if h == 3:
                            last.then_inc(d_block_out, 1)
                if g == 1 and j >= NB // 2:
                    state_terms(j)

            def state_terms(j):
                late = j >= NB // 2
                for half in range(HALVES):
                    mm(ps[half * D:(half + 1) * D, 7 if late else 4, (j % 4) * P:(j % 4 + 1) * P], state_rows[:, 2 * j + half, :],
                       dqd[:, j * P:(j + 1) * P], not late, True).then_inc(d_stated, 1)

            score(0)
            score(1)
            for u in range(0, len(score_units), 2):
                if u + 2 < len(score_units):
                    score(u + 2)
                    score(u + 3)
                if u == 0:
                    pe.wait_ge(v_heads_ready, 2)
                spend_pair(u)
                if u == 16:
                    pe.wait_ge(d_state_ready, 2)
                    for j in range(NB // 2):
                        state_terms(j)
            for c in range(NCH):
                pe.wait_ge(d_out_sb, c + 1)
                last = mm(bank(c), W("dec_proj"), chunk(d_out, c), True, c > 0)
                if c == 0:
                    pe.wait_ge(d_state_sb, 1)
                    last = mm(bank(c), W("dec_proj"), d_state_out[:, :], False, True)
                last.then_inc(d_proj, 1)

            ln(N9 + 2, hres)
            ln(N9 + 3)
            pe.wait_ge(hn_ready, (2 * LAYERS + 2) * NCH)
            for j in range(NB):
                last = mm(bank(4)[:, j * 2 * E:(j + 1) * 2 * E], xn[:, j * P:(j + 1) * P], W("moe_wr"))
            last.then_inc(logits_ps, 1)
            units = [(e, c, half) for e in range(E) for c in range(NCH) for half in range(HALVES)]

            def up(u):
                e, c, half = units[u]
                if u >= 4:
                    pe.wait_ge(m_gelu, u - 3)
                mm(bank(u % 4), W("moe_w1")[:, (half * E + e) * P:(half * E + e + 1) * P], chunk(xn, c)).then_inc(m_up, 1)

            for u in range(4):
                up(u)
            pe.wait_ge(share_ready, 1)
            for j in range(NB):
                last = nc.tensor.transpose(ps[:, 5, :].bitcast(BF16)[0:3 * 2 * E, j * P:(j + 1) * P],
                                           share_parts[:, j, :, :].rearrange("p k e -> p (k e)"), ident_b[:, :])
            last.then_inc(share_turned, 1)
            pe.wait_ge(share_T_ready, 2)
            for v in range(E * NCH):
                e, c = v // NCH, v % NCH
                if v >= 2:
                    pe.wait_ge(share_w_ready, v - 1)
                mm(bank(6 + v % 2), pick_b[:, e * P:(e + 1) * P], chunk(share_T, c)).then_inc(share_w_ps, 1)
                for u in (2 * v + 2, 2 * v + 3):
                    if 4 <= u < len(units):
                        up(u)
                if v >= 2:
                    pe.wait_ge(m_added, v - 1)
                pe.wait_ge(m_gelu, 2 * v + 2)
                for half in range(HALVES):
                    last = mm(ps[half * D:(half + 1) * D, 4 + v % 2, :], W("moe_w2")[:, e * D:(e + 1) * D],
                              act_h[:, (2 * v + half) % 4, :])
                last.then_inc(m_down, 1)
            for c in range(NCH):
                pe.wait_ge(m_added, (E - 1) * NCH + c + 1)
                for j in range(4 * c, 4 * c + 4):
                    last = nc.tensor.transpose(ps[:, c, (j % 4) * P:(j % 4 + 1) * P], hres[:, j * P:(j + 1) * P], C("ident"))
                last.then_inc(final_turned, 1)

        @block.scalar
        def _(act):
            order = Order(act, act_order)
            A_ = nc.scalar.activation
            log_exp = "natural_log_exp_and_others"
            nc.scalar.preload_act_table_set(log_exp)
            act.dma_start(ct[:, :], consts).then_inc(consts_in, 16)
            act.wait_ge(weights_in, 16)
            act.wait_ge(row_stats, 4)
            order.did(A_(tab_rstd[:, :], mv[:, :, 1], ACT.Ln, bias=eps_col[:, 0:1]))
            order.wait()
            A_(tab_rstd[:, :], tab_rstd[:, :], ACT.Exp, scale=-0.5).then_inc(act_prep, 1)
            def ids_out(c):
                act.wait_ge(ids_turned, c + 1)
                A_(chunk(ids_T, c)[0:HALVES * SLOTS, :], ps[:, 7, :].bitcast(BF16)[0:HALVES * SLOTS, c * CH:(c + 1) * CH],
                   ACT.Copy).then_inc(ids_T_ready, 1)

            act.wait_ge(vec_prep, 3)
            ids_out(0)

            def widen(g):
                act.wait_ge(ids_wide_ps, g + 1)
                if g >= 2:
                    act.wait_ge(onehot_ready, g - 1)
                A_(ids_wide[:, g % 2, :, :], ps[:, 0:3, :], ACT.Copy).then_inc(ids_wide_sb, 1)

            def root_mean(n):
                act.wait_ge(rows_summed, HALVES * (n + 1))
                if n >= 2:
                    act.wait_ge(tree_var, n - 1)
                sq = squares[:, (n % 2) * CH:(n % 2 + 1) * CH]
                A_(sq, sum_bank(n), ACT.Square, bias=tree_bias[:, 0:1]).then_inc(tree_sq, 1)

            def root_rest(n):
                lg = logs[:, (n % 2) * CH:(n % 2 + 1) * CH]
                act.wait_ge(tree_var, n + 1)
                order.did(A_(lg, bank(5 + n % 2), ACT.Ln, bias=eps_col[:, 0:1]))
                if n >= 2:
                    act.wait_ge(tree_node, n - 1)
                order.wait()
                A_(rstd[:, (n % 2) * CH:(n % 2 + 1) * CH], lg, ACT.Exp, scale=-0.5).then_inc(tree_rstd, 1)

            decays = [(decay[:, h, :], C("diff"), heads_neg[:, h:h + 1]) for h in range(HEADS)] \
                + [(q_decay[:, :], C("pos_row"), slope_neg[:, 0:1]), (k_decay[:, :], row_neg[:, :], C("pos_left")),
                   (block_decay[:, :], slope_neg[:, :], float(P))]
            for g in range(HALVES):
                widen(g)
            for n in range(len(UNITS)):
                if 2 * n + 2 < STEPS:
                    widen(2 * n + 2)
                if n == 1:
                    ids_out(1)
                if n >= 1:
                    root_rest(n - 1)
                if 2 * n + 3 < STEPS:
                    widen(2 * n + 3)
                root_mean(n)
                if n == 5:
                    act.wait_ge(slopes_ready, 3)
                for dst, src, scale in decays[2 * (n - 5):2 * (n - 4)] if n >= 5 else []:
                    A_(dst, src, ACT.Exp, scale=scale).then_inc(act_prep, 1)
            root_rest(len(UNITS) - 1)

            def ln_square(n, c):
                act.wait_ge(ln_centered, n * NCH + (c + 1))
                A_(chunk(squares, c), bank(c), ACT.Square).then_inc(ln_squared, 1)

            def ln_root(n, c):
                act.wait_ge(ln_var, n * NCH + (c + 1))
                order.did(A_(chunk(logs, c), bank(2 + c), ACT.Ln, bias=eps_col[:, 0:1]))
                order.wait()
                A_(chunk(rstd, c), chunk(logs, c), ACT.Exp, scale=-0.5).then_inc(ln_rstd, 1)

            def ln(n):
                for c in range(NCH):
                    ln_square(n, c)
                for c in range(NCH):
                    ln_root(n, c)

            ln(0)
            ln(1)
            with act.Fori(0, LAYERS) as i:
                order.enter(i, 2 * NCH)
                act.wait_ge(k_negmax, i + 1)
                for c in range(NCH):
                    A_(chunk(k_exp, c), bank(c), ACT.Exp, bias=k_neg[:, 0:1],
                       accum_out=k_sums[:, c:c + 1]).then_inc(k_exped, 1)
                for c in range(NCH):
                    act.wait_ge(q_shifted, i * 4 + (2 * c + 2))
                    A_(q_e[:, 8 * c:8 * c + 8, :], q_sh[:, 8 * c:8 * c + 8, :], ACT.Exp).then_inc(q_exped, 1)
                    for b in range(2 * c, 2 * c + 2):
                        A_(v_tok[:, 4 * b:4 * b + 4, :], bank(4 + b).rearrange("p (n w) -> p n w", n=4)[:, :, D:2 * D],
                           ACT.Copy).then_inc(v_tok_ready, 1)
                    act.wait_ge(k_turned, i * NCH + (c + 1))
                    A_(k_tok[:, 4 * c:4 * c + 4, :], bank(2 + c).rearrange("p (j w) -> p j w", j=4),
                       ACT.Copy).then_inc(k_tok_ready, 1)
                for c in range(NCH):
                    act.wait_ge(q_turned, i * NCH + (c + 1))
                    A_(chunk(q_T, c), bank(4 + c), ACT.Copy).then_inc(q_T_ready, 1)
                ln(i * 2 + 2)
                act.wait_ge(layer_b_in, i * 16 + 16)
                for u in range(8):
                    act.wait_ge(up_ready, i * 8 + (u + 1))
                    if u == 4:
                        act.wait_ge(down_ready, i * 8 + 4)
                    m = u // 2 % 2
                    A_(act_h[:, u % 4, :], bank(4 + u % 4), ACT.Gelu, bias=B("bf1")[:, m:m + 1]).then_inc(gelu_ready, 1)
                nc.scalar.preload_act_table_set(log_exp)
                for c in range(NCH):
                    ln_square(i * 2 + 3, c)
                    ln_root(i * 2 + 3, c)
            order.leave(LAYERS)
            nc.scalar.preload_act_table(ACT.Silu)

            def slot(s, t, ending=False):
                if runs(s, 1, ending, t):
                    g = (t - 1) % NG
                    act.wait_ge(f_mid_ready, s)
                    A_(group(f_gate, g), group(f_mid, g), ACT.Silu, scale=1.0 / NORM_GAIN).then_inc(f_gate_ready, 1)
                if not ending:
                    act.wait_ge(f_turned, s + 1)
                    A_(group(f_tanh, t), bank(4 + t)[:, 0:GC], ACT.Tanh, bias=f_c[:, 0:1], scale=1.0 / NORM_GAIN).then_inc(f_tanh_ready, 1)
                if runs(s, 1, ending, t):
                    g = (t - 1) % NG
                    act.wait_ge(f_centred, s)
                    A_(f_squares[:, 4 * g:4 * g + 4, 0:D].rearrange("p (j h) d -> p j h d", h=HALVES),
                       centred(g).rearrange("p (j h d) -> p j h d", j=2, h=HALVES),
                       ACT.Square).then_inc(f_squared, 1)

            for t in range(NG):
                slot(t, t)
            with act.Fori(1, ITERS) as i:
                for t in range(NG):
                    slot(i * NG + t, t)
            for t in range(3):
                slot(ITERS * NG + t, t, True)

            nc.scalar.preload_act_table_set(log_exp)
            ln(2 + 2 * LAYERS)
            def queries(c):
                act.wait_ge(d_qk_ps, c + 1)
                A_(chunk(dq, c), bank(c), ACT.Copy, scale=DH ** -0.5).then_inc(d_q_ready, 1)

            def keys(c):
                act.wait_ge(d_qk_ps, NCH + c + 1)
                A_(chunk(dk, c), bank(2 + c), ACT.Copy).then_inc(d_k_ready, 1)

            def heads(quarter, g, half):
                for h in range(4 * g, 4 * g + 4):
                    m = half * HEADS + h
                    A_(q_heads[:, quarter % 2, half, h, :], dq[:, quarter * 2 * P:(quarter + 1) * 2 * P], ACT.Copy,
                       scale=C("head_mask")[:, m:m + 1]).then_inc(d_heads_ready, 1)

            queries(0)
            act.wait_ge(d_q_ready, 1)
            heads(0, 0, 0)
            heads(0, 0, 1)
            queries(1)
            keys(0)
            keys(1)
            heads(0, 1, 0)
            heads(0, 1, 1)
            act.wait_ge(d_q_ready, NCH)
            for quarter in range(1, NB // 2):
                if quarter >= 2:
                    act.wait_ge(d_scores, (quarter - 1) * 8)
                for g in range(2):
                    for half in range(HALVES):
                        heads(quarter, g, half)
            for c in range(NCH):
                act.wait_ge(d_stated, (c + 1) * NB)
                A_(chunk(d_out, c), bank(6 + c), ACT.Copy).then_inc(d_out_sb, 1)
                if c == 0:
                    A_(d_state_out[:, :], bank(4), ACT.Copy).then_inc(d_state_sb, 1)

            ln(3 + 2 * LAYERS)
            ln(4 + 2 * LAYERS)
            act.wait_ge(gap_ready, 1)
            A_(gap_e[:, :], gap[:, :], ACT.Exp).then_inc(gap_exped, 1)
            for u in range(E * NCH * HALVES):
                e, v = u // (NCH * HALVES), u // HALVES
                act.wait_ge(m_up, u + 1)
                if u >= 4 and u % 2 == 0:
                    act.wait_ge(m_down, v - 1)
                A_(act_h[:, u % 4, :], bank(u % 4), ACT.Gelu, bias=W("moe_b1")[:, e:e + 1]).then_inc(m_gelu, 1)
                if u % 2 == 1:
                    act.wait_ge(share_w_ps, v + 1)
                    if v >= 2:
                        act.wait_ge(m_added, v - 1)
                    A_(share_w[:, v % 2, :], bank(6 + v % 2), ACT.Copy).then_inc(share_w_ready, 1)
            for c in range(NCH):
                act.wait_ge(final_turned, c + 1)
                A_(out_tok[:, 4 * c:4 * c + 4, :], bank(c).rearrange("p (j w) -> p j w", j=4), ACT.Copy).then_inc(final_tok, 1)

        @block.vector
        def _(dve):
            order = Order(dve, vec_order)
            V = nc.vector

            def TT(o, a, b, op):
                return V.tensor_tensor(o, a, b, op)

            def TS(o, a, s1, s2, op0, op1):
                return V.tensor_scalar(o, a, s1, s2, op0, op1)

            def STT(o, a, s, b, op0, op1):
                return V.scalar_tensor_tensor(out=o, in0=a, scalar=s, in1=b, op0=op0, op1=op1)

            order.did(V.memset(eps_col[:, :], EPS))
            dve.wait_ge(weights_in, 16)
            comp = W("comp").rearrange("p (k d) -> p k d", k=2)
            for k in range(2):
                V.bn_stats(stats[:, k, :], comp[:, k, :]).then_inc(row_stats, 1)
            dve.wait_ge(row_stats, 2)
            for k in range(2):
                V.bn_aggr(mv[:, k, :], stats[:, k, :]).then_inc(row_stats, 1)
            dve.wait_ge(act_prep, 1)
            for k in range(2):
                order.did(TS(comp_n[:, k, :], comp[:, k, :], mv[:, k, 0:1], tab_rstd[:, k:k + 1], ALU.subtract, ALU.mult))
            order.wait()
            for k in range(2):
                order.did(TT(comp_n[:, k, :], comp_n[:, k, :], W("tok_gamma_row"), ALU.mult))
            order.wait()
            last = TT(comp_n[:, 0, :], comp_n[:, 0, :], W("tok_beta_row"), ALU.add)
            order.did(last)
            TT(comp_n[:, 1, :], comp_n[:, 1, :], W("tok_beta_row"), ALU.add).then_inc(vec_prep, 1)
            order.wait()
            dve.wait_ge(consts_in, 16)
            order.did(V.tensor_copy(ident_b[:, :], C("ident")))
            order.did(V.memset(ids_T[:, :], 0.0))
            dve.wait_ge(pe_prep, 2)
            order.did(V.tensor_copy(tree_w[:, :, :], bank(0)[:, 0:3 * P].rearrange("p (k n) -> p k n", k=3)))
            order.did(V.tensor_copy(tree_bias[:, :], bank(1)[:, 0:1]))
            order.did(V.tensor_copy(comp_T[:, :], bank(2)[0:D, 0:2 * P]))
            V.tensor_copy(op_T[:, :], bank(2)[0:D, 2 * P:2 * P + D]).then_inc(vec_prep, 1)
            order.wait()
            order.did(V.tensor_copy(keep_b[:, 0:D], ident_b[:, KEEP_SLOT:KEEP_SLOT + 1].broadcast_to([P, D])))
            V.tensor_copy(keep_b[:, D:P], ident_b[:, SLOTS + KEEP_SLOT:SLOTS + KEEP_SLOT + 1].broadcast_to([P, D])).then_inc(vec_prep, 1)
            dve.wait_ge(pe_prep, 3)
            leaf = bank(4)[:, 0:2 * P].rearrange("p (k n) -> p k n", k=2)
            opp = bank(5)[:, 0:D]
            order.did(V.tensor_copy(leaf_hi[:, :, :], leaf))
            order.did(V.tensor_copy(op_hm[:, :], opp))
            order.wait()
            order.did(TT(leaf_rest[:, :, :], leaf, leaf_hi[:, :, :], ALU.subtract))
            order.did(TT(op_rest[:, :], opp, op_hm[:, :], ALU.subtract))
            order.wait()
            order.did(V.tensor_copy(leaf_mid[:, :, :], leaf_rest[:, :, :]))
            order.did(V.tensor_copy(op_lo[:, :], op_rest[:, :]))
            order.wait()
            order.did(TT(leaf_lo[:, :, :], leaf_rest[:, :, :], leaf_mid[:, :, :], ALU.subtract))
            order.did(V.tensor_copy(op_hm[D:P, :], op_lo[D:P, :]))
            order.wait()
            order.did(TT(op_rest[:, :], op_rest[:, :], op_lo[:, :], ALU.subtract))
            order.wait()
            order.did(V.tensor_copy(op_lo[0:D, :], op_rest[0:D, :]))
            order.did(V.memset(op_lo[D:P, :], 0.0))
            order.wait()
            TS(f_wt[:, :], W("ffn_wT"), W("ffn_ln_w"), None, ALU.mult, ALU.bypass).then_inc(vec_prep, 1)
            def convert(c):
                t = slice(c * (NT // NCH), (c + 1) * (NT // NCH))
                dve.wait_ge(ids_in[c], 16 * NT // NCH)
                order.did(V.tensor_copy(ids_b[:, t, :], ids[:, t, :]))
                order.wait()
                TS(ids_b[:, t, KEEP_SLOT], idx[:, t], 1.0, None, ALU.is_gt, ALU.bypass).then_inc(ids_b_ready, 1)

            convert(0)

            def compare(g):
                dve.wait_ge(ids_wide_sb, g + 1)
                if g >= HOT_BUFS:
                    dve.wait_ge(rows_summed, min(HALVES * (g // 2 - 1), HALVES * UPPER_FROM))
                wide_ids = ids_wide[:, g % 2, :, :]
                if g < len(LEAF_STEPS):
                    hot = onehot[:, g % HOT_BUFS, :, :]
                    for side in range(2):
                        for v in range(2):
                            TS(hot[:, 2 * side + v, :], wide_ids[:, side, :], C("vocab")[:, v:v + 1], None,
                               ALU.is_equal, ALU.bypass)
                    TS(hot[:, 4, :], wide_ids[:, 2, :], C("vocab")[:, 2:3], None, ALU.is_equal, ALU.bypass).then_inc(onehot_ready, 1)
                else:
                    q = 3 * (g - len(LEAF_STEPS))
                    TS(upper_hot[:, q:q + 3, :], wide_ids, C("vocab")[:, 2:3], None, ALU.is_equal, ALU.bypass).then_inc(onehot_ready, 1)

            def normal(n):
                level, k, c = UNITS[n]
                dve.wait_ge(tree_rstd, n + 1)
                o = chunk(norm_tmp, n % 2)
                r = chunk(rstd, n % 2)
                order.did(STT(o, sum_bank(n), tree_bias[:, 0:1], r, ALU.add, ALU.mult))
                order.wait()
                dst = node1[k] if level == 1 else node2[k] if level == 2 else hres
                TS(chunk(dst, c), o, W("tok_gamma"), W("tok_beta"), ALU.mult, ALU.add).then_inc(tree_node, 1)

            for g in range(HALVES):
                compare(g)
            for n in range(len(UNITS)):
                if 2 * n + 2 < STEPS:
                    compare(2 * n + 2)
                if n >= 1:
                    normal(n - 1)
                if 2 * n + 3 < STEPS:
                    compare(2 * n + 3)
                if n == 0:
                    convert(1)
                if n == 4:
                    dve.wait_ge(late_weights_in, 16)
                    TS(slope_neg[:, :], W("slope_col"), -1.0, None, ALU.mult, ALU.bypass).then_inc(slopes_ready, 1)
                    TS(row_neg[:, :], W("slope_row"), -1.0, None, ALU.mult, ALU.bypass).then_inc(slopes_ready, 1)
                    TS(heads_neg[:, :], W("slope_heads"), -1.0, None, ALU.mult, ALU.bypass).then_inc(slopes_ready, 1)
                    V.tensor_copy(pick_b[:, :], C("pick_expert")).then_inc(slopes_ready, 1)
            normal(len(UNITS) - 1)
            dve.wait_ge(tree_node, len(UNITS))
            for c in range(NCH):
                dve.wait_ge(pe_prep, 4 + c)
                order.did(TT(chunk(hres, c), chunk(hres, c), bank(c), ALU.mult))
            order.wait()
            for c in range(NCH):
                V.tensor_copy(chunk(x, c), chunk(hres, c)).then_inc(ln_in, 1)
            dve.wait_ge(pe_prep, 6)
            dve.wait_ge(late_weights_in, 16)
            order.did(TS(f_w[:, :], bank(7)[:, 0:P], NORM_GAIN * D ** 0.5, None, ALU.mult, ALU.bypass))
            order.did(TT(f_c[:, :], bank(7)[:, P:P + 1], W("ffn_b"), ALU.add))
            order.wait()
            TS(f_c_gain[:, :], f_c[:, :], NORM_GAIN, None, ALU.mult, ALU.bypass).then_inc(vec_prep, 1)

            def ln(n, c, dst, inc, gamma=None, beta=None, plus=None, post=None):
                dve.wait_ge(ln_rstd, n * NCH + (c + 1))
                if gamma is None and plus is None:
                    TT(chunk(dst, c), bank(c), chunk(rstd, c), ALU.mult).then_inc(inc, 1)
                    return
                order.did(TT(chunk(norm_tmp, c), bank(c), chunk(rstd, c), ALU.mult))
                order.wait()
                if plus is not None:
                    TT(chunk(dst, c), chunk(norm_tmp, c), chunk(plus, c), ALU.add).then_inc(inc, 1)
                else:
                    TS(chunk(dst, c), chunk(norm_tmp, c), gamma, beta, ALU.mult, ALU.add).then_inc(inc, 1)

            for c in range(NCH):
                ln(0, c, x, ln_in, plus=C("pe"))

            def layer(i, last=False):
                dve.wait_ge(layer_a_in, i * 16 + 16)
                for c in range(NCH):
                    ln(i * 2 + 1, c, hn, hn_ready, gamma=A("g1"), beta=A("b1"))
                for c in range(NCH):
                    dve.wait_ge(k_ready, i * NCH + (c + 1))
                    order.did(V.tensor_reduce(k_part[:, c:c + 1], bank(c), AX.X, ALU.max))
                order.wait()
                TT(k_own[:, :], k_part[:, 0:1], k_part[:, 1:2], ALU.max).then_inc(k_max, 1)
                for b in range(4):
                    dve.wait_ge(qv_ready, i * 4 + (b + 1))
                    q = bank(4 + b).rearrange("p (n w) -> p n w", n=4)[:, :, 0:D].rearrange("p n (h d) -> p n h d", h=HEADS)
                    order.did(V.tensor_reduce(q_max[:, 4 * b:4 * b + 4, :], q, AX.X, ALU.max))
                    if b == 0:
                        dve.wait_ge(k_swapped, i + 1)
                        dve.wait_ge(k_max, i + 1)
                        TS(k_neg[:, :], bank(2)[:, 0:1], k_own[:, 0:1], -1.0, ALU.max, ALU.mult).then_inc(k_negmax, 1)
                    order.wait()
                    ins = TT(q_sh[:, 4 * b:4 * b + 4, :].rearrange("p n (h d) -> p n h d", h=HEADS), q,
                             q_max[:, 4 * b:4 * b + 4, :].unsqueeze(3).broadcast_to([P, 4, HEADS, DH]), ALU.subtract)
                    ins.then_inc(q_shifted, 1)
                for c in range(NCH):
                    t = slice(8 * c, 8 * c + 8)
                    dve.wait_ge(q_exped, i * NCH + (c + 1))
                    order.did(V.tensor_reduce(q_sum[:, t, :], q_e[:, t, :].rearrange("p n (h d) -> p n h d", h=HEADS), AX.X, ALU.add))
                    order.wait()
                    order.did(V.reciprocal(q_inv[:, t, :], q_sum[:, t, :]))
                    order.wait()
                    TT(q_n[:, t, :].rearrange("p n (h d) -> p n h d", h=HEADS),
                       q_e[:, t, :].rearrange("p n (h d) -> p n h d", h=HEADS),
                       q_inv[:, t, :].unsqueeze(3).broadcast_to([P, 8, HEADS, DH]), ALU.mult).then_inc(q_normed, 1)
                dve.wait_ge(k_exped, i * NCH + NCH)
                TT(k_half[:, :], k_sums[:, 0:1], k_sums[:, 1:2], ALU.add).then_inc(k_summed, 1)
                dve.wait_ge(ctx_ready, i * 2 + 2)
                dve.wait_ge(pool_zeroed, 2)
                TT(ctx_T[:, :], ps[:, 0, 0:D], C("head_block"), ALU.mult).then_inc(ctx_masked, 1)
                dve.wait_ge(k_total, i + 1)
                order.did(V.reciprocal(k_inv[:, :], bank(1)[:, 0:1]))
                order.wait()
                dve.wait_ge(mix_ps, i + 1)
                TS(mix[0:D, 0:D], ps[0:D, 2, 0:D], k_inv[0:D, 0:1], DH ** -0.5, ALU.mult, ALU.mult).then_inc(mix_ready, 1)
                TS(mix[D:P, D:P], ps[D:P, 2, 0:D], k_inv[D:P, 0:1], DH ** -0.5, ALU.mult, ALU.mult).then_inc(mix_ready, 1)
                for c in range(NCH):
                    dve.wait_ge(attn_ready, i * NCH + (c + 1))
                    STT(chunk(x, c), bank(6 + c), A("bo"), chunk(x, c), ALU.add, ALU.add).then_inc(ln_in, 1)
                dve.wait_ge(layer_b_in, i * 16 + 16)
                for c in range(NCH):
                    ln(i * 2 + 2, c, hn, hn_ready, gamma=B("g2"), beta=B("b2"))
                for c in range(NCH):
                    dve.wait_ge(down_ready, i * 8 + (4 * c + 4))
                    dve.wait_ge(ln_in, (i * 2 + 3) * NCH)
                    layer_out = STT(chunk(x, c), bank(c), B("bf2"), chunk(x, c), ALU.add, ALU.add)
                    if last:
                        order.did(layer_out)
                        order.wait()
                        TT(chunk(x, c), chunk(hres, c), chunk(x, c), ALU.add).then_inc(ln_in, 1)
                    else:
                        layer_out.then_inc(ln_in, 1)

            with dve.Fori(0, LAYERS - 1) as i:
                order.enter(i, 15)
                layer(i)
            order.leave(LAYERS - 1)
            layer(LAYERS - 1, True)
            N9 = 1 + 2 * LAYERS


            for c in range(NCH):
                dve.wait_ge(ln_in, N9 * NCH + (c + 1))
                order.did(TS(chunk(hres, c), chunk(x, c), f_c[:, 0:1], None, ALU.add, ALU.bypass))
            dve.wait_ge(pool_order, 2)
            for c in range(NCH):
                dve.wait_ge(ln_rstd, N9 * NCH + (c + 1))
                order.did(TT(chunk(norm_tmp, c), bank(c), chunk(rstd, c), ALU.mult))
                order.wait()
                TS(chunk(f_state, c), chunk(norm_tmp, c), NORM_GAIN, f_c_gain[:, 0:1], ALU.mult, ALU.subtract).then_inc(f_state_ready, 1)

            def slot(s, t, ending=False):
                if not ending:
                    dve.wait_ge(f_tanh_ready, s + 1)
                    STT(group(f_mid, t), bank(4 + t)[:, 0:GC], f_c_gain[:, 0:1], group(f_tanh, t), ALU.add, ALU.add).then_inc(f_mid_ready, 1)
                if runs(s, 1, ending, t):
                    g = (t - 1) % NG
                    dve.wait_ge(f_squared, s)
                    V.tensor_reduce(f_sumsq[:, g, :], f_squares[:, 4 * g:4 * g + 4, :], AX.X, ALU.add).then_inc(f_summed, 1)
                if runs(s, 2, ending, t):
                    g = (t - 2) % NG
                    dve.wait_ge(f_rstd, s - 1)
                    dve.wait_ge(f_mapped, s - 1)
                    TT(group(f_tok, g).rearrange("p (j h d) -> p j h d", j=2, h=HALVES),
                       mapped(g).rearrange("p (j h d) -> p j h d", j=2, h=HALVES),
                       f_rstd_sb[:, g, :].rearrange("p (j h) -> p j h", j=2).unsqueeze(3).broadcast_to([P, 2, HALVES, D]), ALU.mult).then_inc(f_scaled, 1)

            for t in range(NG):
                slot(t, t)
            with dve.Fori(1, ITERS) as i:
                for t in range(NG):
                    slot(i * NG + t, t)
            for t in range(3):
                slot(ITERS * NG + t, t, True)
            for c in range(NCH):
                dve.wait_ge(f_turned, ITERS * NG + 2 * c + 2)
                h = chunk(hres, c).rearrange("p (g w) -> p g w", g=2)
                STT(h, ps[:, 4 + 2 * c:6 + 2 * c, 0:GC], 1.0 / NORM_GAIN, h, ALU.mult, ALU.add).then_inc(ln_in, 1)

            for c in range(NCH):
                ln(N9 + 1, c, hn, hn_ready)
            dve.wait_ge(act_prep, 12)
            for b in range(4):
                dve.wait_ge(d_kv_ps, b + 1)
                kv = bank(4 + b).rearrange("p (n w) -> p n w", n=4)
                order.did(TT(kd_tok[:, 4 * b:4 * b + 4, :], kv[:, :, 0:D],
                             k_decay[:, :].unsqueeze(1).broadcast_to([P, 4, D]), ALU.mult))
                V.tensor_copy(dv_tok[:, 4 * b:4 * b + 4, :], kv[:, :, D:2 * D]).then_inc(d_kv_ready, 1)
            dve.wait_ge(pool_zeroed, 3)
            dve.wait_ge(d_kv_ready, 4)
            for part in range(2):
                t = slice(part * NB, part * NB + NB)
                V.tensor_copy(v_heads[:, t, :].rearrange("p n (h w) -> p n h w", h=HEADS)[:, :, :, 0:DH],
                              dv_tok[:, t, :].rearrange("p n (h d) -> p n h d", h=HEADS)).then_inc(v_heads_ready, 1)
            dve.wait_ge(d_q_ready, NCH)
            order.did(TT(dqd[:, :].rearrange("p (j t) -> p j t", j=NB), dq[:, :].rearrange("p (j t) -> p j t", j=NB),
                         q_decay[:, :].unsqueeze(1).broadcast_to([P, NB, P]), ALU.mult))
            dve.wait_ge(d_upd_ps, 1)
            order.did(TT(updates[:, :, :], ps[:, 4:6, :].rearrange("p b (n d) -> p (b n) d", d=D),
                         C("head_block").unsqueeze(1).broadcast_to([P, NT, D]), ALU.mult))
            order.did(V.memset(state[:, 0, :], 0.0))
            tiles = [2 * j + half for half in range(HALVES) for j in range(NB)]
            dve.wait_ge(decay_masked, HEADS)
            for u in range(2 * NT):
                g = u // 2 % 2
                dve.wait_ge(d_scores, u + 1)
                if u >= 4:
                    dve.wait_ge(d_block_out, u - 3)
                TT(scored[:, u % 4, :], bank(u % 4), decay[:, 4 * g:4 * g + 4, :].rearrange("p h t -> p (h t)"),
                   ALU.mult).then_inc(d_scored, 1)
                if 1 <= u + 1 < NT:
                    order.wait()
                    order.did(STT(state[:, u + 1, :], state[:, u, :], block_decay[:, 0:1], updates[:, tiles[u], :], ALU.mult, ALU.add))
                elif u + 1 == NT:
                    order.wait()
                    for half in range(HALVES):
                        rows = slice(half * D, (half + 1) * D)
                        V.tensor_copy(state_rows[rows, :, :].rearrange("p (j h) d -> p j h d", h=HALVES)[:, :, half, :],
                                      state[rows, half * NB:(half + 1) * NB, :]).then_inc(d_state_ready, 1)
            for c in range(NCH):
                dve.wait_ge(d_proj, c + 1)
                STT(chunk(hres, c), bank(c), W("dec_b"), chunk(hres, c), ALU.add, ALU.add).then_inc(ln_in, 1)

            for c in range(NCH):
                ln(N9 + 2, c, x, ln_in)
            for c in range(NCH):
                ln(N9 + 3, c, xn, hn_ready, gamma=W("moe_gamma"), beta=W("moe_beta"))
            dve.wait_ge(logits_ps, 1)
            order.did(TT(logits[:, :, :], bank(4)[:, 0:NT * E].rearrange("p (n e) -> p n e", e=E),
                         W("moe_br")[:, 0:E].unsqueeze(1).broadcast_to([P, NT, E]), ALU.add))
            order.wait()
            for n in range(NT):
                order.did(V.max(top[:, n, :], logits[:, n, :]))
            order.wait()
            TT(gap[:, :], top[:, :, 1], top[:, :, 0], ALU.subtract).then_inc(gap_ready, 1)
            for n in range(NT):
                order.did(V.max_index(top_i[:, n, :], top[:, n, :], logits[:, n, :]))
            order.wait()
            order.did(V.tensor_copy(top_f[:, :, :], top_i[:, :, 0:2]))
            order.wait()
            iota = C("iota_e").unsqueeze(1).broadcast_to([P, NT, E])
            order.did(TT(pick_1[:, :, :], iota, top_f[:, :, 0:1].broadcast_to([P, NT, E]), ALU.is_equal))
            order.did(TT(pick_2[:, :, :], iota, top_f[:, :, 1:2].broadcast_to([P, NT, E]), ALU.is_equal))
            dve.wait_ge(gap_exped, 1)
            order.did(TS(den[:, :], gap_e[:, :], 1.0, None, ALU.add, ALU.bypass))
            order.wait()
            order.did(V.reciprocal(w_1[:, :], den[:, :]))
            order.wait()
            order.did(TT(w_2[:, :], gap_e[:, :], w_1[:, :], ALU.mult))
            order.did(TT(share_1[:, :, :], pick_1[:, :, :], w_1[:, :].unsqueeze(2).broadcast_to([P, NT, E]), ALU.mult))
            order.wait()
            order.did(TT(share_2[:, :, :], pick_2[:, :, :], w_2[:, :].unsqueeze(2).broadcast_to([P, NT, E]), ALU.mult))
            order.wait()
            order.did(TT(share[:, :, :], share_1[:, :, :], share_2[:, :, :], ALU.add))
            order.wait()
            whole = share[:, :, :].rearrange("p (j h) e -> p j (h e)", h=HALVES)
            rest = share_rest[:, :, :]
            order.did(V.tensor_copy(share_parts[:, :, 0, :], whole))
            order.wait()
            order.did(TT(rest, whole, share_parts[:, :, 0, :], ALU.subtract))
            order.wait()
            order.did(V.tensor_copy(share_parts[:, :, 1, :], rest))
            order.wait()
            TT(share_parts[:, :, 2, :], rest, share_parts[:, :, 1, :], ALU.subtract).then_inc(share_ready, 1)
            V.memset(share_T[:, :], 0.0).then_inc(share_T_ready, 1)
            dve.wait_ge(share_turned, 1)
            dve.wait_ge(share_T_ready, 1)
            V.tensor_copy(share_T[0:3 * 2 * E, :], ps[:, 5, :].bitcast(BF16)[0:3 * 2 * E, :]).then_inc(share_T_ready, 1)
            for v in range(E * NCH):
                e, c = v // 2, v % 2
                dve.wait_ge(m_down, v + 1)
                dve.wait_ge(share_w_ready, v + 1)
                order.did(STT(y_part[:, v % 2, :], bank(4 + v % 2), W("moe_b2")[:, e:e + 1], share_w[:, v % 2, :], ALU.add, ALU.mult))
                order.wait()
                if v >= 2:
                    dve.wait_ge(m_added, v - 1)
                TT(chunk(hres, c), chunk(hres, c), y_part[:, v % 2, :], ALU.add).then_inc(m_added, 1)


def pack(table, columns, n):
    at, width = offsets(table)
    out = np.zeros(n + (P, width), np.float32)
    for name, (a, w) in at.items():
        v = np.asarray(columns[name])
        out[..., a:a + w] = v
    return out


def twice(v):
    return np.concatenate([v, v]).reshape(P, 1)


def diagonal(*blocks):
    a, b = blocks
    out = np.zeros(a.shape[:-2] + (P, a.shape[-1] + b.shape[-1]), np.float32)
    out[..., :D, :a.shape[-1]] = a
    out[..., D:, a.shape[-1]:] = b
    return out


def make_consts():
    c = {}
    eye = np.eye(P, dtype=np.float32)
    same = np.kron(np.eye(HALVES), np.ones((D, D)))
    p = np.arange(P)
    c["center"] = eye - same / D
    c["mean"] = same / D
    c["ident"] = eye
    c["swap"] = eye[(p + D) % P]
    c["both"] = eye + c["swap"]
    pos = np.arange(S, dtype=np.float32)[:, None]
    div = np.exp(np.arange(0, D, 2, dtype=np.float32) * np.float32(-np.log(10000.0) / D)).astype(np.float32)
    table = np.zeros((S, D), np.float32)
    table[:, 0::2] = np.sin((pos * div).astype(np.float32))
    table[:, 1::2] = np.cos((pos * div).astype(np.float32))
    c["pe"] = table.reshape(HALVES, COLS, D).transpose(0, 2, 1).reshape(P, COLS)
    f = p % D
    c["head_block"] = (f[:, None] // DH == np.arange(D)[None, :] // DH)
    c["head_mask"] = (p[:, None] // DH == np.arange(HALVES * HEADS)[None, :])
    c["diff"] = np.maximum(p[None, :] - p[:, None], 0)
    c["causal"] = p[None, :] >= p[:, None]
    c["pos_row"] = np.broadcast_to(p[None, :], (P, P))
    c["pos_left"] = (P - p)[:, None]
    c["vocab"] = np.stack([p, p + P, f], 1)
    c["pick_expert"] = np.concatenate([(p[:, None] % E == e) & (p[:, None] // E % HALVES == p[None, :] // D)
                                       & (p[:, None] < 3 * HALVES * E) for e in range(E)], 1)
    c["iota_e"] = np.broadcast_to(np.arange(E)[None, :], (P, E))
    return pack(CONSTS, c, ())


def kernel(**inputs):
    import concourse.bacc as bacc
    from concourse.bass_utils import run_bass_kernel_spmd

    a = {k: np.asarray(v) for k, v in inputs.items()}
    tok = {k[7:]: v for k, v in a.items() if k.startswith("L0_tok_")}
    att = {k[8:]: v for k, v in a.items() if k.startswith("L0_attn_")}
    ffn = {k[7:]: v for k, v in a.items() if k.startswith("L0_ffn_")}
    dec = {k[8:]: v for k, v in a.items() if k.startswith("L1_attn_")}
    moe = {k[7:]: v for k, v in a.items() if k.startswith("L1_ffn_")}

    w = {}
    w["comp"] = tok["comp_emb"].reshape(2, P, D).transpose(1, 0, 2).reshape(P, 2 * D)
    w["op"] = np.concatenate([tok["op_emb"], np.zeros((D, D), np.float32)])
    w["tok_gamma_row"] = np.broadcast_to(tok["gamma"], (P, D))
    w["tok_beta_row"] = np.broadcast_to(tok["beta"], (P, D))
    for k, name in enumerate(("wo_T", "wl_T", "wr_T")):
        t = tok["W_bin"][k * D:(k + 1) * D].T
        w[name] = diagonal(t, t)
    w["tok_b"], w["tok_gamma"], w["tok_beta"] = twice(tok["b_bin"]), twice(tok["gamma"]), twice(tok["beta"])
    w["ffn_wT"] = diagonal(ffn["W"].T, ffn["W"].T)
    w["ffn_ln_w"], w["ffn_ln_b"], w["ffn_b"] = twice(ffn["ln_w"]), twice(ffn["ln_b"]), twice(ffn["b"])
    wq, wk, wv = (dec["w_qkv"][:, k * D:(k + 1) * D] for k in range(3))
    w["dec_q"], w["dec_k"] = diagonal(wq, wq), diagonal(wk, wk)
    kv = np.concatenate([wk, wv], 1)
    w["dec_kv"] = diagonal(kv, kv)
    w["dec_proj"] = diagonal(dec["w_proj"], dec["w_proj"])
    w["dec_b"] = twice(dec["b_proj"])
    w["slope_col"] = twice(np.repeat(dec["slopes"], DH))
    w["slope_row"] = np.broadcast_to(np.repeat(dec["slopes"], DH), (P, D))
    w["slope_heads"] = np.broadcast_to(dec["slopes"], (P, HEADS))
    w["moe_gamma"], w["moe_beta"] = twice(moe["gamma"]), twice(moe["beta"])
    w["moe_wr"] = diagonal(moe["Wr"], moe["Wr"])
    w["moe_br"] = np.broadcast_to(np.concatenate([moe["br"], moe["br"]]), (P, 2 * E))
    w["moe_b1"] = moe["b1"].T
    w["moe_b2"] = np.concatenate([moe["b2"].T, moe["b2"].T])
    w["moe_w2"] = moe["W2"].transpose(1, 0, 2).reshape(HID, E * D)
    up = np.zeros((P, HALVES, E, HID), np.float32)
    for half in range(HALVES):
        up[half * D:(half + 1) * D, half] = moe["W1"].transpose(1, 0, 2)
    w["moe_w1"] = up.reshape(P, HALVES * E * HID)

    def column(v):
        return np.concatenate([v, v], 1)[:, :, None]

    la = {"wk": diagonal(att["Wk"], att["Wk"]), "wo": np.concatenate([att["Wo"], att["Wo"]], 1),
          "g1": column(att["g1"]), "b1": column(att["b1"]), "bo": column(att["bo"])}
    qv = np.concatenate([att["Wq"], att["Wv"]], 2)
    la["wqv"] = diagonal(qv, qv)
    lb = {"w1": diagonal(att["W1"], att["W1"]), "w2": att["W2"].reshape(LAYERS, 2, P, D).transpose(0, 2, 1, 3).reshape(LAYERS, P, 2 * D),
          "bf1": att["bf1"].reshape(LAYERS, 2, P).transpose(0, 2, 1), "bf2": column(att["bf2"]),
          "g2": column(att["g2"]), "b2": column(att["b2"])}

    table = np.zeros((tok["leaf_ids"].shape[0], SLOTS), np.int32)
    table[:, :LEAVES] = tok["leaf_ids"]
    table[:, LEAVES:2 * LEAVES - 1] = tok["op_ids"]
    arrays = {
        "token_idx": np.ascontiguousarray(a["x"].reshape(HALVES, NB, P).transpose(2, 1, 0).reshape(P, NT)),
        "id_table": table,
        "weights": pack(WEIGHTS, w, ()),
        "consts": make_consts(),
        "layer_a": pack(LAYER_A, la, (LAYERS,)),
        "layer_b": pack(LAYER_B, lb, (LAYERS,)),
    }
    nc = bacc.Bacc("TRN2", target_bir_lowering=False, num_devices=1)
    args = [nc.dram_tensor(name, v.shape, mybir.dt.from_np(v.dtype), kind="ExternalInput").ap() for name, v in arrays.items()]
    out = nc.dram_tensor("out", (1, S, D), F32, kind="ExternalOutput").ap()
    build(nc, *args, out)
    r = run_bass_kernel_spmd(nc, [arrays], core_ids=[0])
    return r.results[0]["out"]
```
